# Optimizing a Trainium2 kernel written in Bass

```python
import numpy as np
import jax
import jax.numpy as jnp

def _softmax(x, axis=-1):
    return jax.nn.softmax(x, axis=axis)

def _gelu(x):
    return jax.nn.gelu(x, approximate=True)

def _silu(x):
    return jax.nn.silu(x)

def _sigmoid(x):
    return jax.nn.sigmoid(x)

def _layernorm(x, axis=-1, eps=1e-05):
    m = jnp.mean(x, axis=axis, keepdims=True)
    v = jnp.var(x, axis=axis, keepdims=True)
    return (x - m) / jnp.sqrt(v + eps)

def _scatter_add(tgt, idx, src, axis=0):
    return tgt.at[idx].add(src)

def _segment_sum(src, seg, n):
    return jax.ops.segment_sum(src, seg, n)
kernel_name = 'mk_gnn_resnorm_d4_gnn_r16_710817'

def setup_inputs(seed: int=0):
    np.random.seed(seed)
    _w = jnp.asarray

    def _rec_inputs():
        import jax
        import jax.numpy as jnp
        _gk = jax.random.key(seed)
        x = -0.0002117 + 1 * jax.random.normal(jax.random.fold_in(_gk, 1), (6250, 256), jnp.float32)
        _s = jax.random.randint(jax.random.fold_in(_gk, 2), (50000,), 0, 6250, jnp.int32)
        _d = jax.random.randint(jax.random.fold_in(_gk, 3), (50000,), 0, 6250, jnp.int32)
        _loop = jnp.arange(6250, dtype=jnp.int32)
        src = jnp.concatenate([_s, _d, _loop])
        dst = jnp.concatenate([_d, _s, _loop])
        _o = jnp.argsort(dst, stable=True)
        src = src[_o]
        dst = dst[_o]
        edge_attr_128 = 9.41057e-06 + 1 * jax.random.normal(jax.random.fold_in(_gk, 11), (106250, 128), jnp.float32)
        edge_weight1 = jax.random.uniform(jax.random.fold_in(_gk, 14), (106250, 1), jnp.float32, 0.0, 1)
        node_vec1 = jax.random.uniform(jax.random.fold_in(_gk, 15), (6250, 1), jnp.float32, 0.0, 0.999973)
        node_vec1_n2 = jax.random.uniform(jax.random.fold_in(_gk, 16), (6250, 1), jnp.float32, 0.0, 0.999973)
        return (x, src, dst, edge_attr_128, edge_weight1, node_vec1, node_vec1_n2)
    x, src, dst, edge_attr_128, edge_weight1, node_vec1, node_vec1_n2 = _rec_inputs()

    def _L0_gnn_setup():
        import jax, jax.numpy as jnp
        import numpy as np
        N = 6250
        D = 256
        E = 18750
        BN_EPS = 1e-05

        def _batchnorm(x, gamma, beta):
            mean = jnp.mean(x, axis=0)
            var = jnp.var(x, axis=0)
            return (x - mean) * jax.lax.rsqrt(var + BN_EPS) * gamma + beta
        key = jax.random.key(seed)
        ks = jax.random.split(key, 8)
        h = jax.random.normal(ks[0], (N, D), dtype=jnp.float32)
        edge_index = jax.random.randint(ks[1], (2, E), 0, N, dtype=jnp.int64)
        W1 = jax.random.normal(ks[2], (D, 2 * D), dtype=jnp.float32) / np.sqrt(D)
        b1 = jnp.zeros((2 * D,), dtype=jnp.float32)
        g1 = jnp.ones((2 * D,), dtype=jnp.float32)
        bt1 = jnp.zeros((2 * D,), dtype=jnp.float32)
        W2 = jax.random.normal(ks[3], (2 * D, D), dtype=jnp.float32) / np.sqrt(2 * D)
        b2 = jnp.zeros((D,), dtype=jnp.float32)
        g2 = jnp.ones((D,), dtype=jnp.float32)
        bt2 = jnp.zeros((D,), dtype=jnp.float32)
        eps_gin = jnp.zeros((), dtype=jnp.float32)
        return {'h': h, 'edge_index': edge_index, 'W1': W1, 'b1': b1, 'g1': g1, 'bt1': bt1, 'W2': W2, 'b2': b2, 'g2': g2, 'bt2': bt2, 'eps_gin': eps_gin}
    _L0_gnn_all = _L0_gnn_setup()
    _L0_gnn_in = {k: v for k, v in _L0_gnn_all.items() if k in ('W1', 'b1', 'g1', 'bt1', 'W2', 'b2', 'g2', 'bt2', 'eps_gin')}
    del _L0_gnn_all

    def _L1_gnn_setup():
        import jax, jax.numpy as jnp
        import numpy as np
        BS = 512
        EMBED = 256
        NHEAD = 8
        HDIM = EMBED // NHEAD
        E = BS * BS

        def _xavier(key, shape):
            lim = float(np.sqrt(6.0 / (shape[0] + shape[1])))
            return jax.random.uniform(key, shape, jnp.float32, -lim, lim)
        key = jax.random.key(seed)
        ks = jax.random.split(key, 6)
        feats = jax.random.normal(ks[0], (BS, EMBED), jnp.float32)
        dst = jnp.repeat(jnp.arange(BS), BS)
        src = jnp.tile(jnp.arange(BS), BS)
        edge_index = jnp.stack([src, dst], axis=1).astype(jnp.int32)
        edge_attr = jnp.zeros((E, 1), jnp.float32)
        return {'feats': feats, 'edge_index': edge_index, 'edge_attr': edge_attr, 'Wq': _xavier(ks[1], (EMBED, EMBED)), 'bq': jnp.zeros((EMBED,), jnp.float32), 'Wk': _xavier(ks[2], (EMBED, EMBED)), 'bk': jnp.zeros((EMBED,), jnp.float32), 'Wv': _xavier(ks[3], (EMBED, EMBED)), 'bv': jnp.zeros((EMBED,), jnp.float32), 'Wo': _xavier(ks[4], (EMBED, EMBED)), 'bo': jnp.zeros((EMBED,), jnp.float32)}
    _L1_gnn_all = _L1_gnn_setup()
    _L1_gnn_in = {k: v for k, v in _L1_gnn_all.items() if k in ('Wq', 'bq', 'Wk', 'bk', 'Wv', 'bv', 'Wo', 'bo')}
    del _L1_gnn_all

    def _L2_gnn_setup():
        import jax, jax.numpy as jnp
        import numpy as np
        NUM_NODES = 3125
        NUM_EDGES = 100000
        NODE_DIM = 256
        EDGE_DIM = 128
        MAX_IN_DEGREE = 512
        MAX_OUT_DEGREE = 512
        key = jax.random.key(seed)
        ks = jax.random.split(key, 12)
        x = jax.random.normal(ks[0], (NUM_NODES, NODE_DIM), dtype=jnp.float32)
        edge_index = jax.random.randint(ks[1], (2, NUM_EDGES), 0, NUM_NODES, dtype=jnp.int64 if jax.config.read('jax_enable_x64') else jnp.int32)
        edge_attr = jax.random.normal(ks[2], (NUM_EDGES, EDGE_DIM), dtype=jnp.float32)
        voronoi_values = jax.random.uniform(ks[3], (NUM_NODES, 1), dtype=jnp.float32)
        centralities = jax.random.uniform(ks[4], (NUM_NODES, 1), dtype=jnp.float32)
        z_in = jax.random.normal(ks[5], (MAX_IN_DEGREE, NODE_DIM), dtype=jnp.float32)
        z_out = jax.random.normal(ks[6], (MAX_OUT_DEGREE, NODE_DIM), dtype=jnp.float32)
        W_cent = jax.random.normal(ks[7], (1, NODE_DIM), dtype=jnp.float32) * 0.5
        b_cent = jnp.zeros((NODE_DIM,), dtype=jnp.float32)
        W_vor = jax.random.normal(ks[8], (1, NODE_DIM), dtype=jnp.float32) * 0.5
        b_vor = jnp.zeros((NODE_DIM,), dtype=jnp.float32)
        W_sum = jax.random.normal(ks[9], (EDGE_DIM, NODE_DIM), dtype=jnp.float32) * (1.0 / np.sqrt(EDGE_DIM))
        b_sum = jnp.zeros((NODE_DIM,), dtype=jnp.float32)
        return {'x': x, 'edge_index': edge_index, 'edge_attr': edge_attr, 'voronoi_values': voronoi_values, 'centralities': centralities, 'z_in': z_in, 'z_out': z_out, 'W_cent': W_cent, 'b_cent': b_cent, 'W_vor': W_vor, 'b_vor': b_vor, 'W_sum': W_sum, 'b_sum': b_sum}
    _L2_gnn_all = _L2_gnn_setup()
    _L2_gnn_in = {k: v for k, v in _L2_gnn_all.items() if k in ('z_in', 'z_out', 'W_cent', 'b_cent', 'W_vor', 'b_vor', 'W_sum', 'b_sum')}
    del _L2_gnn_all

    def _L3_gnn_setup():
        import jax, jax.numpy as jnp
        import numpy as np
        N = 3125
        DIM = 256
        E = 50000

        def _srgnn_conv(x, W, b, src, dst, num_nodes):
            xl = x @ W.T + b
            msgs = xl[src]
            agg = jax.ops.segment_sum(msgs, dst, num_segments=num_nodes)
            cnt = jax.ops.segment_sum(jnp.ones((src.shape[0],), x.dtype), dst, num_segments=num_nodes)
            return agg / jnp.maximum(cnt, 1.0)[:, None]
        key = jax.random.key(seed)
        ks = jax.random.split(key, 11)
        stdv = 1.0 / np.sqrt(DIM)
        u = lambda k, shape: jax.random.uniform(k, shape, jnp.float32, -stdv, stdv)
        hidden = jax.random.normal(ks[0], (N, DIM), jnp.float32)
        edge_index = jax.random.randint(ks[1], (2, E), 0, N, jnp.int64)
        return {'hidden': hidden, 'edge_index': edge_index, 'W_in': u(ks[2], (DIM, DIM)), 'b_in': u(ks[3], (DIM,)), 'W_out': u(ks[4], (DIM, DIM)), 'b_out': u(ks[5], (DIM,)), 'W_ih': u(ks[6], (3 * DIM, 2 * DIM)), 'b_ih': u(ks[7], (3 * DIM,)), 'W_hh': u(ks[8], (3 * DIM, DIM)), 'b_hh': u(ks[9], (3 * DIM,))}
    _L3_gnn_all = _L3_gnn_setup()
    _L3_gnn_in = {k: v for k, v in _L3_gnn_all.items() if k in ('W_in', 'b_in', 'W_out', 'b_out', 'W_ih', 'b_ih', 'W_hh', 'b_hh')}
    del _L3_gnn_all
    return {'x': x, 'src': src, 'dst': dst, 'edge_attr_128': edge_attr_128, 'edge_weight1': edge_weight1, 'node_vec1': node_vec1, 'node_vec1_n2': node_vec1_n2, 'L0_gnn_W1': _L0_gnn_in['W1'], 'L0_gnn_b1': _L0_gnn_in['b1'], 'L0_gnn_g1': _L0_gnn_in['g1'], 'L0_gnn_bt1': _L0_gnn_in['bt1'], 'L0_gnn_W2': _L0_gnn_in['W2'], 'L0_gnn_b2': _L0_gnn_in['b2'], 'L0_gnn_g2': _L0_gnn_in['g2'], 'L0_gnn_bt2': _L0_gnn_in['bt2'], 'L0_gnn_eps_gin': _L0_gnn_in['eps_gin'], 'L1_gnn_Wq': _L1_gnn_in['Wq'], 'L1_gnn_bq': _L1_gnn_in['bq'], 'L1_gnn_Wk': _L1_gnn_in['Wk'], 'L1_gnn_bk': _L1_gnn_in['bk'], 'L1_gnn_Wv': _L1_gnn_in['Wv'], 'L1_gnn_bv': _L1_gnn_in['bv'], 'L1_gnn_Wo': _L1_gnn_in['Wo'], 'L1_gnn_bo': _L1_gnn_in['bo'], 'L2_gnn_z_in': _L2_gnn_in['z_in'], 'L2_gnn_z_out': _L2_gnn_in['z_out'], 'L2_gnn_W_cent': _L2_gnn_in['W_cent'], 'L2_gnn_b_cent': _L2_gnn_in['b_cent'], 'L2_gnn_W_vor': _L2_gnn_in['W_vor'], 'L2_gnn_b_vor': _L2_gnn_in['b_vor'], 'L2_gnn_W_sum': _L2_gnn_in['W_sum'], 'L2_gnn_b_sum': _L2_gnn_in['b_sum'], 'L3_gnn_W_in': _L3_gnn_in['W_in'], 'L3_gnn_b_in': _L3_gnn_in['b_in'], 'L3_gnn_W_out': _L3_gnn_in['W_out'], 'L3_gnn_b_out': _L3_gnn_in['b_out'], 'L3_gnn_W_ih': _L3_gnn_in['W_ih'], 'L3_gnn_b_ih': _L3_gnn_in['b_ih'], 'L3_gnn_W_hh': _L3_gnn_in['W_hh'], 'L3_gnn_b_hh': _L3_gnn_in['b_hh']}

def reference(x, src, dst, edge_attr_128, edge_weight1, node_vec1, node_vec1_n2, L0_gnn_W1, L0_gnn_b1, L0_gnn_g1, L0_gnn_bt1, L0_gnn_W2, L0_gnn_b2, L0_gnn_g2, L0_gnn_bt2, L0_gnn_eps_gin, L1_gnn_Wq, L1_gnn_bq, L1_gnn_Wk, L1_gnn_bk, L1_gnn_Wv, L1_gnn_bv, L1_gnn_Wo, L1_gnn_bo, L2_gnn_z_in, L2_gnn_z_out, L2_gnn_W_cent, L2_gnn_b_cent, L2_gnn_W_vor, L2_gnn_b_vor, L2_gnn_W_sum, L2_gnn_b_sum, L3_gnn_W_in, L3_gnn_b_in, L3_gnn_W_out, L3_gnn_b_out, L3_gnn_W_ih, L3_gnn_b_ih, L3_gnn_W_hh, L3_gnn_b_hh):
    import jax
    import jax.numpy as jnp

    def _L0_gnn_ref(h, edge_index, W1, b1, g1, bt1, W2, b2, g2, bt2, eps_gin):
        import jax, jax.numpy as jnp
        import numpy as np
        N = 6250
        D = 256
        E = 18750
        BN_EPS = 1e-05

        def _batchnorm(x, gamma, beta):
            mean = jnp.mean(x, axis=0)
            var = jnp.var(x, axis=0)
            return (x - mean) * jax.lax.rsqrt(var + BN_EPS) * gamma + beta
        src, dst = (edge_index[0], edge_index[1])
        agg = jax.ops.segment_sum(h[src], dst, num_segments=N)
        z = (1.0 + eps_gin) * h + agg
        t = jnp.dot(z, W1) + b1
        t = jax.nn.relu(_batchnorm(t, g1, bt1))
        conv_out = jnp.dot(t, W2) + b2
        out = jax.nn.relu(_batchnorm(conv_out + h, g2, bt2))
        return out

    def _L1_gnn_ref(feats, edge_index, edge_attr, Wq, bq, Wk, bk, Wv, bv, Wo, bo):
        import jax, jax.numpy as jnp
        import numpy as np
        BS = 512
        EMBED = 256
        NHEAD = 8
        HDIM = EMBED // NHEAD
        E = BS * BS

        def _xavier(key, shape):
            lim = float(np.sqrt(6.0 / (shape[0] + shape[1])))
            return jax.random.uniform(key, shape, jnp.float32, -lim, lim)
        bs = feats.shape[0]
        scale = 1.0 / np.sqrt(HDIM)
        q = (feats @ Wq.T + bq).reshape(bs, NHEAD, HDIM).transpose(1, 0, 2)
        k = (feats @ Wk.T + bk).reshape(bs, NHEAD, HDIM).transpose(1, 0, 2)
        v = (feats @ Wv.T + bv).reshape(bs, NHEAD, HDIM).transpose(1, 0, 2)
        r, c = (edge_index[:, 0], edge_index[:, 1])
        qe = q[:, c, :]
        ke = k[:, r, :]
        ve = v[:, r, :]
        sim = jnp.einsum('hed,hed->eh', qe, ke) * scale
        m = jax.ops.segment_max(sim, c, num_segments=bs)
        p = jnp.exp(sim - m[c])
        s = jax.ops.segment_sum(p, c, num_segments=bs)
        attn = p / s[c]
        out_e = attn.T[..., None] * ve
        out_e = out_e.transpose(1, 0, 2).reshape(-1, NHEAD * HDIM)
        agg = jax.ops.segment_sum(out_e, c, num_segments=bs)
        return agg @ Wo.T + bo

    def _L2_gnn_ref(x, edge_index, edge_attr, voronoi_values, centralities, z_in, z_out, W_cent, b_cent, W_vor, b_vor, W_sum, b_sum):
        import jax, jax.numpy as jnp
        import numpy as np
        NUM_NODES = 3125
        NUM_EDGES = 100000
        NODE_DIM = 256
        EDGE_DIM = 128
        MAX_IN_DEGREE = 512
        MAX_OUT_DEGREE = 512
        num_nodes = x.shape[0]
        src = edge_index[0]
        dst = edge_index[1]
        ones = jnp.ones_like(src, dtype=jnp.int32)
        in_deg = jnp.minimum(jax.ops.segment_sum(ones, dst, num_segments=num_nodes), MAX_IN_DEGREE - 1)
        out_deg = jnp.minimum(jax.ops.segment_sum(ones, src, num_segments=num_nodes), MAX_OUT_DEGREE - 1)
        edge_proj = edge_attr @ W_sum + b_sum
        sum3d = jax.ops.segment_sum(edge_proj, src, num_segments=num_nodes)
        cent_term = jax.nn.sigmoid(centralities @ W_cent + b_cent)
        vor_term = jax.nn.sigmoid(voronoi_values @ W_vor + b_vor)
        return x + z_in[in_deg] + z_out[out_deg] + cent_term + vor_term + sum3d

    def _L3_gnn_ref(hidden, edge_index, W_in, b_in, W_out, b_out, W_ih, b_ih, W_hh, b_hh):
        import jax, jax.numpy as jnp
        import numpy as np
        N = 3125
        DIM = 256
        E = 50000

        def _srgnn_conv(x, W, b, src, dst, num_nodes):
            xl = x @ W.T + b
            msgs = xl[src]
            agg = jax.ops.segment_sum(msgs, dst, num_segments=num_nodes)
            cnt = jax.ops.segment_sum(jnp.ones((src.shape[0],), x.dtype), dst, num_segments=num_nodes)
            return agg / jnp.maximum(cnt, 1.0)[:, None]
        src, dst = (edge_index[0], edge_index[1])
        n = hidden.shape[0]
        input_in = _srgnn_conv(hidden, W_in, b_in, src, dst, n)
        input_out = _srgnn_conv(hidden, W_out, b_out, dst, src, n)
        inputs = jnp.concatenate([input_in, input_out], axis=-1)
        gi = inputs @ W_ih.T + b_ih
        gh = hidden @ W_hh.T + b_hh
        i_r, i_i, i_n = jnp.split(gi, 3, axis=-1)
        h_r, h_i, h_n = jnp.split(gh, 3, axis=-1)
        reset_gate = jax.nn.sigmoid(i_r + h_r)
        input_gate = jax.nn.sigmoid(i_i + h_i)
        new_gate = jnp.tanh(i_n + reset_gate * h_n)
        return (1.0 - input_gate) * hidden + input_gate * new_gate
    edge_index = jnp.stack([src, dst])
    edge_index_t = jnp.stack([src, dst], axis=1)
    x = _layernorm(x + _L0_gnn_ref(x, edge_index, L0_gnn_W1, L0_gnn_b1, L0_gnn_g1, L0_gnn_bt1, L0_gnn_W2, L0_gnn_b2, L0_gnn_g2, L0_gnn_bt2, L0_gnn_eps_gin), axis=-1)
    x = _layernorm(x + _L1_gnn_ref(x, edge_index_t, edge_weight1, L1_gnn_Wq, L1_gnn_bq, L1_gnn_Wk, L1_gnn_bk, L1_gnn_Wv, L1_gnn_bv, L1_gnn_Wo, L1_gnn_bo), axis=-1)
    x = _layernorm(x + _L2_gnn_ref(x, edge_index, edge_attr_128, node_vec1, node_vec1_n2, L2_gnn_z_in, L2_gnn_z_out, L2_gnn_W_cent, L2_gnn_b_cent, L2_gnn_W_vor, L2_gnn_b_vor, L2_gnn_W_sum, L2_gnn_b_sum), axis=-1)
    x = _layernorm(x + _L3_gnn_ref(x, edge_index, L3_gnn_W_in, L3_gnn_b_in, L3_gnn_W_out, L3_gnn_b_out, L3_gnn_W_ih, L3_gnn_b_ih, L3_gnn_W_hh, L3_gnn_b_hh), axis=-1)
    return x

_drawn_inputs = setup_inputs


def setup_inputs(seed=0):
    import zlib

    import numpy as np

    out = dict(_drawn_inputs(seed))
    spreads = {'L0_gnn_b1': (0.0, 2.0),
     'L0_gnn_g1': (1.0, 0.6),
     'L0_gnn_bt1': (0.0, 0.8),
     'L0_gnn_b2': (0.0, 2.0),
     'L0_gnn_g2': (1.0, 0.2),
     'L0_gnn_bt2': (0.0, 0.354),
     'L1_gnn_bq': (0.0, 0.733),
     'L1_gnn_bk': (0.0, 2.0),
     'L1_gnn_bv': (0.0, 0.1),
     'L1_gnn_bo': (0.0, 0.1),
     'L2_gnn_b_cent': (0.0, 2.0),
     'L2_gnn_b_vor': (0.0, 2.0),
     'L2_gnn_b_sum': (0.0, 0.1)}
    factors = {'node_vec1': 8.0,
     'node_vec1_n2': 8.0,
     'L2_gnn_W_cent': 3.894,
     'L2_gnn_W_vor': 4.192,
     'L3_gnn_b_in': 8.0,
     'L3_gnn_b_out': 7.585,
     'L3_gnn_b_ih': 4.763,
     'L3_gnn_b_hh': 7.011}
    for name, (base, spread) in spreads.items():
        noise = np.random.default_rng([zlib.crc32(name.encode()), seed]).standard_normal(out[name].shape)
        drawn = base * np.exp(spread * noise) if base else spread * noise
        out[name] = jnp.asarray(drawn.astype(out[name].dtype))
    for name, factor in factors.items():
        out[name] = (out[name] * factor).astype(out[name].dtype)
    return out
```

```python
import numpy as np
import concourse.bass as bass
from concourse import mybir
from contextlib import ExitStack

F32 = mybir.dt.float32
BF16 = mybir.dt.bfloat16
I32 = mybir.dt.int32
ALU = mybir.AluOpType
ACT = mybir.ActivationFunctionType
AX = mybir.AxisListType

P = 128
N, D, E, EA = 6250, 256, 106250, 128
HID = 2 * D
HEADS, HD = 8, 32
SCALE = 1.0 / float(np.sqrt(HD))
EPS = 1e-5
NW = -(-N // P)
NPAD = NW * P
TAIL = N - (NW - 1) * P
NC = -(-E // P) + 1
U = 16
IT = -(-(NC - 1 + NW - 1) // U)
STEPS = IT * U
ROWS = -(-STEPS // P) * P
RT = ROWS // P
HALF = U // 2
AW = D + HEADS
GROUPS = P // HEADS
GS = STEPS // GROUPS
SCAN = GS * P
PAD_DST = 1 << 20
BIG = 1e30
LOW = -1e37
BANKS = 4
SUMROWS = NPAD + P
EW = EA + 1
DEGMAX = 511

assert STEPS % GROUPS == 0 and STEPS >= NC - 1 + NW - 1 + 0


class Kit:
    pass


def sbuf(nc, ctx, name, shape, dt=F32):
    return ctx.enter_context(nc.sbuf_tensor(name, shape, dt))


class Arena:

    def __init__(self, region):
        self.region, self.at = region, 0

    def take(self, shape, dt=F32):
        words = int(np.prod(shape[1:])) * (2 if dt == BF16 else 4)
        words = -(-words // 4)
        part = self.region[0:shape[0], self.at:self.at + words]
        self.at += words
        assert self.at <= self.region.shape[1], (self.at, self.region.shape)
        if dt != F32:
            part = part.bitcast(dt)
        if len(shape) == 3:
            part = part.rearrange("p (a b) -> p a b", a=shape[1])
        return part


def psum(nc, ctx, name, shape, dt=F32):
    return ctx.enter_context(nc.psum_tensor(name, shape, dt))


def sems(nc, k, *names):
    new = [nc.alloc_semaphore(n) for n in names]
    k.stage_sems += new
    return new


def end_stage(nc, k):
    nc.clear_and_free_semaphores(k.stage_sems)
    k.stage_sems = []
    nc.all_engine_barrier()


def load_steps(nc, engine, row, it, top):
    return nc.values_load_multi_w_load_instructions(
        row[0:1, bass.ds(it * U, U)], engines=[engine.engine], min_val=0, max_val=top,
        skip_runtime_bounds_check_because="step_tables clamps the entries")[1]


def step_tables(nc, k, dst_rows, src_rows, x_rows):
    with ExitStack() as ctx:
        room = Arena(k.big[:, :])
        last_i = room.take([1, NC], I32)
        last_f = room.take([1, NC])
        limit = room.take([NW - 1, 1])
        wnum = room.take([NW - 1, 1])
        ahead = room.take([NW - 1, NC])
        count = room.take([NW - 1, 1])
        ends = room.take([NW - 1, 1])
        step_no = room.take([NW - 1, ROWS])
        ended = room.take([NW - 1, ROWS])
        step_col = room.take([P, RT])
        win_col = room.take([P, RT])
        base_col = room.take([P, RT])
        chunk_f = room.take([P, RT])
        chunk_i = room.take([P, RT], I32)
        crow_f = room.take([1, ROWS])
        dst_i = room.take([P, RT, P], I32)
        src_i = room.take([P, RT, P], I32)
        dst_f = room.take([P, RT, P])
        src_f = room.take([P, RT, P])
        key_f = room.take([P, RT, P])
        flag = room.take([P, ROWS])
        low_key = room.take([1, 1])
        last_ps = psum(nc, ctx, "last_ps", [NW - 1, 2, 512])
        wrow_ps = psum(nc, ctx, "wrow_ps", [1, 2, 512])
        wcol_ps = psum(nc, ctx, "wcol_ps", [P, RT])
        turn_ps = [psum(nc, ctx, f"turn_ps{i}", [P, P]) for i in range(2)]
        (s_last, s_x, s_const, s_ident, s_lastf, s_lastb, s_count, s_ended, s_wps, s_chunk, s_gat, s_rel, s_rows,
         s_turn, s_tab, s_dve) = sems(
            nc, k, "t_last", "t_x", "t_const", "t_ident", "t_lastf", "t_lastb", "t_count", "t_ended", "t_wps",
            "t_chunk", "t_gat", "t_rel", "t_rows", "t_turn", "t_tab", "t_dve")
        HB, HR = NC // 2, ROWS // 2
        block = ctx.enter_context(nc.Block())

        @block.sync
        def _(sp):
            sp.dma_start(last_i[:, :], dst_rows[:, P - 1:P].rearrange("c o -> o c"),
                         allow_slow_non_contiguous=True).then_inc(s_last, 16)
            sp.dma_start(k.X, x_rows.rearrange("(w p) d -> p w d", p=P)).then_inc(s_x, 16)
            sp.wait_ge(s_rel, 3 * RT)
            sp.dma_start(k.dst_row.rearrange("(t p) e -> p t e", p=P), dst_f[:, :, :]).then_inc(s_rows, 16)
            sp.dma_start(k.src_row.rearrange("(t p) e -> p t e", p=P), src_f[:, :, :]).then_inc(s_rows, 16)
            sp.dma_start(k.key_row[P:].rearrange("(t p e) -> p t e", p=P, e=P), key_f[:, :, :]).then_inc(s_rows, 16)
            sp.dma_start(k.key_row[P - 1:P].rearrange("(a b) -> a b", a=1), low_key[:, :]).then_inc(s_rows, 16)
            sp.wait_ge(s_rows, 64)
            sp.wait_ge(s_x, 16)

        @block.gpsimd
        def _(pool):
            iota = lambda out, pattern, base, mult: pool.iota(
                out, pattern, base=base, channel_multiplier=mult, allow_small_or_imprecise_dtypes=True)
            pool.memset(k.ident[:, :], 0.0).then_inc(s_ident, 1)
            pool.memset(k.ones[:, :], 1.0).then_inc(s_const, 1)
            pool.memset(k.eps[:, :], EPS)
            pool.memset(low_key[:, :], -5.0).then_inc(s_const, 1)
            iota(limit[:, :], [[0, 1]], P, P).then_inc(s_const, 1)
            iota(wnum[:, :], [[0, 1]], 0, 1).then_inc(s_const, 1)
            iota(step_no[:, :], [[1, ROWS]], 0, 0).then_inc(s_const, 1)
            iota(step_col[:, :], [[P, RT]], 0, 1).then_inc(s_const, 1)
            iota(k.iota_row[:, :], [[1, P]], 0, 0).then_inc(s_const, 1)
            iota(k.iota_col[:, :], [[0, 1]], 0, 1).then_inc(s_const, 1)
            iota(k.trash[:, :], [[0, 1]], NPAD, 1).then_inc(s_const, 1)
            pool.wait_ge(s_ident, 1)
            pool.affine_select(out=k.ident[:, :], in_=k.ident[:, :], compare_op=ALU.not_equal, fill=1.0, base=0,
                               pattern=[[-1, P]], channel_multiplier=1).then_inc(s_ident, 1)
            pool.wait_ge(s_const, 1)
            pool.affine_select(out=k.below[:, :], in_=k.ones[:, :], compare_op=ALU.is_gt, fill=0.0, base=0,
                               pattern=[[-1, P]], channel_multiplier=1).then_inc(s_const, 1)
            pool.wait_ge(s_chunk, 1)
            for t in range(RT):
                for table, rows in ((dst_i, dst_rows), (src_i, src_rows)):
                    pool.indirect_dma_start(table[:, t, :], None, rows,
                                            bass.IndirectOffsetOnAxis(ap=chunk_i[:, t:t + 1], axis=0)).then_inc(s_gat, 16)
            pool.wait_ge(s_gat, 32 * RT)

        @block.tensor
        def _(pe):
            pe.wait_ge(s_const, 10)
            pe.wait_ge(s_lastf, 1)
            for h in range(2):
                pe.matmul(last_ps[:, h, 0:HB], k.ones[0:1, 0:NW - 1], last_f[:, h * HB:(h + 1) * HB],
                          start=True, stop=True).then_inc(s_lastb, 1)
            pe.wait_ge(s_ended, 1)
            for h in range(2):
                pe.matmul(wrow_ps[:, h, 0:HR], k.ones[0:NW - 1, 0:1], ended[:, h * HR:(h + 1) * HR],
                          start=True, stop=True).then_inc(s_wps, 1)
            for t in range(RT):
                pe.matmul(wcol_ps[:, t:t + 1], ended[:, t * P:(t + 1) * P], k.ones[0:NW - 1, 0:1],
                          start=True, stop=True).then_inc(s_wps, 1)
            pe.wait_ge(s_ident, 2)
            for t in range(RT):
                for n, rows in enumerate((dst_f, src_f)):
                    pe.wait_ge(s_rel, 3 * t + 1 + n)
                    if t:
                        pe.wait_ge(s_tab, 2 * t - 1 + n)
                    pe.transpose(turn_ps[n][:, :], rows[:, t, :], k.ident[:, :]).then_inc(s_turn, 1)

        @block.vector
        def _(dve):
            dve.wait_ge(s_last, 16)
            dve.tensor_copy(last_f[:, :], last_i[:, :]).then_inc(s_lastf, 1)
            dve.wait_ge(s_lastb, 2)
            dve.wait_ge(s_const, 10)
            dve.tensor_scalar(ahead[:, :].rearrange("w (h c) -> w h c", h=2), last_ps[:, :, 0:HB], limit[:, 0:1], None,
                              ALU.is_lt).then_inc(s_dve, 1)
            dve.wait_ge(s_dve, 1)
            dve.tensor_reduce(count[:, :], ahead[:, :], AX.X, ALU.add).then_inc(s_dve, 1)
            dve.wait_ge(s_dve, 2)
            dve.tensor_tensor(ends[:, :], count[:, :], wnum[:, :], ALU.add).then_inc(s_dve, 1)
            dve.wait_ge(s_dve, 3)
            dve.tensor_scalar(ended[:, :], step_no[:, :], ends[:, 0:1], None, ALU.is_gt).then_inc(s_ended, 1)
            dve.wait_ge(s_wps, 2 + RT)
            dve.tensor_copy(win_col[:, :], wcol_ps[:, :]).then_inc(s_dve, 1)
            dve.tensor_copy(k.win[:, :].rearrange("o (h c) -> o h c", h=2), wrow_ps[:, :, 0:HR]).then_inc(s_dve, 1)
            dve.tensor_tensor(crow_f[:, :].rearrange("o (h c) -> o h c", h=2),
                              step_no[0:1, :].rearrange("o (h c) -> o h c", h=2), wrow_ps[:, :, 0:HR],
                              ALU.subtract).then_inc(s_dve, 1)
            dve.wait_ge(s_dve, 4)
            dve.tensor_scalar(base_col[:, :], win_col[:, :], float(P), None, ALU.mult).then_inc(s_dve, 1)
            dve.tensor_tensor(chunk_f[:, :], step_col[:, :], win_col[:, :], ALU.subtract).then_inc(s_dve, 1)
            dve.wait_ge(s_dve, 8)
            dve.tensor_scalar(chunk_i[:, :], chunk_f[:, :], float(NC - 1), None, ALU.min).then_inc(s_chunk, 1)
            dve.tensor_scalar(k.chunk[:, :], crow_f[:, :], float(NC - 1), None, ALU.min).then_inc(s_dve, 1)
            dve.wait_ge(s_gat, 32 * RT)
            for t in range(RT):
                dve.tensor_scalar(dst_f[:, t, :], dst_i[:, t, :], base_col[:, t:t + 1], None,
                                  ALU.subtract).then_inc(s_rel, 1)
                dve.tensor_copy(src_f[:, t, :], src_i[:, t, :]).then_inc(s_rel, 1)
                dve.wait_ge(s_rel, 3 * t + 1)
                dve.tensor_scalar(key_f[:, t, :], dst_f[:, t, :], -0.5, P - 0.5, ALU.max, ALU.min).then_inc(s_dve, 1)
                dve.wait_ge(s_dve, 10 + t)
                dve.tensor_scalar(key_f[:, t, :], key_f[:, t, :], base_col[:, t:t + 1], None,
                                  ALU.add).then_inc(s_rel, 1)
            for t in range(RT):
                dve.wait_ge(s_turn, 2 * t + 1)
                dve.tensor_copy(k.dst[:, t * P:(t + 1) * P], turn_ps[0][:, :]).then_inc(s_tab, 1)
                dve.wait_ge(s_turn, 2 * t + 2)
                dve.tensor_copy(k.src[:, t * P:(t + 1) * P], turn_ps[1][:, :]).then_inc(s_tab, 1)
            dve.wait_ge(s_tab, 2 * RT)
            dve.tensor_scalar(flag, k.dst[:, :], 0.0, None, ALU.is_ge).then_inc(s_dve, 1)
            dve.wait_ge(s_dve, 10 + RT)
            dve.scalar_tensor_tensor(out=k.inside[:, :], in0=k.dst[:, :], scalar=float(P), in1=flag,
                                     op0=ALU.is_lt, op1=ALU.mult).then_inc(s_dve, 1)
            dve.tensor_copy(k.idx[:, :], k.src[:, :]).then_inc(s_dve, 1)


def gather_sums(nc, k, tag, table, first):
    width = D + 1 if first else D
    with ExitStack() as ctx:
        room = Arena(k.side)
        ring = room.take([P, U, D + 1])
        spread = room.take([P, U, P]) if first else None
        onehot = room.take([P, 4, P])
        cur_idx = room.take([P, U], I32)
        cur_dst = room.take([P, U])
        cur_src = room.take([P, U])
        same = room.take([P, P], BF16)
        before = room.take([P, U])
        away = room.take([P, U])
        sums = [psum(nc, ctx, f"{tag}_sums{i}", [P, 512]) for i in range(4)]
        s_zero, s_cur, s_tick, s_hot, s_sum, s_acc, s_seen, s_idx, s_clear = sems(
            nc, k, *(f"{tag}_{n}" for n in ("zero", "cur", "tick", "hot", "sum", "acc", "seen", "idx", "clear")))
        s_spread = sems(nc, k, *(f"{tag}_spread{h}" for h in range(2))) if first else None
        s_row, row0 = k.s_row, k.rows_before
        k.rows_before += 16 * IT
        block = ctx.enter_context(nc.Block())

        @block.gpsimd
        def _(pool):
            with pool.Fori(0, IT) as it:
                for u in range(U):
                    if u % HALF == 0:
                        pool.wait_ge(s_cur, it * 2 + (1 + u // HALF))
                    pool.wait_ge(s_sum, it * U + (u + 1))
                    pool.sem_inc(s_tick, 1)
                    pool.indirect_dma_start(ring[:, u, 0:D], None, table, bass.IndirectOffsetOnAxis(
                        ap=cur_idx[:, u:u + 1], axis=0)).then_inc(s_row[u], 16)

        if first:
            @block.sync
            def _(sp):
                sp.wait_ge(s_zero, 2)
                for b in range(BANKS):
                    sp.dma_start(k.attr_sum[b].rearrange("(p r) d -> p (r d)", p=P),
                                 k.sims[:, 0:SUMROWS // P * EW]).then_inc(s_clear, 16)
                    for half in range(2):
                        sp.dma_start(k.out_sum[b].rearrange("(p h r) d -> p h (r d)", p=P, h=2)[:, half, :],
                                     k.sims[:, 0:SUMROWS // P * D // 2]).then_inc(s_clear, 16)
                with sp.Fori(0, IT) as it:
                    for h in range(2):
                        sp.wait_ge(s_seen, it * U + (h + 1) * HALF)
                        sp.dma_start(spread[:, h * HALF:(h + 1) * HALF, :].rearrange("p u e -> p (u e)"),
                                     k.src_row[bass.ds(it * U + h * HALF, HALF), :].rearrange(
                                         "(o u) e -> o (u e)", o=1).to_broadcast([P, HALF * P])).then_inc(s_spread[h], 16)
                sp.wait_ge(s_clear, 16 * 3 * BANKS)

        @block.tensor
        def _(pe):
            pe.sem_inc(s_sum, U)
            with pe.Fori(0, IT) as it:
                for u in range(U):
                    pe.wait_ge(s_row[u], it * 16 + (row0 + 16))
                    pe.wait_ge(s_hot, it * U + (u + 1))
                    pe.wait_ge(s_acc, it * U + (u + 1))
                    pe.matmul(sums[u % 4][:, 0:width], onehot[:, u % 4, :], ring[:, u, 0:width],
                              start=True, stop=True).then_inc(s_sum, 1)

        @block.vector
        def _(dve):
            def refill(h, at):
                part = slice(h * HALF, (h + 1) * HALF)
                dve.tensor_copy(cur_dst[:, part], k.dst[:, bass.ds(at, HALF)])
                if first:
                    dve.tensor_copy(cur_src[:, part], k.src[:, bass.ds(at, HALF)])
                dve.tensor_copy(cur_idx[:, part], k.idx[:, bass.ds(at, HALF)]).then_inc(s_cur, 1)

            def hot(it, u):
                dve.wait_ge(s_sum, it * U + (u + 1 + U - 4))
                dve.tensor_scalar(onehot[:, u % 4, :], k.iota_row[:, :], cur_dst[:, u:u + 1], None,
                                  ALU.is_equal).then_inc(s_hot, 1)

            def add(it, u, win):
                dve.wait_ge(s_sum, it * U + (u + 1 + U))
                dve.wait_ge(s_acc, it * U + (u + 4))
                here = k.acc[:, bass.ds(win * AW, width)]
                dve.tensor_tensor(here, sums[u % 4][:, 0:width], here, ALU.add).then_inc(s_acc, 1)

            def compare(it, u):
                if u % HALF == 0:
                    dve.wait_ge(s_spread[u // HALF], it * 16 + 16)
                dve.wait_ge(s_seen, it * U + (U + u))
                dve.scalar_tensor_tensor(out=same[:, :], in0=spread[:, u, :], scalar=cur_src[:, u:u + 1],
                                         in1=k.below[:, :], op0=ALU.is_equal, op1=ALU.mult,
                                         accum_out=before[:, u:u + 1]).then_inc(s_seen, 1)

            def scatter_rows(it, h):
                part = slice(h * HALF, (h + 1) * HALF)
                dve.wait_ge(s_seen, it * U + (U + (h + 1) * HALF))
                dve.tensor_scalar(before[:, part], before[:, part], 0.0, None, ALU.is_gt).then_inc(s_idx, 1)
                dve.tensor_scalar(away[:, part], cur_src[:, part], -1.0, k.trash[:, 0:1], ALU.mult,
                                  ALU.add).then_inc(s_idx, 1)
                dve.wait_ge(s_idx, it * 8 + (4 * h + 2))
                dve.tensor_tensor(away[:, part], away[:, part], before[:, part], ALU.mult).then_inc(s_idx, 1)
                dve.wait_ge(s_idx, it * 8 + (4 * h + 3))
                dve.tensor_tensor(k.sidx[:, bass.ds(it * U + h * HALF, HALF)], away[:, part], cur_src[:, part],
                                  ALU.add).then_inc(s_idx, 1)
                dve.wait_ge(s_idx, it * 8 + (4 * h + 4))

            dve.memset(k.acc[:, :], 0.0)
            if first:
                dve.memset(k.sims[:, :], 0.0).then_inc(s_zero, 1)
                dve.memset(ring[:, :, D:D + 1], 1.0).then_inc(s_zero, 1)
                dve.wait_ge(s_zero, 2)
                dve.sem_inc(s_seen, U)
            for h in range(2):
                refill(h, h * HALF)
            dve.sem_inc(s_acc, 4)
            with dve.Fori(0, IT) as it:
                win = load_steps(nc, dve, k.win, it, NW - 1)
                for h in range(2):
                    dve.wait_ge(s_cur, it * 2 + (1 + h))
                    for u in range(h * HALF, (h + 1) * HALF):
                        if u % HALF == 0:
                            hot(it, u)
                            hot(it, u + 1)
                        if u % HALF + 2 < HALF:
                            hot(it, u + 2)
                        if first:
                            compare(it, u)
                        add(it, u, win[u])
                    if first:
                        scatter_rows(it, h)
                    refill(h, it * U + (U + h * HALF))


def scatter_attributes(nc, k, attr_rows):
    with ExitStack() as ctx:
        room = Arena(k.side)
        ring = room.take([P, U, EW])
        spread = room.take([P, U, P])
        equal = room.take([P, 4, P])
        ready = room.take([P, HALF, EW])
        cur_src = room.take([P, U])
        cur_in = room.take([P, U])
        cur_row = room.take([P, U], I32)
        spare = room.take([P, 1], I32)
        sums = [psum(nc, ctx, f"at_sums{i}", [P, 512]) for i in range(4)]
        s_one, s_cur, s_rowcur, s_equal, s_mm, s_ready, s_prime, s_tick = sems(
            nc, k, *(f"at_{n}" for n in ("one", "cur", "rowcur", "equal", "mm", "ready", "prime", "tick")))
        s_attr = sems(nc, k, *(f"at_attr{u}" for u in range(U)))
        s_spread = sems(nc, k, *(f"at_spread{h}" for h in range(2)))
        s_sent = k.s_sent
        block = ctx.enter_context(nc.Block())

        @block.sync
        def _(sp):
            with sp.Fori(0, IT) as it:
                chunk = load_steps(nc, sp, k.chunk, it, NC - 1)
                for u in range(U):
                    sp.wait_ge(s_mm, it * U + (u // HALF + 1) * HALF if u % HALF == 0 else it * U + (u + 1))
                    if u % HALF == 0:
                        sp.dma_start(spread[:, u:u + HALF, :].rearrange("p u e -> p (u e)"),
                                     k.src_row[bass.ds(it * U + u, HALF), :].rearrange(
                                         "(o u) e -> o (u e)", o=1).to_broadcast([P, HALF * P])).then_inc(
                                             s_spread[u // HALF], 16)
                    sp.dma_start(ring[:, u, 0:EA], attr_rows[bass.ds(chunk[u] * P, P), :]).then_inc(s_attr[u], 16)

        @block.vector
        def _(dve):
            def refill(h, at):
                part = slice(h * HALF, (h + 1) * HALF)
                dve.tensor_copy(cur_src[:, part], k.src[:, bass.ds(at, HALF)])
                dve.tensor_copy(cur_in[:, part], k.inside[:, bass.ds(at, HALF)]).then_inc(s_cur, 1)

            dve.memset(ring[:, :, EA:EW], 1.0).then_inc(s_one, 1)
            dve.memset(ready[:, :, :], 0.0).then_inc(s_prime, 1)
            dve.tensor_copy(spare[:, :], k.trash[:, :]).then_inc(s_prime, 1)
            for h in range(2):
                refill(h, h * HALF)
            with dve.Fori(0, IT) as it:
                for h in range(2):
                    part = slice(h * HALF, (h + 1) * HALF)
                    dve.wait_ge(s_ready, it * U + (U + h * HALF))
                    dve.tensor_copy(cur_row[:, part], k.sidx[:, bass.ds(it * U + h * HALF, HALF)]).then_inc(s_rowcur, 1)
                    dve.wait_ge(s_cur, it * 2 + (h + 1))
                    dve.wait_ge(s_spread[h], it * 16 + 16)
                    for u in range(h * HALF, (h + 1) * HALF):
                        dve.wait_ge(s_mm, it * U + (u + 1 + U - 4))
                        dve.tensor_scalar(equal[:, u % 4, :], spread[:, u, :], cur_src[:, u:u + 1], cur_in[:, u:u + 1],
                                          ALU.is_equal, ALU.mult).then_inc(s_equal, 1)
                    dve.wait_ge(s_equal, it * U + (h + 1) * HALF)
                    refill(h, it * U + (U + h * HALF))

        @block.tensor
        def _(pe):
            pe.sem_inc(s_mm, U)
            pe.wait_ge(s_one, 1)
            with pe.Fori(0, IT) as it:
                for u in range(U):
                    pe.wait_ge(s_attr[u], it * 16 + 16)
                    pe.wait_ge(s_equal, it * U + (u + 1))
                    pe.wait_ge(s_ready, it * U + (U + u + 1 - 4))
                    pe.matmul(sums[u % 4][:, 0:EW], equal[:, u % 4, :], ring[:, u, :],
                              start=True, stop=True).then_inc(s_mm, 1)

        @block.scalar
        def _(act):
            act.sem_inc(s_ready, U)
            with act.Fori(0, IT) as it:
                for u in range(U):
                    act.wait_ge(s_mm, it * U + (U + u + 1))
                    act.wait_ge(s_sent[u % HALF], it * 32 + 16 * (1 + u // HALF))
                    act.copy(ready[:, u % HALF, :], sums[u % 4][:, 0:EW]).then_inc(s_ready, 1)

        @block.gpsimd
        def _(pool):
            pool.wait_ge(s_prime, 2)
            for v in range(HALF):
                if v >= BANKS:
                    pool.wait_ge(s_sent[v - BANKS], 16)
                pool.indirect_dma_start(k.attr_sum[v % BANKS], bass.IndirectOffsetOnAxis(ap=spare[:, 0:1], axis=0),
                                        ready[:, v, :], None, compute_op=ALU.add).then_inc(s_sent[v], 16)
            with pool.Fori(0, IT) as it:
                for u in range(U):
                    if u % HALF == 0:
                        pool.wait_ge(s_rowcur, it * 2 + (u // HALF + 1))
                    pool.wait_ge(s_ready, it * U + (U + u + 1))
                    pool.wait_ge(s_sent[(u - BANKS) % HALF], it * 32 + 16 * (2 + (u - BANKS) // HALF))
                    pool.sem_inc(s_tick, 1)
                    pool.indirect_dma_start(k.attr_sum[u % BANKS], bass.IndirectOffsetOnAxis(ap=cur_row[:, u:u + 1], axis=0),
                                            ready[:, u % HALF, :], None, compute_op=ALU.add).then_inc(s_sent[u % HALF], 16)
            for v in range(HALF):
                pool.wait_ge(s_sent[v], 16 * (1 + 2 * IT))


def node_window(w):
    return bass.ds(w * D, D)


def sum_window(w, width=D):
    return bass.ds(w * AW, width)


def over_windows(engine, *stages):
    lead = 4

    def place(n):
        for function, lag in stages:
            if 0 <= n - lag < NW:
                function(n - lag, (n - lag) % 2, TAIL if n - lag == NW - 1 else P)

    for n in range(lead):
        place(n)
    with engine.Fori(0, (NW - 1 - lead) // 2) as pair:
        for half in range(2):
            for function, lag in stages:
                function(pair * 2 + (lead + half - lag), (half - lag) % 2, P)
    for n in range(NW - 1, NW + max(lag for _, lag in stages)):
        place(n)


def row_moments(dve, k, x, stats, chain, base):
    dve.bn_stats(stats[:, 0:6], x).then_inc(chain, 1)
    dve.wait_ge(chain, base + 1)
    dve.sem_inc(k.s_hold, 1)
    return dve.bn_aggr(stats[:, 6:8], stats[:, 0:6])


def gin_front(nc, k, g, tag, t_free):
    s_z, s_zps, s_zt, s_t = sems(nc, k, *(f"{tag}_{n}" for n in ("z", "zps", "zt", "t")))
    x = k.X.rearrange("p w d -> p (w d)")

    def combine(dve):
        def stage(w, slot, nodes):
            dve.wait_ge(s_zps, w + 1)
            dve.scalar_tensor_tensor(out=g.z[:, slot, :], in0=x[:, node_window(w)], scalar=g.eps1[:, 0:1],
                                     in1=k.acc[:, sum_window(w)], op0=ALU.mult, op1=ALU.add).then_inc(s_z, 1)
        return stage

    def turn(pe):
        pe.sem_inc(s_zps, 2)
        pe.sem_inc(s_t, 2)

        def stage(w, slot, nodes):
            pe.wait_ge(s_z, w + 1)
            pe.wait_ge(s_zt, w + 1)
            for c in range(2):
                ins = pe.transpose(g.zps[slot][:, c * P:(c + 1) * P], g.z[:, slot, c * P:(c + 1) * P], k.ident[:, :])
            ins.then_inc(s_zps, 1)
        return stage

    def copy_turned(act):
        act.sem_inc(s_zt, 2)

        def stage(w, slot, nodes):
            act.wait_ge(s_zps, w + 3)
            act.wait_ge(s_t, w + 1)
            act.copy(g.zt[:, slot, :], g.zps[slot][:, 0:D]).then_inc(s_zt, 1)
        return stage

    def hidden(pe):
        def stage(w, slot, nodes):
            pe.wait_ge(s_zt, w + 3)
            pe.wait_ge(t_free, w + 1)
            for m in range(4):
                for c in range(2):
                    ins = pe.matmul(g.tps[slot][:, m * P:(m + 1) * P], g.w1[:, c, m * P:(m + 1) * P],
                                    g.zt[:, slot, c * P:(c + 1) * P], start=(c == 0), stop=(c == 1))
            ins.then_inc(s_t, 1)
        return stage

    return combine, turn, copy_turned, hidden, s_t


def gin_mlp(nc, k, a):
    with ExitStack() as ctx:
        g = Kit()
        room = Arena(k.side)
        g.w1 = room.take([P, 2, HID])
        w2 = room.take([P, 4, D])
        b2 = room.take([P, D])
        cols = room.take([P, 3, 4])
        g2 = room.take([1, D])
        bt2 = room.take([1, D])
        g.eps1 = room.take([P, 1])
        g.z = room.take([P, 2, D])
        g.zt = room.take([P, 2, D])
        act1 = room.take([P, 2, HID])
        ustat = room.take([P, 2, HID])
        stats = room.take([P, 4, NW * 6])
        moments = room.take([P, 4, 2])
        scale1 = room.take([P, 4])
        shift1 = room.take([P, 4])
        mean1 = room.take([P, 4])
        root1 = room.take([P, 4])
        row = room.take([1, 4, D])
        zero = room.take([P, HID])
        g.zps = [psum(nc, ctx, f"gin_z{i}", [P, 512]) for i in range(2)]
        g.tps = [psum(nc, ctx, f"gin_t{i}", [P, 512]) for i in range(2)]
        ups = [psum(nc, ctx, f"gin_u{i}", [P, 512]) for i in range(2)]
        tot_ps = psum(nc, ctx, "gin_tot", [1, 512])
        bc_ps = psum(nc, ctx, "gin_bc", [P, 512])
        x = k.X.rearrange("p w d -> p (w d)")
        s_w, s_eps, s_stat, s_norm1, s_act1, s_u, s_x, s_usum, s_usq, s_tot, s_row, s_bc, s_kept, s_zero, s_root = sems(
            nc, k, *(f"gin_{n}" for n in ("w", "eps", "stat", "norm1", "act1", "u", "x", "usum", "usq", "tot", "row",
                                          "bc", "kept", "zero", "root")))

        combine, turn, copy_turned, hidden, s_t = gin_front(nc, k, g, "gina", s_stat)
        with nc.Block() as block:
            @block.sync
            def _(sp):
                sp.dma_start(g.w1[:, :, :], a["L0_gnn_W1"].rearrange("(c p) m -> p c m", p=P)).then_inc(s_w, 16)
                sp.dma_start(w2[:, :, :], a["L0_gnn_W2"].rearrange("(c p) m -> p c m", p=P)).then_inc(s_w, 16)
                sp.dma_start(b2[:, :], a["L0_gnn_b2"].to_broadcast([P, D])).then_inc(s_w, 16)
                for n, name in enumerate(("L0_gnn_b1", "L0_gnn_g1", "L0_gnn_bt1")):
                    sp.dma_start(cols[:, n, :], a[name].rearrange("o (c p) -> p (o c)", p=P),
                                 allow_slow_non_contiguous=True).then_inc(s_w, 16)
                sp.dma_start(g2[:, :], a["L0_gnn_g2"]).then_inc(s_w, 16)
                sp.dma_start(bt2[:, :], a["L0_gnn_bt2"]).then_inc(s_w, 16)
                sp.dma_start(g.eps1[:, :], a["L0_gnn_eps_gin"].to_broadcast([P, 1])).then_inc(s_w, 16)

            @block.vector
            def _(dve):
                dve.tensor_copy(k.count_in[:, :], k.acc.rearrange("p (w d) -> p w d", d=AW)[:, :, D])
                dve.wait_ge(s_w, 16 * 9)
                dve.tensor_scalar(g.eps1[:, :], g.eps1[:, :], 1.0, None, ALU.add).then_inc(s_eps, 1)
                dve.sem_inc(s_stat, 2)
                dve.wait_ge(s_eps, 1)

                def measure(w, slot, nodes):
                    dve.wait_ge(s_t, w + 3)
                    for m in range(4):
                        ins = dve.bn_stats(stats[:, m, bass.ds(w * 6, 6)], g.tps[slot][:, m * P:m * P + nodes])
                    ins.then_inc(s_stat, 1)

                over_windows(dve, (combine(dve), 0), (measure, 1))
                dve.wait_ge(s_stat, NW + 2)
                for m in range(4):
                    dve.bn_aggr(moments[:, m, :], stats[:, m, :]).then_inc(s_norm1, 1)
                dve.wait_ge(s_norm1, 4)
                dve.wait_ge(s_root, 1)
                dve.reciprocal(scale1[:, :], root1[:, :]).then_inc(s_norm1, 1)
                dve.tensor_tensor(mean1[:, :], moments[:, :, 0], cols[:, 0, :], ALU.add).then_inc(s_norm1, 1)
                dve.wait_ge(s_norm1, 6)
                dve.tensor_tensor(scale1[:, :], scale1[:, :], cols[:, 1, :], ALU.mult).then_inc(s_norm1, 1)
                dve.tensor_tensor(shift1[:, :], cols[:, 0, :], mean1[:, :], ALU.subtract).then_inc(s_norm1, 1)
                dve.wait_ge(s_norm1, 8)
                dve.tensor_tensor(shift1[:, :], shift1[:, :], scale1[:, :], ALU.mult).then_inc(s_norm1, 1)
                dve.wait_ge(s_norm1, 9)
                dve.tensor_tensor(shift1[:, :], shift1[:, :], cols[:, 2, :], ALU.add).then_inc(s_norm1, 1)

            @block.tensor
            def _(pe):
                pe.wait_ge(s_w, 16 * 9)
                over_windows(pe, (turn(pe), 0), (hidden(pe), 1))

            @block.scalar
            def _(act):
                over_windows(act, (copy_turned(act), 0))
                act.wait_ge(s_norm1, 4)
                act.activation(root1[:, :], moments[:, :, 1], ACT.Sqrt, bias=k.eps[:, 0:1]).then_inc(s_root, 1)

        combine, turn, copy_turned, hidden, s_t = gin_front(nc, k, g, "ginb", s_act1)
        with nc.Block() as block:
            @block.vector
            def _(dve):
                dve.memset(zero[:, :], 0.0).then_inc(s_zero, 1)
                dve.sem_inc(s_u, 2)

                def close(w, slot, nodes):
                    dve.wait_ge(s_x, w + 3)
                    dve.wait_ge(s_tot, w + 1)
                    dve.tensor_tensor(ustat[:, slot, 0:D], ups[slot][:, 0:D], x[:, node_window(w)],
                                      ALU.add).then_inc(s_u, 1)
                    dve.wait_ge(s_u, w + 3)
                    dve.tensor_tensor(ustat[:, slot, 0:D], ustat[:, slot, 0:D], b2[:, :], ALU.add).then_inc(s_usum, 1)

                over_windows(dve, (combine(dve), 0), (close, 2))
                mean, var, scale, shift = (row[:, n, :] for n in range(4))
                dve.wait_ge(s_tot, NW + 2)
                dve.tensor_scalar(mean, tot_ps[:, 0:D], 1.0 / N, None, ALU.mult).then_inc(s_row, 1)
                dve.wait_ge(s_row, 1)
                dve.tensor_tensor(scale, mean, mean, ALU.mult).then_inc(s_row, 1)
                dve.wait_ge(s_row, 2)
                dve.scalar_tensor_tensor(out=var, in0=tot_ps[:, D:2 * D], scalar=1.0 / N, in1=scale, op0=ALU.mult,
                                         op1=ALU.subtract).then_inc(s_row, 1)
                dve.wait_ge(s_row, 3)
                dve.tensor_scalar(var, var, 0.0, None, ALU.max).then_inc(s_row, 1)
                dve.wait_ge(s_root, 2)
                dve.reciprocal(var, shift).then_inc(s_row, 1)
                dve.wait_ge(s_row, 5)
                dve.tensor_tensor(scale, var, g2[:, :], ALU.mult).then_inc(s_row, 1)
                dve.wait_ge(s_row, 6)
                dve.tensor_tensor(mean, mean, scale, ALU.mult).then_inc(s_row, 1)
                dve.wait_ge(s_row, 7)
                dve.tensor_tensor(shift, bt2[:, :], mean, ALU.subtract).then_inc(s_row, 1)
                dve.wait_ge(s_bc, 1)
                dve.tensor_copy(k.norm2, bc_ps[:, :])

            @block.scalar
            def _(act):
                act.sem_inc(s_act1, 2)
                act.sem_inc(s_kept, 2)

                def activate(w, slot, nodes):
                    act.wait_ge(s_t, w + 3)
                    act.wait_ge(s_x, w + 1)
                    for m in range(4):
                        ins = act.activation(act1[:, slot, m * P:(m + 1) * P], g.tps[slot][:, m * P:(m + 1) * P],
                                             ACT.Relu, bias=shift1[:, m:m + 1], scale=scale1[:, m:m + 1])
                    ins.then_inc(s_act1, 1)

                def square(w, slot, nodes):
                    act.wait_ge(s_usum, w + 1)
                    act.activation(ustat[:, slot, D:2 * D], ustat[:, slot, 0:D], ACT.Square).then_inc(s_usq, 1)
                    act.copy(k.acc[:, sum_window(w)], ustat[:, slot, 0:D]).then_inc(s_kept, 1)

                over_windows(act, (copy_turned(act), 0), (activate, 1), (square, 2))
                act.wait_ge(s_row, 4)
                act.activation(row[:, 3, :], row[:, 1, :], ACT.Sqrt, bias=k.eps[0:1, 0:1]).then_inc(s_root, 1)

            @block.tensor
            def _(pe):
                pe.sem_inc(s_x, 2)
                turn_z, hidden_t = turn(pe), hidden(pe)
                pe.wait_ge(s_zero, 1)
                pe.matmul(tot_ps[:, :], k.ones[:, 0:1], zero[:, :], start=True, stop=False, skip_group_check=True)
                pe.sem_inc(s_tot, 2)

                def product(w, slot, nodes):
                    pe.wait_ge(s_act1, w + 3)
                    pe.wait_ge(s_u, w + 1)
                    for m in range(4):
                        ins = pe.matmul(ups[slot][:, 0:D], act1[:, slot, m * P:(m + 1) * P], w2[:, m, :],
                                        start=(m == 0), stop=(m == 3))
                    ins.then_inc(s_x, 1)

                def column_sums(w, slot, nodes):
                    pe.wait_ge(s_usq, w + 1)
                    pe.wait_ge(s_kept, w + 3)
                    pe.matmul(tot_ps[:, :], k.ones[0:nodes, 0:1], ustat[0:nodes, slot, :], start=False,
                              stop=(nodes == TAIL), skip_group_check=True).then_inc(s_tot, 1)

                over_windows(pe, (turn_z, 0), (hidden_t, 1), (product, 2), (column_sums, 3))
                pe.wait_ge(s_row, 8)
                pe.matmul(bc_ps[:, :], k.ones[0:1, :], row[:, 2:4, :].rearrange("o a d -> o (a d)"),
                          start=True, stop=True).then_inc(s_bc, 1)


def gin_close_and_project(nc, k, a):
    with ExitStack() as ctx:
        room = Arena(k.sims[:, 2 * D:])
        wq = room.take([P, 2, D])
        wkv = room.take([P, 2, 2 * D])
        bias = room.take([P, 3 * D])
        new = room.take([P, 2, D])
        turned = room.take([P, 2, D])
        kv = room.take([P, 2, 2 * D])
        part = room.take([P, 2, D])
        stats = room.take([P, 2 * 9])
        zps = [psum(nc, ctx, f"qkv_z{i}", [P, 512]) for i in range(2)]
        qps = [psum(nc, ctx, f"qkv_q{i}", [P, 512]) for i in range(2)]
        kps = [psum(nc, ctx, f"qkv_k{i}", [P, 512]) for i in range(2)]
        x = k.X.rearrange("p w d -> p (w d)")
        s_w, s_part, s_mom, s_root, s_inv, s_new, s_kept, s_zps, s_zt, s_qkv, s_q, s_kv = sems(
            nc, k, *(f"qkv_{n}" for n in ("w", "part", "mom", "root", "inv", "new", "kept", "zps", "zt", "qkv", "q", "kv")))
        s_out = sems(nc, k, "qkv_out0", "qkv_out1")
        block = ctx.enter_context(nc.Block())

        @block.sync
        def _(sp):
            sp.dma_start(wq[:, :, :], a["wq_t"].rearrange("(c p) m -> p c m", p=P)).then_inc(s_w, 16)
            sp.dma_start(wkv[:, :, 0:D], a["wk_t"].rearrange("(c p) m -> p c m", p=P)).then_inc(s_w, 16)
            sp.dma_start(wkv[:, :, D:], a["wv_t"].rearrange("(c p) m -> p c m", p=P)).then_inc(s_w, 16)
            for n, name in enumerate(("L1_gnn_bq", "L1_gnn_bk", "L1_gnn_bv")):
                sp.dma_start(bias[:, n * D:(n + 1) * D], a[name].to_broadcast([P, D])).then_inc(s_w, 16)

            def send(w, slot, nodes):
                sp.wait_ge(s_kv, w + 1)
                sp.dma_start(k.kv_rows[bass.ds(w * P, P), :], kv[:, slot, :]).then_inc(s_out[slot], 16)

            over_windows(sp, (send, 0))
            sp.wait_ge(s_out[0], 16 * (NW + 1) // 2)
            sp.wait_ge(s_out[1], 16 * (NW // 2))

        @block.vector
        def _(dve):
            dve.sem_inc(s_new, 2)
            dve.wait_ge(s_w, 16 * 6)

            def norm(w, slot, nodes):
                st = stats[:, slot * 9:slot * 9 + 9]
                here = part[:, slot, :]
                dve.wait_ge(s_new, w + 1)
                dve.tensor_tensor(here, k.acc[:, sum_window(w)], k.norm2[:, 0:D], ALU.mult).then_inc(s_part, 1)
                dve.wait_ge(s_part, w * 4 + 1)
                dve.tensor_tensor(here, here, k.norm2[:, D:2 * D], ALU.add).then_inc(s_part, 1)
                dve.wait_ge(s_part, w * 4 + 2)
                dve.scalar_tensor_tensor(out=here, in0=here, scalar=0.0, in1=x[:, node_window(w)], op0=ALU.max,
                                         op1=ALU.add).then_inc(s_part, 1)
                dve.wait_ge(s_part, w * 4 + 3)
                row_moments(dve, k, here, st, s_part, w * 4 + 3).then_inc(s_mom, 1)

            def scale(w, slot, nodes):
                st = stats[:, slot * 9:slot * 9 + 9]
                dve.wait_ge(s_root, w + 1)
                dve.reciprocal(st[:, 8:9], st[:, 8:9]).then_inc(s_inv, 1)
                dve.wait_ge(s_inv, w + 1)
                dve.wait_ge(s_zps, w + 1)
                dve.wait_ge(s_kept, w + 1)
                dve.tensor_scalar(new[:, slot, :], part[:, slot, :], st[:, 6:7], st[:, 8:9], ALU.subtract,
                                  ALU.mult).then_inc(s_new, 1)

            def biases(w, slot, nodes):
                dve.wait_ge(s_qkv, w + 3)
                dve.tensor_tensor(k.side[:, node_window(w)], qps[slot][:, 0:D], bias[:, 0:D], ALU.add)
                if isinstance(w, int) and w < 2:
                    pass
                else:
                    dve.wait_ge(s_out[slot], (w - slot) * 8)
                dve.tensor_tensor(kv[:, slot, :], kps[slot][:, :], bias[:, D:], ALU.add).then_inc(s_kv, 1)

            over_windows(dve, (norm, 0), (scale, 1), (biases, 3))

        @block.tensor
        def _(pe):
            pe.sem_inc(s_zps, 2)
            pe.sem_inc(s_qkv, 2)
            pe.wait_ge(s_w, 16 * 6)

            def turn(w, slot, nodes):
                pe.wait_ge(s_new, w + 3)
                pe.wait_ge(s_zt, w + 1)
                for c in range(2):
                    ins = pe.transpose(zps[slot][:, c * P:(c + 1) * P], new[:, slot, c * P:(c + 1) * P], k.ident[:, :])
                ins.then_inc(s_zps, 1)

            def project(w, slot, nodes):
                pe.wait_ge(s_zt, w + 3)
                if isinstance(w, int) and w < 2:
                    pass
                else:
                    pe.wait_ge(s_kv, w - 1)
                for c in range(2):
                    pe.matmul(qps[slot][:, 0:D], turned[:, slot, c * P:(c + 1) * P], wq[:, c, :], start=(c == 0),
                              stop=(c == 1))
                for c in range(2):
                    ins = pe.matmul(kps[slot][:, :], turned[:, slot, c * P:(c + 1) * P], wkv[:, c, :], start=(c == 0),
                                    stop=(c == 1))
                ins.then_inc(s_qkv, 1)

            over_windows(pe, (turn, 1), (project, 2))

        @block.scalar
        def _(act):
            act.sem_inc(s_zt, 2)
            act.sem_inc(s_kept, 2)

            def keep(w, slot, nodes):
                act.wait_ge(s_new, w + 3)
                act.copy(x[:, node_window(w)], new[:, slot, :]).then_inc(s_kept, 1)
                act.wait_ge(s_zps, w + 3)
                act.wait_ge(s_qkv, w + 1)
                act.copy(turned[:, slot, :], zps[slot][:, 0:D]).then_inc(s_zt, 1)

            def root(w, slot, nodes):
                act.wait_ge(s_mom, w + 1)
                st = stats[:, slot * 9:slot * 9 + 9]
                act.activation(st[:, 8:9], st[:, 7:8], ACT.Sqrt, bias=k.eps[:, 0:1]).then_inc(s_root, 1)

            over_windows(act, (root, 0), (keep, 1))


def edge_scores(nc, k):
    with ExitStack() as ctx:
        room = Arena(k.acc)
        ring = room.take([P, U, 2 * D])
        spread = room.take([P, U, P])
        onehot = room.take([P, 4, P])
        prod = room.take([P, 2, D])
        cur_idx = room.take([P, U], I32)
        cur_sim = room.take([P, U, HEADS])
        query = k.side
        qps = [psum(nc, ctx, f"es_q{i}", [P, 512]) for i in range(4)]
        s_cur, s_tick, s_hot, s_q, s_prod, s_sim, s_stored, s_copied = sems(
            nc, k, *(f"es_{n}" for n in ("cur", "tick", "hot", "q", "prod", "sim", "stored", "copied")))
        s_spread = sems(nc, k, *(f"es_spread{h}" for h in range(2)))
        s_vout = sems(nc, k, *(f"es_vout{u}" for u in range(U)))
        s_row, row0 = k.s_row, k.rows_before
        k.rows_before += 16 * IT
        block = ctx.enter_context(nc.Block())

        @block.gpsimd
        def _(pool):
            with pool.Fori(0, IT) as it:
                for u in range(U):
                    if u % HALF == 0:
                        pool.wait_ge(s_cur, it * 2 + (1 + u // HALF))
                    pool.wait_ge(s_prod, it * U + (u + 1))
                    pool.wait_ge(s_stored, it * U + (u + 1))
                    pool.sem_inc(s_tick, 1)
                    pool.indirect_dma_start(ring[:, u, :], None, k.kv_rows, bass.IndirectOffsetOnAxis(
                        ap=cur_idx[:, u:u + 1], axis=0)).then_inc(s_row[u], 16)

        @block.sync
        def _(sp):
            sp.sem_inc(s_stored, U)
            LAG = 4

            def stored(it, u):
                sp.wait_ge(s_vout[u], it * 16 + 16)
                sp.sem_inc(s_stored, 1)

            with sp.Fori(0, IT) as it:
                for u in range(U):
                    if u % HALF == 0:
                        sp.wait_ge(s_hot, it * U + (u + HALF))
                        sp.dma_start(spread[:, u:u + HALF, :].rearrange("p u e -> p (u e)"),
                                     k.dst_row[bass.ds(it * U + u, HALF), :].rearrange(
                                         "(o u) e -> o (u e)", o=1).to_broadcast([P, HALF * P])).then_inc(
                                             s_spread[u // HALF], 16)
                    sp.wait_ge(s_row[u], it * 16 + (row0 + 16))
                    sp.dma_start(k.v_edge[bass.ds(it * U * P + u * P, P), :], ring[:, u, D:]).then_inc(s_vout[u], 16)
                    if u >= LAG:
                        stored(it, u - LAG)
                for u in range(U - LAG, U):
                    stored(it, u)

        @block.tensor
        def _(pe):
            pe.sem_inc(s_q, 4)
            with pe.Fori(0, IT) as it:
                win = load_steps(nc, pe, k.win, it, NW - 1)
                for u in range(U):
                    pe.wait_ge(s_hot, it * U + (U + u + 1))
                    pe.wait_ge(s_prod, it * U + (U + u + 1 - 4))
                    pe.matmul(qps[u % 4][:, 0:D], onehot[:, u % 4, :], query[:, node_window(win[u])],
                              start=True, stop=True).then_inc(s_q, 1)

        @block.vector
        def _(dve):
            def refill(h, at):
                part = slice(h * HALF, (h + 1) * HALF)
                dve.tensor_copy(cur_idx[:, part], k.idx[:, bass.ds(at, HALF)]).then_inc(s_cur, 1)

            def hot(it, u):
                dve.wait_ge(s_q, it * U + (u + 1))
                if u % HALF == 0:
                    dve.wait_ge(s_spread[u // HALF], it * 16 + 16)
                dve.tensor_scalar(onehot[:, u % 4, :], spread[:, u, :], k.iota_col[:, 0:1], None,
                                  ALU.is_equal).then_inc(s_hot, 1)

            def score(it, u):
                dve.wait_ge(s_q, it * U + (u + 1 + 4))
                dve.wait_ge(s_row[u], it * 16 + (row0 + 16))
                dve.wait_ge(s_sim, it * U + (u + 1))
                dve.tensor_tensor(prod[:, u % 2, :], qps[u % 4][:, 0:D], ring[:, u, 0:D], ALU.mult).then_inc(s_prod, 1)

            def heads(it, u):
                dve.wait_ge(s_prod, it * U + (U + u + 1))
                dve.tensor_reduce(cur_sim[:, u, :], prod[:, u % 2, :].rearrange("p (h d) -> p h d", h=HEADS), AX.X,
                                  ALU.add).then_inc(s_sim, 1)

            for h in range(2):
                refill(h, h * HALF)
            dve.sem_inc(s_hot, U)
            dve.sem_inc(s_prod, U)
            dve.sem_inc(s_sim, 2)
            with dve.Fori(0, IT) as it:
                for h in range(2):
                    for u in range(h * HALF, (h + 1) * HALF):
                        if u % HALF == 0:
                            hot(it, u)
                            hot(it, u + 1)
                        if u % HALF + 2 < HALF:
                            hot(it, u + 2)
                        score(it, u)
                        if u % HALF:
                            heads(it, u - 1)
                    heads(it, (h + 1) * HALF - 1)
                    dve.wait_ge(s_sim, it * U + ((h + 1) * HALF + 2))
                    dve.sem_inc(k.s_hold, 1)
                    dve.tensor_copy(k.sims[:, bass.ds(it * U * HEADS + h * HALF * HEADS, HALF * HEADS)],
                                    cur_sim[:, h * HALF:(h + 1) * HALF, :].rearrange("p u h -> p (u h)")).then_inc(
                                        s_copied, 1)
                    dve.wait_ge(s_copied, it * 2 + (h + 1))
                    dve.sem_inc(k.s_hold, 1)
                    refill(h, it * U + (U + h * HALF))


def softmax_weights(nc, k):
    T = 5
    with ExitStack() as ctx:
        room = Arena(k.big[:, :])
        one = room.take([P, SCAN])
        two = room.take([P, SCAN])
        three = room.take([P, SCAN])
        neg = room.take([P, STEPS])
        stage = room.take([P, T, P])
        edge = room.take([P, 2, 2])
        carry = room.take([P, 2])
        row_last = room.take([1, P])
        row_open = room.take([1, P])
        row_scan = room.take([1, P])
        row_in = room.take([1, P])
        tps = [psum(nc, ctx, f"sm_t{i}", [P, P]) for i in range(T)]
        rps = psum(nc, ctx, "sm_r", [1, 2, P])
        cps = psum(nc, ctx, "sm_c", [P, 2])
        s_key, s_mask, s_stage, s_turn, s_in, s_c, s_edge, s_row, s_col, s_back, s_bturn, s_out = sems(
            nc, k, *(f"sm_{n}" for n in ("key", "mask", "stage", "turn", "in", "c", "edge", "row", "col", "back",
                                         "bturn", "out")))
        sims = k.sims.rearrange("p (g j h) -> p j g h", g=GROUPS, h=HEADS)
        flat = k.key_row

        def keys(offset):
            run = flat[P + offset:P + offset + GROUPS * SCAN].rearrange("(g o t) -> g o t", g=GROUPS, o=1)
            return run.to_broadcast([GROUPS, HEADS, SCAN])

        block = ctx.enter_context(nc.Block())

        @block.sync
        def _(sp):
            sp.dma_start(one, keys(0)).then_inc(s_key, 16)
            sp.dma_start(two, keys(-1)).then_inc(s_key, 16)
            sp.wait_ge(s_c, 11)
            sp.dma_start(three, keys(0)).then_inc(s_key, 16)
            sp.dma_start(two, keys(1)).then_inc(s_key, 16)

        @block.scalar
        def _(act):
            act.sem_inc(s_stage, T)
            act.wait_ge(s_mask, 2)
            with act.Fori(0, GS // T) as it:
                for u in range(T):
                    act.wait_ge(s_turn, it * T + (u + 1))
                    act.copy(stage[:, u, :].rearrange("p (g h) -> p g h", g=GROUPS),
                             sims[:, bass.ds(it * T + u, 1), :, :].rearrange("p j g h -> p (j g) h")).then_inc(s_stage, 1)
            act.wait_ge(s_c, 22)
            with act.Fori(0, GS // T) as it:
                for u in range(T):
                    act.wait_ge(s_turn, it * T + (GS + u + 1))
                    act.copy(stage[:, u, :], three[:, bass.ds(it * T * P + u * P, P)]).then_inc(s_stage, 1)
            act.wait_ge(s_out, GS + T)
            act.activation(k.sims, k.sims, ACT.Exp, scale=SCALE).then_inc(s_back, 1)

        @block.tensor
        def _(pe):
            pe.sem_inc(s_turn, T)

            def turn(base):
                with pe.Fori(0, GS // T) as it:
                    for u in range(T):
                        pe.wait_ge(s_stage, it * T + (base + T + u + 1))
                        pe.wait_ge(s_in if base == 0 else s_out, it * T + (u + 1))
                        pe.transpose(tps[u][:, :], stage[:, u, :], k.ident[:, :]).then_inc(s_turn, 1)

            def edges(n):
                pe.wait_ge(s_edge, 2 * n + 2)
                pe.transpose(rps[:, 0, :], edge[:, n, 0:1], k.ident[:, :])
                pe.transpose(rps[:, 1, :], edge[:, n, 1:2], k.ident[:, :]).then_inc(s_row, 1)
                pe.wait_ge(s_col, n + 1)
                pe.matmul(cps[:, n:n + 1], row_in[:, :], k.ones[0:1, 0:1], start=True, stop=True).then_inc(s_row, 1)

            turn(0)
            edges(0)
            edges(1)
            turn(GS)

        @block.vector
        def _(dve):
            dve.tensor_scalar(neg[:, :], k.inside[:, 0:STEPS], BIG, -BIG, ALU.mult, ALU.add).then_inc(s_mask, 1)
            dve.wait_ge(s_mask, 1)
            by_step = k.sims.rearrange("p (i h) -> p i h", h=HEADS)
            dve.tensor_tensor(by_step, by_step, neg[:, :].unsqueeze(2).to_broadcast([P, STEPS, HEADS]),
                              ALU.add).then_inc(s_mask, 1)
            dve.sem_inc(s_in, T)
            with dve.Fori(0, GS // T) as it:
                for u in range(T):
                    dve.wait_ge(s_turn, it * T + (T + u + 1))
                    dve.tensor_scalar(three[:, bass.ds(it * T * P + u * P, P)], tps[u][:, :], 1.0, None,
                                      ALU.mult).then_inc(s_in, 1)

            def scan(n, out, key, near, data, lead, tail, done):
                flip = (lambda x: x) if n == 0 else (lambda x: x[:, ::-1])
                c = lambda: dve.wait_ge(s_c, done[0])

                def next_c(ins):
                    ins.then_inc(s_c, 1)
                    done[0] += 1
                next_c(dve.tensor_tensor(edge[:, n, 1:2], key[:, tail], near[:, lead], ALU.not_equal))
                c()
                dve.tensor_scalar(edge[:, n, 1:2], edge[:, n, 1:2], LOW, None, ALU.mult).then_inc(s_edge, 1)
                next_c(dve.tensor_tensor(near, key, near, ALU.not_equal))
                c()
                next_c(dve.tensor_scalar(near, near, LOW, None, ALU.mult))
                c()
                next_c(dve.tensor_tensor_scan(flip(out), flip(near), flip(data), LOW, ALU.add, ALU.max))
                c()
                dve.tensor_copy(edge[:, n, 0:1], out[:, tail]).then_inc(s_edge, 1)
                by_head = lambda row: row.rearrange("o (h g) -> o h g", h=HEADS)
                by_run = lambda row: row.rearrange("o (g h) -> o h g", h=HEADS)
                dve.wait_ge(s_row, 2 * n + 1)
                next_c(dve.tensor_copy(by_head(row_last), by_run(rps[:, 0, :])))
                next_c(dve.tensor_copy(by_head(row_open), by_run(rps[:, 1, :])))
                c()
                first = 0 if n == 0 else GROUPS - 1
                next_c(dve.memset(by_head(row_open)[:, :, first:first + 1], LOW))
                next_c(dve.memset(row_in[:, :], LOW))
                c()
                next_c(dve.tensor_tensor_scan(flip(row_scan), flip(row_open), flip(row_last), LOW, ALU.add, ALU.max))
                c()
                to, of = (slice(1, GROUPS), slice(0, GROUPS - 1)) if n == 0 else (slice(0, GROUPS - 1), slice(1, GROUPS))
                dve.tensor_copy(by_run(row_in)[:, :, to], by_head(row_scan)[:, :, of]).then_inc(s_col, 1)
                dve.wait_ge(s_row, 2 * n + 2)
                next_c(dve.tensor_copy(carry[:, n:n + 1], cps[:, n:n + 1]))
                c()
                next_c(dve.tensor_tensor_scan(flip(out), flip(near), flip(data), carry[:, n:n + 1], ALU.add, ALU.max))
                c()
            done = [0]
            start, end = slice(0, 1), slice(SCAN - 1, SCAN)
            dve.wait_ge(s_in, GS + T)
            dve.wait_ge(s_key, 32)
            scan(0, one, one, two, three, start, end, done)
            assert done[0] == 11, done
            dve.wait_ge(s_key, 64)
            scan(1, three, three, two, one, end, start, done)
            dve.sem_inc(s_out, T)
            with dve.Fori(0, GS // T) as it:
                for u in range(T):
                    here = sims[:, bass.ds(it * T + u, 1), :, :].rearrange("p j g h -> p (j g) h")
                    dve.wait_ge(s_turn, it * T + (GS + T + u + 1))
                    dve.tensor_tensor(here, here, tps[u][:, :].rearrange("p (g h) -> p g h", g=GROUPS),
                                      ALU.subtract).then_inc(s_out, 1)


def weighted_sums(nc, k):
    with ExitStack() as ctx:
        room = Arena(k.side)
        ring = room.take([P, U, D])
        weighted = room.take([P, 4, AW])
        onehot = room.take([P, 4, P])
        cur_dst = room.take([P, U])
        sums = [psum(nc, ctx, f"ws_sums{i}", [P, 512]) for i in range(4)]
        s_cur, s_hot, s_weight, s_side, s_sum, s_acc, s_zero = sems(
            nc, k, *(f"ws_{n}" for n in ("cur", "hot", "weight", "side", "sum", "acc", "zero")))
        s_v = sems(nc, k, *(f"ws_v{u}" for u in range(U)))
        block = ctx.enter_context(nc.Block())

        @block.sync
        def _(sp):
            with sp.Fori(0, IT) as it:
                for u in range(U):
                    sp.wait_ge(s_weight, it * U + (u + 1))
                    sp.dma_start(ring[:, u, :], k.v_edge[bass.ds(it * U * P + u * P, P), :]).then_inc(s_v[u], 16)

        @block.scalar
        def _(act):
            with act.Fori(0, IT) as it:
                for u in range(U):
                    act.wait_ge(s_sum, it * U + (u + 1))
                    act.copy(weighted[:, u % 4, D:], k.sims[:, bass.ds(it * U * HEADS + u * HEADS, HEADS)]).then_inc(
                        s_side, 1)

        @block.tensor
        def _(pe):
            pe.sem_inc(s_sum, 4)
            with pe.Fori(0, IT) as it:
                for u in range(U):
                    pe.wait_ge(s_weight, it * U + (U + u + 1))
                    pe.wait_ge(s_side, it * U + (u + 1))
                    pe.wait_ge(s_hot, it * U + (u + 1))
                    pe.wait_ge(s_acc, it * U + (u + 1))
                    pe.matmul(sums[u % 4][:, 0:AW], onehot[:, u % 4, :], weighted[:, u % 4, :],
                              start=True, stop=True).then_inc(s_sum, 1)

        @block.vector
        def _(dve):
            def refill(h, at):
                part = slice(h * HALF, (h + 1) * HALF)
                dve.tensor_copy(cur_dst[:, part], k.dst[:, bass.ds(at, HALF)]).then_inc(s_cur, 1)

            def weigh(it, u):
                dve.wait_ge(s_sum, it * U + (u + 1))
                dve.tensor_scalar(onehot[:, u % 4, :], k.iota_row[:, :], cur_dst[:, u:u + 1], None,
                                  ALU.is_equal).then_inc(s_hot, 1)
                dve.wait_ge(s_v[u], it * 16 + 16)
                weight = k.sims[:, bass.ds(it * U * HEADS + u * HEADS, HEADS)]
                dve.tensor_tensor(weighted[:, u % 4, 0:D].rearrange("p (h d) -> p h d", h=HEADS),
                                  ring[:, u, :].rearrange("p (h d) -> p h d", h=HEADS),
                                  weight.unsqueeze(2).to_broadcast([P, HEADS, HD]), ALU.mult).then_inc(s_weight, 1)

            def add(it, u, win):
                dve.wait_ge(s_sum, it * U + (u + 1 + 4))
                dve.wait_ge(s_acc, it * U + (u + 4))
                here = k.acc[:, sum_window(win, AW)]
                dve.tensor_tensor(here, sums[u % 4][:, 0:AW], here, ALU.add).then_inc(s_acc, 1)

            dve.memset(k.acc, 0.0).then_inc(s_zero, 1)
            dve.wait_ge(s_zero, 1)
            for h in range(2):
                refill(h, h * HALF)
            dve.sem_inc(s_weight, U)
            dve.sem_inc(s_acc, 4)
            with dve.Fori(0, IT) as it:
                win = load_steps(nc, dve, k.win, it, NW - 1)
                for h in range(2):
                    dve.wait_ge(s_cur, it * 2 + (1 + h))
                    for u in range(h * HALF, (h + 1) * HALF):
                        if u % HALF == 0:
                            weigh(it, u)
                            weigh(it, u + 1)
                        if u % HALF + 2 < HALF:
                            weigh(it, u + 2)
                        add(it, u, win[u])
                    refill(h, it * U + (U + h * HALF))


def node_terms(nc, k, a):
    terms = k.side
    with ExitStack() as ctx:
        room = Arena(k.sims)
        banks = room.take([P, 2 * BANKS, EW])
        z = room.take([P, 4, D])
        gates = room.take([P, 4, D])
        lines = room.take([P, 5, D])
        w_sum = room.take([P, D])
        sum_t = room.take([P, 2, P])
        degree = room.take([P, 2, P])
        index = room.take([P, 2, 2], I32)
        nodes_in = room.take([P, 2, NW])
        tps = [psum(nc, ctx, f"nt_t{i}", [P, 512]) for i in range(2)]
        pps = [psum(nc, ctx, f"nt_p{i}", [P, 512]) for i in range(2)]
        s_w, s_count, s_index, s_diag, s_line, s_gate, s_turn, s_turned, s_proj, s_part, s_tick = sems(
            nc, k, *(f"nt_{n}" for n in ("w", "count", "index", "diag", "line", "gate", "turn", "turned", "proj",
                                         "part", "tick")))
        s_bank = sems(nc, k, "nt_bank0", "nt_bank1")
        block = ctx.enter_context(nc.Block())

        @block.sync
        def _(sp):
            sp.dma_start(w_sum, a["L2_gnn_W_sum"]).then_inc(s_w, 16)
            for n, name in enumerate(("W_cent", "b_cent", "W_vor", "b_vor", "b_sum")):
                sp.dma_start(lines[:, n, :], a[f"L2_gnn_{name}"].to_broadcast([P, D])).then_inc(s_w, 16)
            sp.dma_start(nodes_in[:, 0, :], a["node_vec1_n2"]).then_inc(s_w, 16)
            sp.dma_start(nodes_in[:, 1, :], a["node_vec1"]).then_inc(s_w, 16)

            def load(w, slot, nodes):
                if not (isinstance(w, int) and w < 2):
                    sp.wait_ge(s_turn, w - 1)
                    sp.wait_ge(s_count, w - 1)
                for b in range(BANKS):
                    sp.dma_start(banks[:, slot * BANKS + b, :], k.attr_sum[b][bass.ds(w * P, P), :]).then_inc(
                        s_bank[slot], 16)

            over_windows(sp, (load, 0))

        @block.gpsimd
        def _(pool):
            def fetch(w, slot, nodes):
                pool.wait_ge(s_index, w * 2 + 2)
                pool.sem_inc(s_tick, 1)
                for n, table in enumerate((a["L2_gnn_z_in"], a["L2_gnn_z_out"])):
                    pool.indirect_dma_start(z[:, slot * 2 + n, :], None, table, bass.IndirectOffsetOnAxis(
                        ap=index[:, slot, n:n + 1], axis=0)).then_inc(k.s_z[slot], 16)

            over_windows(pool, (fetch, 1))

        @block.tensor
        def _(pe):
            pe.wait_ge(s_w, 16 * 8)

            def turn(w, slot, nodes):
                pe.wait_ge(s_bank[slot], (w - slot) * (8 * BANKS) + 16 * BANKS)
                if not (isinstance(w, int) and w < 2):
                    pe.wait_ge(s_turned, w - 1)
                for b in range(BANKS):
                    ins = pe.matmul(tps[slot][:, 0:P], banks[:, slot * BANKS + b, 0:EA], k.ident[:, :],
                                    start=(b == 0), stop=(b == BANKS - 1))
                ins.then_inc(s_turn, 1)

            def project(w, slot, nodes):
                pe.wait_ge(s_turned, w + 1)
                pe.wait_ge(s_diag, w + 1)
                if not (isinstance(w, int) and w < 2):
                    pe.wait_ge(s_part, w * 4 - 4)
                pe.matmul(pps[slot][:, 0:D], sum_t[:, slot, :], w_sum[:, :], start=True, stop=False)
                pe.matmul(pps[slot][:, 0:D], degree[:, slot, :], lines[:, 4, :], start=False, stop=True).then_inc(s_proj, 1)

            over_windows(pe, (turn, 0), (project, 1))

        @block.scalar
        def _(act):
            def copy_turned(w, slot, nodes):
                act.wait_ge(s_turn, w + 1)
                if not (isinstance(w, int) and w < 2):
                    act.wait_ge(s_proj, w - 1)
                act.copy(sum_t[:, slot, :], tps[slot][:, 0:P]).then_inc(s_turned, 1)

            def gate(w, slot, nodes):
                act.wait_ge(s_line, w * 2 + 2)
                act.activation(gates[:, slot * 2:slot * 2 + 2, :], gates[:, slot * 2:slot * 2 + 2, :],
                               ACT.Sigmoid).then_inc(s_gate, 1)

            over_windows(act, (copy_turned, 0), (gate, 1))

        @block.vector
        def _(dve):
            dve.wait_ge(s_w, 16 * 8)

            def count(w, slot, nodes):
                dve.wait_ge(s_bank[slot], (w - slot) * (8 * BANKS) + 16 * BANKS)
                dve.sem_inc(k.s_hold, 1)
                dve.tensor_reduce(k.count_out[:, bass.ds(w, 1)], banks[:, slot * BANKS:(slot + 1) * BANKS, EA],
                                  AX.X, ALU.add).then_inc(s_count, 1)
                if not (isinstance(w, int) and w < 2):
                    dve.wait_ge(k.s_z[slot], (w - slot) * 16)
                dve.tensor_scalar(index[:, slot, 0:1], k.count_in[:, bass.ds(w, 1)], float(DEGMAX), None,
                                  ALU.min).then_inc(s_index, 1)
                dve.wait_ge(s_count, w + 1)
                dve.tensor_scalar(index[:, slot, 1:2], k.count_out[:, bass.ds(w, 1)], float(DEGMAX), None,
                                  ALU.min).then_inc(s_index, 1)
                if not (isinstance(w, int) and w < 2):
                    dve.wait_ge(s_proj, w - 1)
                dve.tensor_scalar(degree[:, slot, :], k.ident[:, :], k.count_out[:, bass.ds(w, 1)], None,
                                  ALU.mult).then_inc(s_diag, 1)

            def line(w, slot, nodes):
                if not (isinstance(w, int) and w < 2):
                    dve.wait_ge(s_part, w * 4 - 4)
                for n in range(2):
                    dve.scalar_tensor_tensor(out=gates[:, slot * 2 + n, :], in0=lines[:, 2 * n, :],
                                             scalar=nodes_in[:, n, bass.ds(w, 1)], in1=lines[:, 2 * n + 1, :],
                                             op0=ALU.mult, op1=ALU.add).then_inc(s_line, 1)

            def add(w, slot, nodes):
                here = terms[:, node_window(w)]
                dve.wait_ge(s_gate, w + 1)
                dve.tensor_tensor(here, gates[:, slot * 2, :], gates[:, slot * 2 + 1, :], ALU.add).then_inc(s_part, 1)
                dve.wait_ge(k.s_z[slot], (w - slot) * 16 + 32)
                dve.wait_ge(s_part, w * 4 + 1)
                for n in range(2):
                    dve.tensor_tensor(here, here, z[:, slot * 2 + n, :], ALU.add).then_inc(s_part, 1)
                    if n == 0:
                        dve.wait_ge(s_part, w * 4 + 2)
                dve.wait_ge(s_proj, w + 1)
                dve.wait_ge(s_part, w * 4 + 3)
                dve.tensor_tensor(here, here, pps[slot][:, 0:D], ALU.add).then_inc(s_part, 1)

            over_windows(dve, (count, 0), (line, 0), (add, 1))


def attend_close(nc, k, a):
    terms = k.side
    with ExitStack() as ctx:
        room = Arena(k.sims)
        wo = room.take([P, 2, D])
        bo = room.take([1, D])
        share = room.take([P, 2, HEADS])
        agg = room.take([P, 2, D])
        agg_t = room.take([P, 2, D])
        part = room.take([P, 2, D])
        stats = room.take([P, 4 * 9])
        tps = [psum(nc, ctx, f"ac_t{i}", [P, 512]) for i in range(2)]
        ops = [psum(nc, ctx, f"ac_o{i}", [P, 512]) for i in range(2)]
        x = k.X.rearrange("p w d -> p (w d)")
        s_w, s_share, s_agg, s_turn, s_turned, s_out, s_part, s_mom, s_root, s_new, s_sent = sems(
            nc, k, *(f"ac_{n}" for n in ("w", "share", "agg", "turn", "turned", "out", "part", "mom", "root", "new",
                                         "sent")))
        block = ctx.enter_context(nc.Block())

        @block.sync
        def _(sp):
            sp.dma_start(wo[:, :, :], a["wo_t"].rearrange("(c p) m -> p c m", p=P)).then_inc(s_w, 16)
            sp.dma_start(bo[:, :], a["L1_gnn_bo"]).then_inc(s_w, 16)

            def send(w, slot, nodes):
                sp.wait_ge(s_new, w + 1)
                sp.dma_start(k.x3_rows[bass.ds(w * P, P), :], x[:, node_window(w)]).then_inc(s_sent, 16)

            over_windows(sp, (send, 3))
            sp.wait_ge(s_sent, 16 * NW)

        @block.tensor
        def _(pe):
            pe.wait_ge(s_w, 32)

            def turn(w, slot, nodes):
                pe.wait_ge(s_agg, w + 1)
                if not (isinstance(w, int) and w < 2):
                    pe.wait_ge(s_turned, w - 1)
                for c in range(2):
                    ins = pe.transpose(tps[slot][:, c * P:(c + 1) * P], agg[:, slot, c * P:(c + 1) * P], k.ident[:, :])
                ins.then_inc(s_turn, 1)

            def project(w, slot, nodes):
                pe.wait_ge(s_turned, w + 1)
                if not (isinstance(w, int) and w < 2):
                    pe.wait_ge(s_part, w * 6 - 11)
                for c in range(2):
                    pe.matmul(ops[slot][:, 0:D], agg_t[:, slot, c * P:(c + 1) * P], wo[:, c, :], start=(c == 0), stop=False)
                pe.matmul(ops[slot][:, 0:D], k.ones[0:1, :], bo[:, :], start=False, stop=True).then_inc(s_out, 1)

            over_windows(pe, (turn, 0), (project, 1))

        @block.scalar
        def _(act):
            def copy_turned(w, slot, nodes):
                act.wait_ge(s_turn, w + 1)
                if not (isinstance(w, int) and w < 2):
                    act.wait_ge(s_out, w - 1)
                act.copy(agg_t[:, slot, :], tps[slot][:, 0:D]).then_inc(s_turned, 1)

            def root(n):
                def stage(w, slot, nodes):
                    act.wait_ge(s_mom, w * 2 + 1 + n)
                    st = stats[:, (slot * 2 + n) * 9:(slot * 2 + n) * 9 + 9]
                    act.activation(st[:, 8:9], st[:, 7:8], ACT.Sqrt, bias=k.eps[:, 0:1]).then_inc(s_root, 1)
                return stage

            over_windows(act, (copy_turned, 0), (root(0), 1), (root(1), 1))

        @block.vector
        def _(dve):
            def divide(w, slot, nodes):
                if not (isinstance(w, int) and w < 2):
                    dve.wait_ge(s_turn, w - 1)
                dve.tensor_scalar(share[:, slot, :], k.acc[:, bass.ds(w * AW + D, HEADS)], 0.5, None,
                                  ALU.max).then_inc(s_share, 1)
                dve.wait_ge(s_share, w * 2 + 1)
                dve.reciprocal(share[:, slot, :], share[:, slot, :]).then_inc(s_share, 1)
                dve.wait_ge(s_share, w * 2 + 2)
                dve.tensor_tensor(agg[:, slot, :].rearrange("p (h d) -> p h d", h=HEADS),
                                  k.acc[:, sum_window(w)].rearrange("p (h d) -> p h d", h=HEADS),
                                  share[:, slot, :].unsqueeze(2).to_broadcast([P, HEADS, HD]), ALU.mult).then_inc(s_agg, 1)

            def norms(w, slot, nodes):
                here = part[:, slot, :]
                st = [stats[:, (slot * 2 + n) * 9:(slot * 2 + n) * 9 + 9] for n in range(2)]
                dve.wait_ge(s_out, w + 1)
                dve.tensor_tensor(here, ops[slot][:, 0:D], x[:, node_window(w)], ALU.add).then_inc(s_part, 1)
                dve.wait_ge(s_part, w * 6 + 1)
                row_moments(dve, k, here, st[0], s_part, w * 6 + 1).then_inc(s_mom, 1)
                dve.wait_ge(s_root, w * 2 + 1)
                dve.reciprocal(st[0][:, 8:9], st[0][:, 8:9]).then_inc(s_part, 1)
                dve.wait_ge(s_part, w * 6 + 3)
                dve.tensor_scalar(here, here, st[0][:, 6:7], st[0][:, 8:9], ALU.subtract, ALU.mult).then_inc(s_part, 1)
                dve.wait_ge(s_part, w * 6 + 4)
                dve.scalar_tensor_tensor(out=here, in0=here, scalar=2.0, in1=terms[:, node_window(w)], op0=ALU.mult,
                                         op1=ALU.add).then_inc(s_part, 1)
                dve.wait_ge(s_part, w * 6 + 5)
                row_moments(dve, k, here, st[1], s_part, w * 6 + 5).then_inc(s_mom, 1)
                dve.wait_ge(s_root, w * 2 + 2)
                dve.reciprocal(st[1][:, 8:9], st[1][:, 8:9]).then_inc(s_inv, 1)
                dve.wait_ge(s_inv, w + 1)
                dve.tensor_scalar(x[:, node_window(w)], here, st[1][:, 6:7], st[1][:, 8:9], ALU.subtract,
                                  ALU.mult).then_inc(s_new, 1)

            (s_inv,) = sems(nc, k, "ac_inv")
            over_windows(dve, (divide, 0), (norms, 1))


def scatter_features(nc, k):
    with ExitStack() as ctx:
        room = Arena(k.sims)
        spread = room.take([P, U, P])
        equal = room.take([P, 4, P], BF16)
        target = room.take([P, 4, P], BF16)
        often = room.take([P, 4, P])
        ready = k.side[:, 0:HALF * D].rearrange("p (v d) -> p v d", v=HALF)
        cur_src = room.take([P, U])
        cur_in = room.take([P, U])
        cur_dst = room.take([P, U])
        cur_row = room.take([P, U], I32)
        wps = [psum(nc, ctx, f"sf_w{i}", [P, 512]) for i in range(4)]
        sums = [psum(nc, ctx, f"sf_s{i}", [P, 512]) for i in range(4)]
        x = k.X.rearrange("p w d -> p (w d)")
        s_cur, s_rowcur, s_tables, s_w, s_often, s_mm, s_ready, s_tick = sems(
            nc, k, *(f"sf_{n}" for n in ("cur", "rowcur", "tables", "w", "often", "mm", "ready", "tick")))
        s_spread = sems(nc, k, *(f"sf_spread{h}" for h in range(2)))
        s_sent, sent0 = k.s_sent, k.sent_before
        k.sent_before += 32 * IT
        block = ctx.enter_context(nc.Block())

        @block.sync
        def _(sp):
            with sp.Fori(0, IT) as it:
                for h in range(2):
                    sp.wait_ge(s_tables, it * 2 * U + (h + 1) * 2 * HALF)
                    sp.dma_start(spread[:, h * HALF:(h + 1) * HALF, :].rearrange("p u e -> p (u e)"),
                                 k.src_row[bass.ds(it * U + h * HALF, HALF), :].rearrange(
                                     "(o u) e -> o (u e)", o=1).to_broadcast([P, HALF * P])).then_inc(s_spread[h], 16)

        @block.vector
        def _(dve):
            def refill(h, at):
                part = slice(h * HALF, (h + 1) * HALF)
                dve.tensor_copy(cur_src[:, part], k.src[:, bass.ds(at, HALF)])
                dve.tensor_copy(cur_dst[:, part], k.dst[:, bass.ds(at, HALF)])
                dve.tensor_copy(cur_in[:, part], k.inside[:, bass.ds(at, HALF)]).then_inc(s_cur, 1)

            for h in range(2):
                refill(h, h * HALF)
            dve.sem_inc(s_tables, 2 * U)
            with dve.Fori(0, IT) as it:
                for h in range(2):
                    part = slice(h * HALF, (h + 1) * HALF)
                    for v in range(HALF):
                        dve.wait_ge(s_sent[v], it * 32 + (sent0 - 16 + 16 * h))
                    dve.sem_inc(k.s_hold, 1)
                    dve.tensor_copy(cur_row[:, part], k.sidx[:, bass.ds(it * U + h * HALF, HALF)]).then_inc(s_rowcur, 1)
                    dve.wait_ge(s_cur, it * 2 + (h + 1))
                    dve.wait_ge(s_spread[h], it * 16 + 16)
                    for u in range(h * HALF, (h + 1) * HALF):
                        dve.wait_ge(s_w, it * U + (u + 1))
                        dve.tensor_scalar(equal[:, u % 4, :], spread[:, u, :], cur_src[:, u:u + 1], cur_in[:, u:u + 1],
                                          ALU.is_equal, ALU.mult).then_inc(s_tables, 1)
                        dve.tensor_scalar(target[:, u % 4, :], k.iota_row[:, :], cur_dst[:, u:u + 1], None,
                                          ALU.is_equal).then_inc(s_tables, 1)
                    dve.wait_ge(s_tables, it * 2 * U + (2 * U + (h + 1) * 2 * HALF))
                    refill(h, it * U + (U + h * HALF))

        @block.tensor
        def _(pe):
            pe.sem_inc(s_w, 4)
            pe.sem_inc(s_mm, 4)

            def weights(it, u):
                pe.wait_ge(s_tables, it * 2 * U + (2 * U + 2 * u + 2))
                pe.wait_ge(s_often, it * U + (u + 1))
                pe.matmul(wps[u % 4][:, 0:P], target[:, u % 4, :], equal[:, u % 4, :], start=True, stop=True).then_inc(s_w, 1)

            def carried(it, u, win):
                pe.wait_ge(s_often, it * U + (4 + u + 1))
                pe.wait_ge(s_ready, it * U + (u + 1))
                pe.matmul(sums[u % 4][:, 0:D], often[:, u % 4, :], x[:, node_window(win)], start=True, stop=True).then_inc(s_mm, 1)

            with pe.Fori(0, IT) as it:
                win = load_steps(nc, pe, k.win, it, NW - 1)
                weights(it, 0)
                weights(it, 1)
                for u in range(U):
                    if u + 2 < U:
                        weights(it, u + 2)
                    carried(it, u, win[u])

        @block.scalar
        def _(act):
            act.sem_inc(s_often, 4)
            act.sem_inc(s_ready, 4)

            def copy_often(it, u):
                act.wait_ge(s_w, it * U + (4 + u + 1))
                act.wait_ge(s_mm, it * U + (u + 1))
                act.copy(often[:, u % 4, :], wps[u % 4][:, 0:P]).then_inc(s_often, 1)

            def copy_sums(it, u):
                act.wait_ge(s_mm, it * U + (4 + u + 1))
                act.wait_ge(s_sent[u % HALF], it * 32 + (sent0 + 16 * (u // HALF)))
                act.copy(ready[:, u % HALF, :], sums[u % 4][:, 0:D]).then_inc(s_ready, 1)

            with act.Fori(0, IT) as it:
                copy_often(it, 0)
                copy_often(it, 1)
                for u in range(U):
                    if u + 2 < U:
                        copy_often(it, u + 2)
                    copy_sums(it, u)

        @block.gpsimd
        def _(pool):
            with pool.Fori(0, IT) as it:
                for u in range(U):
                    if u % HALF == 0:
                        pool.wait_ge(s_rowcur, it * 2 + (u // HALF + 1))
                    pool.wait_ge(s_ready, it * U + (4 + u + 1))
                    pool.wait_ge(s_sent[(u - BANKS) % HALF], it * 32 + (sent0 + 16 * (1 + (u - BANKS) // HALF)))
                    pool.sem_inc(s_tick, 1)
                    pool.indirect_dma_start(k.out_sum[u % BANKS], bass.IndirectOffsetOnAxis(ap=cur_row[:, u:u + 1], axis=0),
                                            ready[:, u % HALF, :], None, compute_op=ALU.add).then_inc(s_sent[u % HALF], 16)
            for v in range(HALF):
                pool.wait_ge(s_sent[v], sent0 + 32 * IT)


def gru_close(nc, k, a):
    H3 = 3 * D
    with ExitStack() as ctx:
        room = Arena(k.side)
        w_ih = room.take([P, 4, H3])
        w_hh = room.take([P, 2, H3])
        w_dir = room.take([P, 4, D])
        b_dir = room.take([P, 2, D])
        b_ih = room.take([1, H3])
        b_hh = room.take([1, H3])
        share = room.take([P, 2, NW])
        met = room.take([P, 2, NW])
        more = Arena(k.sims)
        banks = more.take([P, 2 * BANKS, D])
        mean = more.take([P, 2, D])
        diag = more.take([P, 2, P])
        mean_t = more.take([P, 2 * D])
        x_t = more.take([P, D])
        dir_t = more.take([P, 2 * D])
        gate = more.take([P, 2, 2 * D])
        cand = more.take([P, 2, D])
        part = more.take([P, D])
        done = room.take([P, 2, D])
        stats = room.take([P, 9])
        xs = room.take([P, D])
        aps = psum(nc, ctx, "gr_a", [P, 512])
        xps = psum(nc, ctx, "gr_x", [P, 512])
        dps = psum(nc, ctx, "gr_d", [P, 512])
        gps = [psum(nc, ctx, f"gr_g{i}", [P, 512]) for i in range(2)]
        nps = [psum(nc, ctx, f"gr_n{i}", [P, 512]) for i in range(2)]
        x = k.X.rearrange("p w d -> p (w d)")
        s_w, s_share, s_half, s_mean, s_diag, s_turn, s_at, s_xs, s_xt, s_dir, s_dt, s_gates, s_gate, s_part, s_cand, \
            s_mom, s_root, s_done = sems(nc, k, *(f"gr_{n}" for n in (
                "w", "share", "half", "mean", "diag", "turn", "at", "xs", "xt", "dir", "dt", "gates", "gate", "part",
                "cand", "mom", "root", "done")))
        s_bank = sems(nc, k, "gr_bank0", "gr_bank1")
        s_out = sems(nc, k, "gr_out0", "gr_out1")
        LOADS = 8
        CH = 7
        block = ctx.enter_context(nc.Block())
        early = lambda w, n: isinstance(w, int) and w < n

        @block.sync
        def _(sp):
            sp.dma_start(w_ih[:, :, :], a["w_ih_t"].rearrange("(c p) m -> p c m", p=P)).then_inc(s_w, 16)
            sp.dma_start(w_hh[:, :, :], a["w_hh_t"].rearrange("(c p) m -> p c m", p=P)).then_inc(s_w, 16)
            for n, name in enumerate(("in", "out")):
                sp.dma_start(w_dir[:, 2 * n:2 * n + 2, :], a[f"w_{name}_t"].rearrange("(c p) m -> p c m", p=P)).then_inc(s_w, 16)
                sp.dma_start(b_dir[:, n, :], a[f"L3_gnn_b_{name}"].to_broadcast([P, D])).then_inc(s_w, 16)
            sp.dma_start(b_ih[:, :], a["L3_gnn_b_ih"]).then_inc(s_w, 16)
            sp.dma_start(b_hh[:, :], a["L3_gnn_b_hh"]).then_inc(s_w, 16)

            def load(w, slot, nodes):
                if not early(w, 2):
                    sp.wait_ge(s_half, w * 3 - 3)
                for b in range(BANKS):
                    sp.dma_start(banks[:, slot * BANKS + b, :], k.out_sum[b][bass.ds(w * P, P), :]).then_inc(
                        s_bank[slot], 16)

            def send(w, slot, nodes):
                sp.wait_ge(s_done, w + 1)
                sp.dma_start(a["out"][bass.ds(w * P, nodes), :], done[0:nodes, slot, :]).then_inc(s_out[slot], 16)

            over_windows(sp, (load, 0), (send, 3))
            sp.wait_ge(s_out[0], 16 * (NW + 1) // 2)
            sp.wait_ge(s_out[1], 16 * (NW // 2))

        @block.gpsimd
        def _(pool):
            def add(w, slot, nodes):
                pool.wait_ge(s_bank[slot], (w - slot) * (8 * BANKS) + 16 * BANKS)
                b = [banks[:, slot * BANKS + n, :] for n in range(BANKS)]
                pool.tensor_tensor(b[0], b[0], b[1], ALU.add).then_inc(s_half, 1)
                pool.tensor_tensor(b[2], b[2], b[3], ALU.add).then_inc(s_half, 1)
                pool.wait_ge(s_half, w * 3 + 2)
                if not early(w, 1):
                    pool.wait_ge(s_turn, w)
                pool.tensor_tensor(mean[:, 1, :], b[0], b[2], ALU.add).then_inc(s_half, 1)

            over_windows(pool, (add, 0))

        @block.tensor
        def _(pe):
            pe.wait_ge(s_w, 16 * LOADS)

            def turn(w, slot, nodes):
                pe.wait_ge(s_mean, w * 2 + 2)
                pe.wait_ge(s_xs, w + 1)
                if not early(w, 1):
                    pe.wait_ge(s_at, w)
                    pe.wait_ge(s_xt, w)
                for n in range(4):
                    ins = pe.transpose(aps[:, n * P:(n + 1) * P], mean[:, n // 2, (n % 2) * P:(n % 2 + 1) * P],
                                       k.ident[:, :])
                for c in range(2):
                    ins = pe.transpose(xps[:, c * P:(c + 1) * P], xs[:, c * P:(c + 1) * P], k.ident[:, :])
                ins.then_inc(s_turn, 1)

            def direct(w, slot, nodes):
                pe.wait_ge(s_at, w + 1)
                pe.wait_ge(s_diag, w * 2 + 2)
                if not early(w, 1):
                    pe.wait_ge(s_dt, w)
                for n in range(4):
                    out = dps[:, n * P:(n + 1) * P]
                    way, m = n // 2, slice((n % 2) * P, (n % 2 + 1) * P)
                    for c in range(2):
                        pe.matmul(out, w_dir[:, way * 2 + c, m], mean_t[:, (way * 2 + c) * P:(way * 2 + c + 1) * P],
                                  start=(c == 0), stop=False)
                    ins = pe.matmul(out, b_dir[:, way, m], diag[:, way, :], start=False, stop=True)
                ins.then_inc(s_dir, 1)

            def cell(w, slot, nodes):
                if not early(w, 2):
                    pe.wait_ge(s_gate, w - 1)
                    pe.wait_ge(s_cand, w - 1)
                pe.wait_ge(s_xt, w + 1)
                half = slice(0, 2 * D)
                last = slice(2 * D, 3 * D)
                states = [(x_t[:, c * P:(c + 1) * P], w_hh[:, c, :]) for c in range(2)] + [(k.ones[0:1, :], b_hh[:, :])]
                inputs = [(dir_t[:, c * P:(c + 1) * P], w_ih[:, c, :]) for c in range(4)] + [(k.ones[0:1, :], b_ih[:, :])]
                for n, (left, right) in enumerate(states):
                    pe.matmul(gps[slot][:, :], left, right[:, half], start=(n == 0), stop=False)
                for n, (left, right) in enumerate(states):
                    pe.matmul(nps[slot][:, D:2 * D], left, right[:, last], start=(n == 0), stop=(n == 2))
                pe.wait_ge(s_dt, w + 1)
                for n, (left, right) in enumerate(inputs):
                    pe.matmul(gps[slot][:, :], left, right[:, half], start=False, stop=(n == 4))
                for n, (left, right) in enumerate(inputs):
                    ins = pe.matmul(nps[slot][:, 0:D], left, right[:, last], start=(n == 0), stop=(n == 4))
                ins.then_inc(s_gates, 1)

            over_windows(pe, (turn, 0), (direct, 0), (cell, 0))

        @block.scalar
        def _(act):
            def copies(w, slot, nodes):
                act.wait_ge(s_turn, w + 1)
                if not early(w, 1):
                    act.wait_ge(s_gates, w)
                act.copy(mean_t[:, :], aps[:, :]).then_inc(s_at, 1)
                act.copy(x_t[:, :], xps[:, 0:D]).then_inc(s_xt, 1)
                act.wait_ge(s_dir, w + 1)
                act.copy(dir_t[:, :], dps[:, :]).then_inc(s_dt, 1)

            def gates(w, slot, nodes):
                act.wait_ge(s_gates, w + 1)
                if not early(w, 2):
                    act.wait_ge(s_part, w * CH - (CH + 3))
                act.activation(gate[:, slot, :], gps[slot][:, :], ACT.Sigmoid).then_inc(s_gate, 1)

            def candidate(w, slot, nodes):
                act.wait_ge(s_part, w * CH + 2)
                act.activation(cand[:, slot, :], cand[:, slot, :], ACT.Tanh).then_inc(s_root, 1)

            def root(w, slot, nodes):
                act.wait_ge(s_mom, w + 1)
                act.activation(stats[:, 8:9], stats[:, 7:8], ACT.Sqrt, bias=k.eps[:, 0:1]).then_inc(s_root, 1)

            over_windows(act, (copies, 0), (gates, 0), (candidate, 0), (root, 0))

        @block.vector
        def _(dve):
            for n, count in enumerate((k.count_in, k.count_out)):
                dve.tensor_scalar(met[:, n, :], count[:, :], 1.0, None, ALU.min).then_inc(s_share, 1)
                dve.tensor_scalar(share[:, n, :], count[:, :], 1.0, None, ALU.max).then_inc(s_share, 1)
            dve.wait_ge(s_share, 4)
            dve.reciprocal(share[:, :, :], share[:, :, :]).then_inc(s_share, 1)
            dve.wait_ge(s_share, 5)

            def means(w, slot, nodes):
                if not early(w, 1):
                    dve.wait_ge(s_turn, w)
                    dve.wait_ge(s_dir, w)
                dve.tensor_scalar(mean[:, 0, :], k.acc[:, sum_window(w)], share[:, 0, bass.ds(w, 1)], None,
                                  ALU.mult).then_inc(s_mean, 1)
                dve.tensor_scalar(xs[:, :], x[:, node_window(w)], 1.0, None, ALU.mult).then_inc(s_xs, 1)
                for n in range(2):
                    dve.tensor_scalar(diag[:, n, :], k.ident[:, :], met[:, n, bass.ds(w, 1)], None,
                                      ALU.mult).then_inc(s_diag, 1)
                dve.wait_ge(s_half, w * 3 + 3)
                dve.tensor_scalar(mean[:, 1, :], mean[:, 1, :], share[:, 1, bass.ds(w, 1)], None,
                                  ALU.mult).then_inc(s_mean, 1)

            def close(w, slot, nodes):
                reset, keep = gate[:, slot, 0:D], gate[:, slot, D:2 * D]
                here = cand[:, slot, :]
                state = x[:, node_window(w)]
                dve.wait_ge(s_gate, w + 1)
                dve.tensor_tensor(here, reset, nps[slot][:, D:2 * D], ALU.mult).then_inc(s_part, 1)
                dve.wait_ge(s_part, w * CH + 1)
                dve.tensor_tensor(here, here, nps[slot][:, 0:D], ALU.add).then_inc(s_part, 1)
                dve.sem_inc(s_cand, 1)
                dve.wait_ge(s_root, w * 2 + 1)
                dve.tensor_tensor(here, here, state, ALU.subtract).then_inc(s_part, 1)
                dve.wait_ge(s_part, w * CH + 3)
                dve.tensor_tensor(here, here, keep, ALU.mult).then_inc(s_part, 1)
                dve.wait_ge(s_part, w * CH + 4)
                dve.scalar_tensor_tensor(out=part[:, :], in0=state, scalar=2.0, in1=here, op0=ALU.mult,
                                         op1=ALU.add).then_inc(s_part, 1)
                dve.wait_ge(s_part, w * CH + 5)
                row_moments(dve, k, part[:, :], stats, s_part, w * CH + 5).then_inc(s_mom, 1)
                dve.wait_ge(s_root, w * 2 + 2)
                dve.reciprocal(stats[:, 8:9], stats[:, 8:9]).then_inc(s_part, 1)
                dve.wait_ge(s_part, w * CH + 7)
                if not early(w, 2):
                    dve.wait_ge(s_out[slot], (w - slot) * 8)
                dve.tensor_scalar(done[:, slot, :], part[:, :], stats[:, 6:7], stats[:, 8:9], ALU.subtract,
                                  ALU.mult).then_inc(s_done, 1)
                dve.wait_ge(s_done, w + 1)

            over_windows(dve, (means, 0), (close, 1))


def build(nc, k, a):
    with ExitStack() as ctx:
        k.ctx = ctx
        k.rows_before = 0
        k.sent_before = 16 * (1 + 2 * IT)
        dram = lambda name, shape, dt=F32: nc.dram_tensor(name, shape, dt)
        k.dst_row = dram("dst_row", [ROWS, P]).ap()
        k.src_row = dram("src_row", [ROWS, P]).ap()
        k.key_row = dram("key_row", [P + ROWS * P]).ap()
        k.kv_rows = dram("kv_rows", [NPAD, 2 * D]).ap()
        k.x3_rows = dram("x3_rows", [NPAD, D]).ap()
        k.v_edge = dram("v_edge", [STEPS * P, D]).ap()
        k.attr_sum = [dram(f"attr_sum{b}", [SUMROWS, EW]).ap() for b in range(BANKS)]
        k.out_sum = [dram(f"out_sum{b}", [SUMROWS, D]).ap() for b in range(BANKS)]
        k.xs = sbuf(nc, ctx, "xs", [P, NW, D])
        k.X = k.xs[:, :, :]
        k.big = sbuf(nc, ctx, "big", [P, NW * AW + NW * D])
        k.acc = k.big[:, 0:NW * AW]
        k.side = k.big[:, NW * AW:NW * AW + NW * D]
        k.sims = sbuf(nc, ctx, "sims", [P, STEPS * HEADS])[:, :]
        k.dst = sbuf(nc, ctx, "dst_tab", [P, ROWS])
        k.src = sbuf(nc, ctx, "src_tab", [P, ROWS])
        k.inside = sbuf(nc, ctx, "inside_tab", [P, ROWS])
        k.count_in = sbuf(nc, ctx, "count_in", [P, NW])
        k.count_out = sbuf(nc, ctx, "count_out", [P, NW])
        k.norm2 = k.sims[:, 0:2 * D]
        k.idx = sbuf(nc, ctx, "idx_tab", [P, ROWS], I32)
        k.sidx = sbuf(nc, ctx, "sidx_tab", [P, ROWS], I32)
        k.win = sbuf(nc, ctx, "win_row", [1, ROWS], I32)
        k.chunk = sbuf(nc, ctx, "chunk_row", [1, ROWS], I32)
        k.ident = sbuf(nc, ctx, "ident", [P, P])
        k.ones = sbuf(nc, ctx, "ones", [P, P])
        k.below = sbuf(nc, ctx, "below", [P, P])
        k.iota_row = sbuf(nc, ctx, "iota_row", [P, P])
        k.iota_col = sbuf(nc, ctx, "iota_col", [P, 1])
        k.eps = sbuf(nc, ctx, "eps", [P, 1])
        k.trash = sbuf(nc, ctx, "trash", [P, 1])
        k.stage_sems = []
        k.s_hold = nc.alloc_semaphore("s_hold")
        k.s_row = [nc.alloc_semaphore(f"s_row{u}") for u in range(U)]
        k.s_z = [nc.alloc_semaphore(f"s_z{i}") for i in range(2)]
        k.s_sent = [nc.alloc_semaphore(f"s_sent{v}") for v in range(HALF)]
        step_tables(nc, k, a["dst"], a["src"], a["x"])
        end_stage(nc, k)
        gather_sums(nc, k, "l0", a["x"], True)
        end_stage(nc, k)
        scatter_attributes(nc, k, a["attr"])
        end_stage(nc, k)
        gin_mlp(nc, k, a)
        end_stage(nc, k)
        gin_close_and_project(nc, k, a)
        end_stage(nc, k)
        edge_scores(nc, k)
        end_stage(nc, k)
        softmax_weights(nc, k)
        end_stage(nc, k)
        weighted_sums(nc, k)
        end_stage(nc, k)
        node_terms(nc, k, a)
        end_stage(nc, k)
        attend_close(nc, k, a)
        end_stage(nc, k)
        scatter_features(nc, k)
        end_stage(nc, k)
        gather_sums(nc, k, "l3", k.x3_rows, False)
        end_stage(nc, k)
        gru_close(nc, k, a)
        end_stage(nc, k)




def padded(rows, shape, fill):
    out = np.full(shape, fill, rows.dtype)
    out.reshape((-1,) + rows.shape[1:])[:rows.shape[0]] = rows
    return out


def kernel(**inputs):
    import concourse.bacc as bacc
    from concourse.bass_utils import run_bass_kernel_spmd

    host = {n: np.ascontiguousarray(v) for n, v in inputs.items()}
    lay = {
        "x": padded(host["x"], (NPAD, D), 0),
        "dst": padded(host["dst"], (NC, P), PAD_DST),
        "src": padded(host["src"], (NC, P), 0),
        "attr": padded(host["edge_attr_128"], (NC * P, EA), 0),
    }
    for name in ("L0_gnn_W1", "L0_gnn_W2"):
        lay[name] = host[name]
    for name in ("b1", "g1", "bt1", "b2", "g2", "bt2", "eps_gin"):
        lay[f"L0_gnn_{name}"] = host[f"L0_gnn_{name}"].reshape(1, -1)
    for name in "qkvo":
        lay[f"w{name}_t"] = np.ascontiguousarray(host[f"L1_gnn_W{name}"].T)
        lay[f"L1_gnn_b{name}"] = host[f"L1_gnn_b{name}"].reshape(1, -1)
    for name in ("z_in", "z_out", "W_cent", "W_vor", "W_sum"):
        lay[f"L2_gnn_{name}"] = host[f"L2_gnn_{name}"]
    for name in ("L2_gnn_b_cent", "L2_gnn_b_vor", "L2_gnn_b_sum", "L3_gnn_b_in", "L3_gnn_b_out", "L3_gnn_b_ih", "L3_gnn_b_hh"):
        lay[name] = host[name].reshape(1, -1)
    for name in ("in", "out", "ih", "hh"):
        lay[f"w_{name}_t"] = np.ascontiguousarray(host[f"L3_gnn_W_{name}"].T)
    for name in ("node_vec1", "node_vec1_n2"):
        lay[name] = np.ascontiguousarray(padded(host[name], (NPAD, 1), 0).reshape(NW, P).T)
    nc = bacc.Bacc("TRN2", target_bir_lowering=False, num_devices=1)
    arrays, handles = {}, {}
    for name, array in lay.items():
        arrays[f"in_{name}"] = array
        handles[name] = nc.dram_tensor(f"in_{name}", array.shape, mybir.dt.from_np(array.dtype), kind="ExternalInput").ap()
    handles["out"] = nc.dram_tensor("out", (N, D), F32, kind="ExternalOutput").ap()
    build(nc, Kit(), handles)
    return run_bass_kernel_spmd(nc, [arrays], core_ids=[0]).results[0]["out"]
```

```python
import numpy as np
import concourse.bass as bass
from concourse import mybir
from contextlib import ExitStack

F32 = mybir.dt.float32
BF16 = mybir.dt.bfloat16
I32 = mybir.dt.int32
ALU = mybir.AluOpType
ACT = mybir.ActivationFunctionType
AX = mybir.AxisListType

P = 128
N, D, E, EA = 6250, 256, 106250, 128
HID = 2 * D
HEADS, HD = 8, 32
SCALE = 1.0 / float(np.sqrt(HD))
EPS = 1e-5
NW = -(-N // P)
NPAD = NW * P
TAIL = N - (NW - 1) * P
NC = -(-E // P) + 1
U = 16
IT = -(-(NC - 1 + NW - 1) // U)
STEPS = IT * U
ROWS = -(-STEPS // P) * P
RT = ROWS // P
HALF = U // 2
QUAD = 4
AW = D + HEADS
GROUPS = P // HEADS
GS = STEPS // GROUPS
SCAN = GS * P
PAD_DST = 1 << 20
BIG = 1e30
LOW = -1e37
KEY = 2.0 ** 110
BANKS = 4
SUMROWS = NPAD + P
EW = EA + 1
DEGMAX = 511

assert (NW - 1 - 4) % 4 == 0
assert STEPS % GROUPS == 0 and STEPS >= NC - 1 + NW - 1 + 0


class Kit:
    pass


def sbuf(nc, ctx, name, shape, dt=F32):
    return ctx.enter_context(nc.sbuf_tensor(name, shape, dt))


class Arena:

    def __init__(self, region):
        self.region, self.at = region, 0

    def take(self, shape, dt=F32):
        words = int(np.prod(shape[1:])) * (2 if dt == BF16 else 4)
        words = -(-words // 4)
        part = self.region[0:shape[0], self.at:self.at + words]
        self.at += words
        assert self.at <= self.region.shape[1], (self.at, self.region.shape)
        if dt != F32:
            part = part.bitcast(dt)
        if len(shape) == 3:
            part = part.rearrange("p (a b) -> p a b", a=shape[1])
        return part


def psum(nc, ctx, name, shape, dt=F32):
    return ctx.enter_context(nc.psum_tensor(name, shape, dt))


def sems(nc, k, *names):
    new = [nc.alloc_semaphore(n) for n in names]
    k.stage_sems += new
    return new


def end_stage(nc, k):
    nc.clear_and_free_semaphores(k.stage_sems)
    k.stage_sems = []
    nc.all_engine_barrier()


def load_steps(nc, engine, row, it, top):
    return nc.values_load_multi_w_load_instructions(
        row[0:1, bass.ds(it * U, U)], engines=[engine.engine], min_val=0, max_val=top,
        skip_runtime_bounds_check_because="step_tables clamps the entries")[1]


def compare(dve, k, out, rows, columns):
    if rows is None:
        rows = k.iota_row[:, :].unsqueeze(1).to_broadcast([P, QUAD, P])
    return dve.tensor_tensor(out, rows, columns.unsqueeze(2).to_broadcast([P, QUAD, P]), ALU.is_equal)


def widen(pe, k, wide, columns):
    for j in range(QUAD):
        ins = pe.transpose(wide[:, j * P:(j + 1) * P], columns[:, j:j + 1].to_broadcast([P, P]), k.ident[:, :])
    return ins


def step_tables(nc, k, dst_rows, src_rows, x_rows):
    with ExitStack() as ctx:
        room = Arena(k.big[:, :])
        last_i = room.take([1, NC], I32)
        last_f = room.take([1, NC])
        limit = room.take([NW - 1, 1])
        wnum = room.take([NW - 1, 1])
        ahead = room.take([NW - 1, NC])
        count = room.take([NW - 1, 1])
        ends = room.take([NW - 1, 1])
        step_no = room.take([NW - 1, ROWS])
        ended = room.take([NW - 1, ROWS])
        step_col = room.take([P, RT])
        win_col = room.take([P, RT])
        base_col = room.take([P, RT])
        chunk_f = room.take([P, RT])
        chunk_i = room.take([P, RT], I32)
        crow_f = room.take([1, ROWS])
        dst_i = room.take([P, RT, P], I32)
        src_i = room.take([P, RT, P], I32)
        dst_f = room.take([P, RT, P])
        src_f = room.take([P, RT, P])
        key_f = room.take([P, RT, P])
        flag = room.take([P, ROWS])
        low_key = room.take([1, 1])
        last_ps = psum(nc, ctx, "last_ps", [NW - 1, 2, 512])
        wrow_ps = psum(nc, ctx, "wrow_ps", [1, 2, 512])
        wcol_ps = psum(nc, ctx, "wcol_ps", [P, RT])
        turn_ps = [psum(nc, ctx, f"turn_ps{i}", [P, P]) for i in range(2)]
        (s_last, s_x, s_const, s_ident, s_lastf, s_lastb, s_count, s_ended, s_wps, s_chunk, s_gat, s_rel, s_rows,
         s_turn, s_tab, s_dve) = sems(
            nc, k, "t_last", "t_x", "t_const", "t_ident", "t_lastf", "t_lastb", "t_count", "t_ended", "t_wps",
            "t_chunk", "t_gat", "t_rel", "t_rows", "t_turn", "t_tab", "t_dve")
        HB, HR = NC // 2, ROWS // 2
        block = ctx.enter_context(nc.Block())

        @block.sync
        def _(sp):
            sp.dma_start(last_i[:, :], dst_rows[:, P - 1:P].rearrange("c o -> o c"),
                         allow_slow_non_contiguous=True).then_inc(s_last, 16)
            sp.dma_start(k.X, x_rows.rearrange("(w p) d -> p w d", p=P)).then_inc(s_x, 16)
            sp.wait_ge(s_rel, 3 * RT)
            sp.dma_start(k.key_row[P:].rearrange("(t p e) -> p t e", p=P, e=P), key_f[:, :, :]).then_inc(s_rows, 16)
            sp.dma_start(k.key_row[P - 1:P].rearrange("(a b) -> a b", a=1), low_key[:, :]).then_inc(s_rows, 16)
            sp.wait_ge(s_rows, 32)
            sp.wait_ge(s_x, 16)

        @block.gpsimd
        def _(pool):
            iota = lambda out, pattern, base, mult: pool.iota(
                out, pattern, base=base, channel_multiplier=mult, allow_small_or_imprecise_dtypes=True)
            pool.memset(k.ident[:, :], 0.0).then_inc(s_ident, 1)
            pool.memset(k.ones[:, :], 1.0).then_inc(s_const, 1)
            pool.memset(k.eps[:, :], EPS)
            pool.memset(low_key[:, :], -5.0 * KEY).then_inc(s_const, 1)
            iota(limit[:, :], [[0, 1]], P, P).then_inc(s_const, 1)
            iota(wnum[:, :], [[0, 1]], 0, 1).then_inc(s_const, 1)
            iota(step_no[:, :], [[1, ROWS]], 0, 0).then_inc(s_const, 1)
            iota(step_col[:, :], [[P, RT]], 0, 1).then_inc(s_const, 1)
            iota(k.iota_row[:, :], [[1, P]], 0, 0).then_inc(s_const, 1)
            iota(k.iota_col[:, :], [[0, 1]], 0, 1).then_inc(s_const, 1)
            iota(k.trash[:, :], [[0, 1]], NPAD, 1).then_inc(s_const, 1)
            pool.wait_ge(s_ident, 1)
            pool.affine_select(out=k.ident[:, :], in_=k.ident[:, :], compare_op=ALU.not_equal, fill=1.0, base=0,
                               pattern=[[-1, P]], channel_multiplier=1).then_inc(s_ident, 1)
            pool.wait_ge(s_const, 1)
            pool.affine_select(out=k.below[:, :], in_=k.ones[:, :], compare_op=ALU.is_gt, fill=0.0, base=0,
                               pattern=[[-1, P]], channel_multiplier=1).then_inc(s_const, 1)
            pool.wait_ge(s_chunk, 1)
            for t in range(RT):
                for table, rows in ((dst_i, dst_rows), (src_i, src_rows)):
                    pool.indirect_dma_start(table[:, t, :], None, rows,
                                            bass.IndirectOffsetOnAxis(ap=chunk_i[:, t:t + 1], axis=0)).then_inc(s_gat, 16)
            pool.wait_ge(s_gat, 32 * RT)

        @block.tensor
        def _(pe):
            pe.wait_ge(s_const, 10)
            pe.wait_ge(s_lastf, 1)
            for h in range(2):
                pe.matmul(last_ps[:, h, 0:HB], k.ones[0:1, 0:NW - 1], last_f[:, h * HB:(h + 1) * HB],
                          start=True, stop=True).then_inc(s_lastb, 1)
            pe.wait_ge(s_ended, 1)
            for h in range(2):
                pe.matmul(wrow_ps[:, h, 0:HR], k.ones[0:NW - 1, 0:1], ended[:, h * HR:(h + 1) * HR],
                          start=True, stop=True).then_inc(s_wps, 1)
            for t in range(RT):
                pe.matmul(wcol_ps[:, t:t + 1], ended[:, t * P:(t + 1) * P], k.ones[0:NW - 1, 0:1],
                          start=True, stop=True).then_inc(s_wps, 1)
            pe.wait_ge(s_ident, 2)
            for t in range(RT):
                for n, rows in enumerate((dst_f, src_f)):
                    pe.wait_ge(s_rel, 3 * t + 1 + n)
                    if t:
                        pe.wait_ge(s_tab, 2 * t - 1 + n)
                    pe.transpose(turn_ps[n][:, :], rows[:, t, :], k.ident[:, :]).then_inc(s_turn, 1)

        @block.vector
        def _(dve):
            dve.wait_ge(s_last, 16)
            dve.tensor_copy(last_f[:, :], last_i[:, :]).then_inc(s_lastf, 1)
            dve.wait_ge(s_lastb, 2)
            dve.wait_ge(s_const, 10)
            dve.tensor_scalar(ahead[:, :].rearrange("w (h c) -> w h c", h=2), last_ps[:, :, 0:HB], limit[:, 0:1], None,
                              ALU.is_lt).then_inc(s_dve, 1)
            dve.wait_ge(s_dve, 1)
            dve.tensor_reduce(count[:, :], ahead[:, :], AX.X, ALU.add).then_inc(s_dve, 1)
            dve.wait_ge(s_dve, 2)
            dve.tensor_tensor(ends[:, :], count[:, :], wnum[:, :], ALU.add).then_inc(s_dve, 1)
            dve.wait_ge(s_dve, 3)
            dve.tensor_scalar(ended[:, :], step_no[:, :], ends[:, 0:1], None, ALU.is_gt).then_inc(s_ended, 1)
            dve.wait_ge(s_wps, 2 + RT)
            dve.tensor_copy(win_col[:, :], wcol_ps[:, :]).then_inc(s_dve, 1)
            dve.tensor_copy(k.win[:, :].rearrange("o (h c) -> o h c", h=2), wrow_ps[:, :, 0:HR]).then_inc(s_dve, 1)
            dve.tensor_tensor(crow_f[:, :].rearrange("o (h c) -> o h c", h=2),
                              step_no[0:1, :].rearrange("o (h c) -> o h c", h=2), wrow_ps[:, :, 0:HR],
                              ALU.subtract).then_inc(s_dve, 1)
            dve.wait_ge(s_dve, 4)
            dve.tensor_scalar(base_col[:, :], win_col[:, :], float(P), None, ALU.mult).then_inc(s_dve, 1)
            dve.tensor_tensor(chunk_f[:, :], step_col[:, :], win_col[:, :], ALU.subtract).then_inc(s_dve, 1)
            dve.wait_ge(s_dve, 8)
            dve.tensor_scalar(chunk_i[:, :], chunk_f[:, :], float(NC - 1), None, ALU.min).then_inc(s_chunk, 1)
            dve.tensor_scalar(k.chunk[:, :], crow_f[:, :], float(NC - 1), None, ALU.min).then_inc(s_dve, 1)
            dve.wait_ge(s_dve, 9)
            by_quad = k.chunk[:, :].rearrange("o (h u) -> o h u", u=QUAD)
            dve.tensor_tensor(k.beyond[:, :].rearrange("o (h u) -> o h u", u=QUAD), by_quad,
                              by_quad[:, :, 0:1].to_broadcast([1, ROWS // QUAD, QUAD]), ALU.subtract)
            dve.wait_ge(s_gat, 32 * RT)
            for t in range(RT):
                dve.tensor_scalar(dst_f[:, t, :], dst_i[:, t, :], base_col[:, t:t + 1], None,
                                  ALU.subtract).then_inc(s_rel, 1)
                dve.tensor_copy(src_f[:, t, :], src_i[:, t, :]).then_inc(s_rel, 1)
                dve.wait_ge(s_rel, 3 * t + 1)
                dve.tensor_scalar(key_f[:, t, :], dst_f[:, t, :], -0.5, P - 0.5, ALU.max, ALU.min).then_inc(s_dve, 1)
                dve.wait_ge(s_dve, 10 + t)
                dve.tensor_scalar(key_f[:, t, :], key_f[:, t, :], base_col[:, t:t + 1], KEY,
                                  ALU.add, ALU.mult).then_inc(s_rel, 1)
            for t in range(RT):
                dve.wait_ge(s_turn, 2 * t + 1)
                dve.tensor_copy(k.dst[:, t * P:(t + 1) * P], turn_ps[0][:, :]).then_inc(s_tab, 1)
                dve.wait_ge(s_turn, 2 * t + 2)
                dve.tensor_copy(k.src[:, t * P:(t + 1) * P], turn_ps[1][:, :]).then_inc(s_tab, 1)
            dve.wait_ge(s_tab, 2 * RT)
            dve.tensor_scalar(flag, k.dst[:, :], 0.0, None, ALU.is_ge).then_inc(s_dve, 1)
            dve.wait_ge(s_dve, 10 + RT)
            dve.scalar_tensor_tensor(out=flag, in0=k.dst[:, :], scalar=float(P), in1=flag,
                                     op0=ALU.is_lt, op1=ALU.mult).then_inc(s_dve, 1)
            dve.tensor_copy(k.idx[:, :], k.src[:, :]).then_inc(s_dve, 1)
            dve.wait_ge(s_dve, 12 + RT)
            dve.scalar_tensor_tensor(out=k.own[:, :], in0=k.src[:, :], scalar=1.0, in1=flag, op0=ALU.add,
                                     op1=ALU.mult).then_inc(s_dve, 1)
            dve.wait_ge(s_dve, 13 + RT)
            dve.tensor_scalar(k.own[:, :], k.own[:, :], -1.0, None, ALU.add).then_inc(s_dve, 1)


def gather_sums(nc, k, tag, table, first, beside=None):
    def turns(engine, one, work=None):
        if beside is None:
            with engine.Fori(0, IT) as it:
                one(it, lambda u: None)
        else:
            with engine.Fori(0, NW) as it:
                one(it, lambda u: work(it, u))
            with engine.Fori(NW, IT) as it:
                one(it, lambda u: None)

    width = D + 1 if first else D
    with ExitStack() as ctx:
        room = Arena(k.side)
        ring = room.take([P, U, D + 1])
        onehot = room.take([P, HALF, P])
        cur_idx = room.take([P, U], I32)
        cur_dst = room.take([P, U])
        cur_src = room.take([P, U])
        same = room.take([P, P], BF16)
        before = room.take([P, U])
        away = room.take([P, U])
        sums = [psum(nc, ctx, f"{tag}_sums{i}", [P, 512]) for i in range(4)]
        s_zero, s_cur, s_tick, s_hot, s_sum, s_acc, s_seen, s_idx = sems(
            nc, k, *(f"{tag}_{n}" for n in ("zero", "cur", "tick", "hot", "sum", "acc", "seen", "idx")))
        wide = [psum(nc, ctx, f"{tag}_wide{i}", [P, 512]) for i in range(2)] if first else None
        (s_wide,) = sems(nc, k, f"{tag}_wide")
        s_row, row0 = k.s_row, k.rows_before
        k.rows_before += 16 * IT
        work = beside(nc, k, ctx, room) if beside else Kit()
        block = ctx.enter_context(nc.Block())

        @block.gpsimd
        def _(pool):
            with pool.Fori(0, IT) as it:
                for u in range(U):
                    if u % HALF == 0:
                        pool.wait_ge(s_cur, it * 2 + (1 + u // HALF))
                    pool.wait_ge(s_sum, it * U + (u + 1))
                    pool.sem_inc(s_tick, 1)
                    pool.indirect_dma_start(ring[:, u, 0:D], None, table, bass.IndirectOffsetOnAxis(
                        ap=cur_idx[:, u:u + 1], axis=0)).then_inc(s_row[u], 16)

        if beside:
            @block.sync
            def _(sp):
                work.sync(sp)

            @block.scalar
            def _(act):
                work.scalar(act)

        @block.tensor
        def _(pe):
            def sources(it, u):
                if u % HALF == 0:
                    pe.wait_ge(s_cur, it * 2 + (1 + u // HALF))
                pe.wait_ge(s_seen, it * U + (u + U - QUAD))
                widen(pe, k, wide[u // QUAD % 2], cur_src[:, u % U:u % U + QUAD]).then_inc(s_wide, QUAD)

            def one(it, beside_step):
                for u in range(U):
                    if first and u % QUAD == 0:
                        sources(it, u + QUAD)
                    pe.wait_ge(s_row[u], it * 16 + (row0 + 16))
                    pe.wait_ge(s_hot, it * U + (u + 1))
                    pe.wait_ge(s_acc, it * U + (u + 1))
                    pe.matmul(sums[u % 4][:, 0:width], onehot[:, u % HALF, :], ring[:, u, 0:width],
                              start=True, stop=True).then_inc(s_sum, 1)
                    beside_step(u)

            pe.sem_inc(s_sum, U)
            if first:
                sources(0, 0)
            turns(pe, one, work.tensor(pe) if beside else None)

        @block.vector
        def _(dve):
            def refill(h, at):
                part = slice(h * HALF, (h + 1) * HALF)
                dve.tensor_copy(cur_dst[:, part], k.dst[:, bass.ds(at, HALF)])
                if first:
                    dve.tensor_copy(cur_src[:, part], k.src[:, bass.ds(at, HALF)])
                dve.tensor_copy(cur_idx[:, part], k.idx[:, bass.ds(at, HALF)]).then_inc(s_cur, 1)

            def hot(it, u):
                if u % HALF == 0:
                    dve.wait_ge(s_cur, it * 2 + (1 + u // HALF))
                dve.wait_ge(s_sum, it * U + (u + QUAD + U - HALF))
                compare(dve, k, onehot[:, u % HALF:u % HALF + QUAD, :], None,
                        cur_dst[:, u % U:u % U + QUAD]).then_inc(s_hot, QUAD)

            def add(it, u, win):
                dve.wait_ge(s_sum, it * U + (u + 1 + U))
                dve.wait_ge(s_acc, it * U + (u + 4))
                here = k.acc[:, bass.ds(win * AW, width)]
                dve.tensor_tensor(here, sums[u % 4][:, 0:width], here, ALU.add).then_inc(s_acc, 1)

            def earlier(it, u):
                if u % QUAD == 0:
                    dve.wait_ge(s_wide, it * U + (u + QUAD))
                dve.wait_ge(s_seen, it * U + (U + u))
                row = wide[u // QUAD % 2][:, u % QUAD * P:(u % QUAD + 1) * P]
                dve.scalar_tensor_tensor(out=same[:, :], in0=row, scalar=cur_src[:, u:u + 1],
                                         in1=k.below[:, :], op0=ALU.is_equal, op1=ALU.mult,
                                         accum_out=before[:, u:u + 1]).then_inc(s_seen, 1)

            def scatter_rows(it, h):
                part = slice(h * HALF, (h + 1) * HALF)
                dve.wait_ge(s_seen, it * U + (U + (h + 1) * HALF))
                dve.tensor_scalar(before[:, part], before[:, part], 0.0, None, ALU.is_gt).then_inc(s_idx, 1)
                dve.tensor_scalar(away[:, part], cur_src[:, part], -1.0, k.trash[:, 0:1], ALU.mult,
                                  ALU.add).then_inc(s_idx, 1)
                dve.wait_ge(s_idx, it * 8 + (4 * h + 2))
                dve.tensor_tensor(away[:, part], away[:, part], before[:, part], ALU.mult).then_inc(s_idx, 1)
                dve.wait_ge(s_idx, it * 8 + (4 * h + 3))
                dve.tensor_tensor(k.sidx[:, bass.ds(it * U + h * HALF, HALF)], away[:, part], cur_src[:, part],
                                  ALU.add).then_inc(s_idx, 1)
                dve.wait_ge(s_idx, it * 8 + (4 * h + 4))

            dve.memset(k.acc[:, :], 0.0)
            if first:
                dve.memset(ring[:, :, D:D + 1], 1.0).then_inc(s_zero, 1)
                dve.wait_ge(s_zero, 1)
                dve.sem_inc(s_seen, U)
            def one(it, beside_step):
                win = load_steps(nc, dve, k.win, it, NW - 1)
                for h in range(2):
                    for u in range(h * HALF, (h + 1) * HALF):
                        if u % QUAD == 0:
                            hot(it, u + QUAD)
                        if first:
                            earlier(it, u)
                        add(it, u, win[u])
                        beside_step(u)
                    if first:
                        scatter_rows(it, h)
                    refill(h, it * U + (U + h * HALF))

            for h in range(2):
                refill(h, h * HALF)
            dve.sem_inc(s_acc, 4)
            hot(0, 0)
            turns(dve, one, work.vector(dve) if beside else None)


def node_window(w):
    return bass.ds(w * D, D)


def sum_window(w, width=D):
    return bass.ds(w * AW, width)


def over_windows(engine, *stages, slots=2):
    lead = 4 if slots + max(lag for _, lag in stages) <= 4 else 8

    def place(n):
        for function, lag in stages:
            if 0 <= n - lag < NW:
                function(n - lag, (n - lag) % slots, TAIL if n - lag == NW - 1 else P)

    for n in range(lead):
        place(n)
    with engine.Fori(0, (NW - 1 - lead) // slots) as turn:
        for part in range(slots):
            for function, lag in stages:
                function(turn * slots + (lead + part - lag), (part - lag) % slots, P)
    for n in range(NW - 1, NW + max(lag for _, lag in stages)):
        place(n)


def early(w, n):
    return isinstance(w, int) and w < n


def row_moments(dve, k, x, stats, chain, base):
    dve.bn_stats(stats[:, 0:6], x).then_inc(chain, 1)
    dve.wait_ge(chain, base + 1)
    dve.sem_inc(k.s_hold, 1)
    return dve.bn_aggr(stats[:, 6:8], stats[:, 0:6])


def gin_front(nc, k, g, tag, t_free):
    s_z, s_zps, s_zt, s_t = sems(nc, k, *(f"{tag}_{n}" for n in ("z", "zps", "zt", "t")))
    x = k.X.rearrange("p w d -> p (w d)")

    def combine(dve):
        def stage(w, slot, nodes):
            dve.wait_ge(s_zps, w + 1)
            dve.scalar_tensor_tensor(out=g.z[:, slot, :], in0=x[:, node_window(w)], scalar=g.eps1[:, 0:1],
                                     in1=k.acc[:, sum_window(w)], op0=ALU.mult, op1=ALU.add).then_inc(s_z, 1)
        return stage

    def turn(pe):
        pe.sem_inc(s_zps, 2)
        pe.sem_inc(s_t, 2)

        def stage(w, slot, nodes):
            pe.wait_ge(s_z, w + 1)
            pe.wait_ge(s_zt, w + 1)
            for c in range(2):
                ins = pe.transpose(g.zps[slot][:, c * P:(c + 1) * P], g.z[:, slot, c * P:(c + 1) * P], k.ident[:, :])
            ins.then_inc(s_zps, 1)
        return stage

    def copy_turned(act):
        act.sem_inc(s_zt, 2)

        def stage(w, slot, nodes):
            act.wait_ge(s_zps, w + 3)
            act.wait_ge(s_t, w + 1)
            act.copy(g.zt[:, slot, :], g.zps[slot][:, 0:D]).then_inc(s_zt, 1)
        return stage

    def hidden(pe):
        def stage(w, slot, nodes):
            pe.wait_ge(s_zt, w + 3)
            pe.wait_ge(t_free, w + 1)
            for m in range(4):
                for c in range(2):
                    ins = pe.matmul(g.tps[slot][:, m * P:(m + 1) * P], g.w1[:, c, m * P:(m + 1) * P],
                                    g.zt[:, slot, c * P:(c + 1) * P], start=(c == 0), stop=(c == 1))
            ins.then_inc(s_t, 1)
        return stage

    return combine, turn, copy_turned, hidden, s_t


def gin_mlp(nc, k, a):
    with ExitStack() as ctx:
        g = Kit()
        room = Arena(k.side)
        g.w1 = room.take([P, 2, HID])
        w2 = room.take([P, 4, D])
        b2 = room.take([P, D])
        cols = room.take([P, 3, 4])
        g2 = room.take([1, D])
        bt2 = room.take([1, D])
        g.eps1 = room.take([P, 1])
        g.z = room.take([P, 2, D])
        g.zt = room.take([P, 2, D])
        act1 = room.take([P, 2, HID])
        part = room.take([P, 2, D])
        squares = room.take([P, 2, D])
        total = room.take([P, 2 * D])
        stats = room.take([P, 4, NW * 6])
        moments = room.take([P, 4, 2])
        scale1 = room.take([P, 4])
        shift1 = room.take([P, 4])
        mean1 = room.take([P, 4])
        root1 = room.take([P, 4])
        row = room.take([1, 4, D])
        zeros = k.sims[:, 2 * D:]
        half_zeros = SUMROWS // P * EW // 2
        lines = room.take([P, 4, D])
        nodes_in = room.take([P, 2, NW])
        gates = room.take([P, 4, D])
        both = room.take([P, 2, D])
        g.zps = [psum(nc, ctx, f"gin_z{i}", [P, 512]) for i in range(2)]
        g.tps = [psum(nc, ctx, f"gin_t{i}", [P, 512]) for i in range(2)]
        ups = [psum(nc, ctx, f"gin_u{i}", [P, 512]) for i in range(2)]
        tot_ps = psum(nc, ctx, "gin_tot", [1, 512])
        bc_ps = psum(nc, ctx, "gin_bc", [P, 512])
        x = k.X.rearrange("p w d -> p (w d)")
        s_w, s_eps, s_stat, s_norm1, s_act1, s_u, s_x, s_usum, s_usq, s_tot, s_row, s_bc, s_all, s_zero, s_clear, s_tick, \
            s_root = sems(
            nc, k, *(f"gin_{n}" for n in ("w", "eps", "stat", "norm1", "act1", "u", "x", "usum", "usq", "tot", "row",
                                          "bc", "all", "zero", "clear", "tick", "root")))

        s_line, s_gate, s_both = sems(nc, k, "ng_line", "ng_gate", "ng_both")
        s_sent = sems(nc, k, "ng_sent0", "ng_sent1")

        combine, turn, copy_turned, hidden, s_t = gin_front(nc, k, g, "gina", s_stat)
        with nc.Block() as block:
            @block.sync
            def _(sp):
                sp.dma_start(g.w1[:, :, :], a["L0_gnn_W1"].rearrange("(c p) m -> p c m", p=P)).then_inc(s_w, 16)
                sp.dma_start(w2[:, :, :], a["L0_gnn_W2"].rearrange("(c p) m -> p c m", p=P)).then_inc(s_w, 16)
                sp.dma_start(b2[:, :], a["L0_gnn_b2"].to_broadcast([P, D])).then_inc(s_w, 16)
                for n, name in enumerate(("L0_gnn_b1", "L0_gnn_g1", "L0_gnn_bt1")):
                    sp.dma_start(cols[:, n, :], a[name].rearrange("o (c p) -> p (o c)", p=P),
                                 allow_slow_non_contiguous=True).then_inc(s_w, 16)
                sp.dma_start(g2[:, :], a["L0_gnn_g2"]).then_inc(s_w, 16)
                sp.dma_start(bt2[:, :], a["L0_gnn_bt2"]).then_inc(s_w, 16)
                sp.dma_start(g.eps1[:, :], a["L0_gnn_eps_gin"].to_broadcast([P, 1])).then_inc(s_w, 16)
                for n, name in enumerate(("W_cent", "b_cent", "W_vor", "b_vor")):
                    sp.dma_start(lines[:, n, :], a[f"L2_gnn_{name}"].to_broadcast([P, D])).then_inc(s_w, 16)
                sp.dma_start(nodes_in[:, 0, :], a["node_vec1_n2"]).then_inc(s_w, 16)
                sp.dma_start(nodes_in[:, 1, :], a["node_vec1"]).then_inc(s_w, 16)

                def send(w, slot, nodes):
                    sp.wait_ge(s_both, w + 1)
                    sp.dma_start(k.node_gates[bass.ds(w * P, P), :], both[:, slot, :]).then_inc(s_sent[slot], 16)

                over_windows(sp, (send, 0))
                sp.wait_ge(s_sent[0], 16 * (NW + 1) // 2)
                sp.wait_ge(s_sent[1], 16 * (NW // 2))

            @block.gpsimd
            def _(pool):
                def add_gates(w, slot, nodes):
                    pool.wait_ge(s_gate, w + 1)
                    if not early(w, 2):
                        pool.wait_ge(s_sent[slot], (w - slot) * 8)
                    pool.tensor_tensor(both[:, slot, :], gates[:, slot * 2, :], gates[:, slot * 2 + 1, :],
                                       ALU.add).then_inc(s_both, 1)

                over_windows(pool, (add_gates, 0))

            @block.vector
            def _(dve):
                dve.tensor_copy(k.count_in[:, :], k.acc.rearrange("p (w d) -> p w d", d=AW)[:, :, D])
                dve.wait_ge(s_w, 16 * 15)
                dve.tensor_scalar(g.eps1[:, :], g.eps1[:, :], 1.0, None, ALU.add).then_inc(s_eps, 1)
                dve.sem_inc(s_stat, 2)
                dve.wait_ge(s_eps, 1)

                def measure(w, slot, nodes):
                    dve.wait_ge(s_t, w + 3)
                    for m in range(4):
                        ins = dve.bn_stats(stats[:, m, bass.ds(w * 6, 6)], g.tps[slot][:, m * P:m * P + nodes])
                    ins.then_inc(s_stat, 1)

                def line(w, slot, nodes):
                    if not early(w, 2):
                        dve.wait_ge(s_both, w - 1)
                    for n in range(2):
                        dve.scalar_tensor_tensor(out=gates[:, slot * 2 + n, :], in0=lines[:, 2 * n, :],
                                                 scalar=nodes_in[:, n, bass.ds(w, 1)], in1=lines[:, 2 * n + 1, :],
                                                 op0=ALU.mult, op1=ALU.add).then_inc(s_line, 1)

                over_windows(dve, (combine(dve), 0), (measure, 2), (line, 1))
                dve.wait_ge(s_stat, NW + 2)
                for m in range(4):
                    dve.bn_aggr(moments[:, m, :], stats[:, m, :]).then_inc(s_norm1, 1)
                dve.wait_ge(s_norm1, 4)
                dve.wait_ge(s_root, 1)
                dve.reciprocal(scale1[:, :], root1[:, :]).then_inc(s_norm1, 1)
                dve.tensor_tensor(mean1[:, :], moments[:, :, 0], cols[:, 0, :], ALU.add).then_inc(s_norm1, 1)
                dve.wait_ge(s_norm1, 6)
                dve.tensor_tensor(scale1[:, :], scale1[:, :], cols[:, 1, :], ALU.mult).then_inc(s_norm1, 1)
                dve.tensor_tensor(shift1[:, :], cols[:, 0, :], mean1[:, :], ALU.subtract).then_inc(s_norm1, 1)
                dve.wait_ge(s_norm1, 8)
                dve.tensor_tensor(shift1[:, :], shift1[:, :], scale1[:, :], ALU.mult).then_inc(s_norm1, 1)
                dve.wait_ge(s_norm1, 9)
                dve.tensor_tensor(shift1[:, :], shift1[:, :], cols[:, 2, :], ALU.add).then_inc(s_norm1, 1)

            @block.tensor
            def _(pe):
                turn_z, hidden_t = turn(pe), hidden(pe)
                pe.wait_ge(s_w, 16 * 15)
                over_windows(pe, (hidden_t, 1), (turn_z, 0))

            @block.scalar
            def _(act):
                def gate(w, slot, nodes):
                    act.wait_ge(s_line, w * 2 + 2)
                    act.activation(gates[:, slot * 2:slot * 2 + 2, :], gates[:, slot * 2:slot * 2 + 2, :],
                                   ACT.Sigmoid).then_inc(s_gate, 1)

                over_windows(act, (gate, 2), (copy_turned(act), 0))
                act.wait_ge(s_norm1, 4)
                act.activation(root1[:, :], moments[:, :, 1], ACT.Sqrt, bias=k.eps[:, 0:1]).then_inc(s_root, 1)

        combine, turn, copy_turned, hidden, s_t = gin_front(nc, k, g, "ginb", s_act1)
        with nc.Block() as block:
            @block.sync
            def _(sp):
                sp.wait_ge(s_zero, 2)
                for b in range(BANKS):
                    sp.dma_start(k.attr_sum[b].rearrange("(p r) d -> p (r d)", p=P),
                                 zeros[:, 0:SUMROWS // P * EW]).then_inc(s_clear, 16)
                    for half in range(2):
                        sp.dma_start(k.out_sum[b].rearrange("(p h r) d -> p h (r d)", p=P, h=2)[:, half, :],
                                     zeros[:, 0:SUMROWS // P * D // 2]).then_inc(s_clear, 16)
                sp.wait_ge(s_clear, 16 * 3 * BANKS)

            @block.gpsimd
            def _(pool):
                pool.memset(total[:, :], 0.0).then_inc(s_tot, 2)

                def column_sums(w, slot, nodes):
                    pool.wait_ge(s_usq, w + 1)
                    pool.wait_ge(s_tot, w * 2 + 2)
                    pool.sem_inc(s_tick, 1)
                    pool.tensor_tensor(total[0:nodes, 0:D], total[0:nodes, 0:D], k.acc[0:nodes, sum_window(w)],
                                       ALU.add).then_inc(s_tot, 1)
                    pool.tensor_tensor(total[0:nodes, D:2 * D], total[0:nodes, D:2 * D], squares[0:nodes, slot, :],
                                       ALU.add).then_inc(s_tot, 1)

                over_windows(pool, (column_sums, 4))

            @block.vector
            def _(dve):
                dve.memset(zeros[:, 0:half_zeros], 0.0).then_inc(s_zero, 1)
                dve.memset(zeros[:, half_zeros:], 0.0).then_inc(s_zero, 1)
                dve.sem_inc(s_u, 2)

                def close(w, slot, nodes):
                    dve.wait_ge(s_x, w + 3)
                    dve.wait_ge(s_usum, w + 1)
                    dve.tensor_tensor(part[:, slot, :], ups[slot][:, 0:D], x[:, node_window(w)], ALU.add).then_inc(s_u, 1)
                    dve.wait_ge(s_u, w + 3)
                    dve.tensor_tensor(k.acc[:, sum_window(w)], part[:, slot, :], b2[:, :], ALU.add).then_inc(s_usum, 1)

                dve.sem_inc(s_usum, 2)
                over_windows(dve, (close, 4), (combine(dve), 0))
                mean, var, scale, shift = (row[:, n, :] for n in range(4))
                dve.wait_ge(s_all, 1)
                dve.tensor_scalar(mean, tot_ps[:, 0:D], 1.0 / N, None, ALU.mult).then_inc(s_row, 1)
                dve.wait_ge(s_row, 1)
                dve.tensor_tensor(scale, mean, mean, ALU.mult).then_inc(s_row, 1)
                dve.wait_ge(s_row, 2)
                dve.scalar_tensor_tensor(out=var, in0=tot_ps[:, D:2 * D], scalar=1.0 / N, in1=scale, op0=ALU.mult,
                                         op1=ALU.subtract).then_inc(s_row, 1)
                dve.wait_ge(s_row, 3)
                dve.tensor_scalar(var, var, 0.0, None, ALU.max).then_inc(s_row, 1)
                dve.wait_ge(s_root, 2)
                dve.reciprocal(var, shift).then_inc(s_row, 1)
                dve.wait_ge(s_row, 5)
                dve.tensor_tensor(scale, var, g2[:, :], ALU.mult).then_inc(s_row, 1)
                dve.wait_ge(s_row, 6)
                dve.tensor_tensor(mean, mean, scale, ALU.mult).then_inc(s_row, 1)
                dve.wait_ge(s_row, 7)
                dve.tensor_tensor(shift, bt2[:, :], mean, ALU.subtract).then_inc(s_row, 1)
                dve.wait_ge(s_bc, 1)
                dve.tensor_copy(k.norm2, bc_ps[:, :])

            @block.scalar
            def _(act):
                act.sem_inc(s_act1, 2)

                def activate(w, slot, nodes):
                    act.wait_ge(s_t, w + 3)
                    act.wait_ge(s_x, w + 1)
                    for m in range(4):
                        ins = act.activation(act1[:, slot, m * P:(m + 1) * P], g.tps[slot][:, m * P:(m + 1) * P],
                                             ACT.Relu, bias=shift1[:, m:m + 1], scale=scale1[:, m:m + 1])
                    ins.then_inc(s_act1, 1)

                def square(w, slot, nodes):
                    act.wait_ge(s_usum, w + 3)
                    if not early(w, 2):
                        act.wait_ge(s_tot, w * 2)
                    act.sem_inc(k.s_hold, 1)
                    act.activation(squares[:, slot, :], k.acc[:, sum_window(w)], ACT.Square).then_inc(s_usq, 1)

                over_windows(act, (activate, 1), (square, 4), (copy_turned(act), 0))
                act.wait_ge(s_row, 4)
                act.activation(row[:, 3, :], row[:, 1, :], ACT.Sqrt, bias=k.eps[0:1, 0:1]).then_inc(s_root, 1)

            @block.tensor
            def _(pe):
                pe.sem_inc(s_x, 2)
                turn_z, hidden_t = turn(pe), hidden(pe)

                def product(w, slot, nodes):
                    pe.wait_ge(s_act1, w + 3)
                    pe.wait_ge(s_u, w + 1)
                    for m in range(4):
                        ins = pe.matmul(ups[slot][:, 0:D], act1[:, slot, m * P:(m + 1) * P], w2[:, m, :],
                                        start=(m == 0), stop=(m == 3))
                    ins.then_inc(s_x, 1)

                over_windows(pe, (product, 3), (hidden_t, 1), (turn_z, 0))
                pe.wait_ge(s_tot, 2 * NW + 2)
                pe.matmul(tot_ps[:, :], k.ones[:, 0:1], total[:, :], start=True, stop=True).then_inc(s_all, 1)
                pe.wait_ge(s_row, 8)
                pe.matmul(bc_ps[:, :], k.ones[0:1, :], row[:, 2:4, :].rearrange("o a d -> o (a d)"),
                          start=True, stop=True).then_inc(s_bc, 1)


def gin_close_and_project(nc, k, a):
    with ExitStack() as ctx:
        room = Arena(k.sims[:, 2 * D:])
        wq = room.take([P, 2, D])
        wkv = room.take([P, 2, 2 * D])
        bias = room.take([P, 3 * D])
        new = room.take([P, 2, D])
        turned = room.take([P, 2, D])
        kv = room.take([P, 2, 2 * D])
        part = room.take([P, 2, D])
        stats = room.take([P, 2 * 9])
        zps = [psum(nc, ctx, f"qkv_z{i}", [P, 512]) for i in range(2)]
        qps = [psum(nc, ctx, f"qkv_q{i}", [P, 512]) for i in range(2)]
        kps = [psum(nc, ctx, f"qkv_k{i}", [P, 512]) for i in range(2)]
        x = k.X.rearrange("p w d -> p (w d)")
        s_w, s_part, s_mom, s_root, s_inv, s_new, s_kept, s_zps, s_zt, s_qkv, s_q, s_kv = sems(
            nc, k, *(f"qkv_{n}" for n in ("w", "part", "mom", "root", "inv", "new", "kept", "zps", "zt", "qkv", "q", "kv")))
        s_out = sems(nc, k, "qkv_out0", "qkv_out1")
        block = ctx.enter_context(nc.Block())

        @block.sync
        def _(sp):
            sp.dma_start(wq[:, :, :], a["wq_t"].rearrange("(c p) m -> p c m", p=P)).then_inc(s_w, 16)
            sp.dma_start(wkv[:, :, 0:D], a["wk_t"].rearrange("(c p) m -> p c m", p=P)).then_inc(s_w, 16)
            sp.dma_start(wkv[:, :, D:], a["wv_t"].rearrange("(c p) m -> p c m", p=P)).then_inc(s_w, 16)
            for n, name in enumerate(("L1_gnn_bq", "L1_gnn_bk", "L1_gnn_bv")):
                sp.dma_start(bias[:, n * D:(n + 1) * D], a[name].to_broadcast([P, D])).then_inc(s_w, 16)

            def send(w, slot, nodes):
                sp.wait_ge(s_kv, w + 1)
                sp.dma_start(k.kv_rows[bass.ds(w * P, P), :], kv[:, slot, :]).then_inc(s_out[slot], 16)

            over_windows(sp, (send, 0))
            sp.wait_ge(s_out[0], 16 * (NW + 1) // 2)
            sp.wait_ge(s_out[1], 16 * (NW // 2))

        @block.vector
        def _(dve):
            dve.sem_inc(s_new, 2)
            dve.wait_ge(s_w, 16 * 6)

            def norm(w, slot, nodes):
                st = stats[:, slot * 9:slot * 9 + 9]
                here = part[:, slot, :]
                dve.wait_ge(s_new, w + 1)
                dve.tensor_tensor(here, k.acc[:, sum_window(w)], k.norm2[:, 0:D], ALU.mult).then_inc(s_part, 1)
                dve.wait_ge(s_part, w * 4 + 1)
                dve.tensor_tensor(here, here, k.norm2[:, D:2 * D], ALU.add).then_inc(s_part, 1)
                dve.wait_ge(s_part, w * 4 + 2)
                dve.scalar_tensor_tensor(out=here, in0=here, scalar=0.0, in1=x[:, node_window(w)], op0=ALU.max,
                                         op1=ALU.add).then_inc(s_part, 1)
                dve.wait_ge(s_part, w * 4 + 3)
                row_moments(dve, k, here, st, s_part, w * 4 + 3).then_inc(s_mom, 1)

            def scale(w, slot, nodes):
                st = stats[:, slot * 9:slot * 9 + 9]
                dve.wait_ge(s_root, w + 1)
                dve.reciprocal(st[:, 8:9], st[:, 8:9]).then_inc(s_inv, 1)
                dve.wait_ge(s_inv, w + 1)
                dve.wait_ge(s_zps, w + 1)
                dve.wait_ge(s_kept, w + 1)
                dve.tensor_scalar(new[:, slot, :], part[:, slot, :], st[:, 6:7], st[:, 8:9], ALU.subtract,
                                  ALU.mult).then_inc(s_new, 1)

            def biases(w, slot, nodes):
                dve.wait_ge(s_qkv, w + 3)
                dve.tensor_tensor(k.side[:, node_window(w)], qps[slot][:, 0:D], bias[:, 0:D], ALU.add)
                if isinstance(w, int) and w < 2:
                    pass
                else:
                    dve.wait_ge(s_out[slot], (w - slot) * 8)
                dve.tensor_tensor(kv[:, slot, :], kps[slot][:, :], bias[:, D:], ALU.add).then_inc(s_kv, 1)

            over_windows(dve, (biases, 4), (scale, 1), (norm, 0))

        @block.tensor
        def _(pe):
            pe.sem_inc(s_zps, 2)
            pe.sem_inc(s_qkv, 2)
            pe.wait_ge(s_w, 16 * 6)

            def turn(w, slot, nodes):
                pe.wait_ge(s_new, w + 3)
                pe.wait_ge(s_zt, w + 1)
                for c in range(2):
                    ins = pe.transpose(zps[slot][:, c * P:(c + 1) * P], new[:, slot, c * P:(c + 1) * P], k.ident[:, :])
                ins.then_inc(s_zps, 1)

            def project(w, slot, nodes):
                pe.wait_ge(s_zt, w + 3)
                if isinstance(w, int) and w < 2:
                    pass
                else:
                    pe.wait_ge(s_kv, w - 1)
                for c in range(2):
                    pe.matmul(qps[slot][:, 0:D], turned[:, slot, c * P:(c + 1) * P], wq[:, c, :], start=(c == 0),
                              stop=(c == 1))
                for c in range(2):
                    ins = pe.matmul(kps[slot][:, :], turned[:, slot, c * P:(c + 1) * P], wkv[:, c, :], start=(c == 0),
                                    stop=(c == 1))
                ins.then_inc(s_qkv, 1)

            over_windows(pe, (project, 3), (turn, 2))

        @block.scalar
        def _(act):
            act.sem_inc(s_zt, 2)
            act.sem_inc(s_kept, 2)

            def keep(w, slot, nodes):
                act.wait_ge(s_new, w + 3)
                act.copy(x[:, node_window(w)], new[:, slot, :]).then_inc(s_kept, 1)
                act.wait_ge(s_zps, w + 3)
                act.wait_ge(s_qkv, w + 1)
                act.copy(turned[:, slot, :], zps[slot][:, 0:D]).then_inc(s_zt, 1)

            def root(w, slot, nodes):
                act.wait_ge(s_mom, w + 1)
                st = stats[:, slot * 9:slot * 9 + 9]
                act.activation(st[:, 8:9], st[:, 7:8], ACT.Sqrt, bias=k.eps[:, 0:1]).then_inc(s_root, 1)

            over_windows(act, (keep, 2), (root, 0))


def edge_scores(nc, k):
    with ExitStack() as ctx:
        room = Arena(k.acc)
        ring = room.take([P, U, 2 * D])
        by_edge = room.take([P, HALF, P])
        onehot = room.take([P, 4, P])
        prod = room.take([P, 2, D])
        cur_idx = room.take([P, U], I32)
        cur_dst = room.take([P, U])
        cur_sim = room.take([P, U, HEADS])
        query = k.side
        qps = [psum(nc, ctx, f"es_q{i}", [P, 512]) for i in range(4)]
        tps = [psum(nc, ctx, f"es_t{i}", [P, 512]) for i in range(4)]
        s_cur, s_tick, s_mark, s_turn, s_hot, s_q, s_prod, s_sim, s_stored, s_copied = sems(
            nc, k, *(f"es_{n}" for n in ("cur", "tick", "mark", "turn", "hot", "q", "prod", "sim", "stored", "copied")))
        s_vout = sems(nc, k, *(f"es_vout{u}" for u in range(U)))
        s_row, row0 = k.s_row, k.rows_before
        k.rows_before += 16 * IT
        block = ctx.enter_context(nc.Block())

        @block.gpsimd
        def _(pool):
            with pool.Fori(0, IT) as it:
                for u in range(U):
                    if u % HALF == 0:
                        pool.wait_ge(s_cur, it * 2 + (1 + u // HALF))
                    pool.wait_ge(s_prod, it * U + (u + 1))
                    pool.wait_ge(s_stored, it * U + (u + 1))
                    pool.sem_inc(s_tick, 1)
                    pool.indirect_dma_start(ring[:, u, :], None, k.kv_rows, bass.IndirectOffsetOnAxis(
                        ap=cur_idx[:, u:u + 1], axis=0)).then_inc(s_row[u], 16)

        @block.sync
        def _(sp):
            sp.sem_inc(s_stored, U)
            LAG = 4

            def stored(it, u):
                sp.wait_ge(s_vout[u], it * 16 + 16)
                sp.sem_inc(s_stored, 1)

            with sp.Fori(0, IT) as it:
                for u in range(U):
                    sp.wait_ge(s_row[u], it * 16 + (row0 + 16))
                    sp.dma_start(k.v_edge[bass.ds(it * U * P + u * P, P), :], ring[:, u, D:]).then_inc(s_vout[u], 16)
                    if u >= LAG:
                        stored(it, u - LAG)
                for u in range(U - LAG, U):
                    stored(it, u)

        @block.tensor
        def _(pe):
            def turn(it, u):
                pe.wait_ge(s_mark, it * U + (u + 1))
                pe.wait_ge(s_hot, it * U + (u + 1))
                pe.transpose(tps[u % 4][:, 0:P], by_edge[:, u % HALF, :], k.ident[:, :]).then_inc(s_turn, 1)

            pe.sem_inc(s_q, 4)
            pe.sem_inc(s_turn, HALF)
            turn(0, 0)
            turn(0, 1)
            with pe.Fori(0, IT) as it:
                win = load_steps(nc, pe, k.win, it, NW - 1)
                for u in range(U):
                    turn(it, u + 2)
                    pe.wait_ge(s_hot, it * U + (4 + u + 1))
                    pe.wait_ge(s_prod, it * U + (U + u + 1 - 4))
                    pe.matmul(qps[u % 4][:, 0:D], onehot[:, u % 4, :], query[:, node_window(win[u])],
                              start=True, stop=True).then_inc(s_q, 1)

        @block.scalar
        def _(act):
            act.sem_inc(s_hot, 4)
            with act.Fori(0, IT) as it:
                for u in range(U):
                    act.wait_ge(s_turn, it * U + (HALF + u + 1))
                    act.wait_ge(s_q, it * U + (u + 1))
                    act.copy(onehot[:, u % 4, :], tps[u % 4][:, 0:P]).then_inc(s_hot, 1)

        @block.vector
        def _(dve):
            def refill(h, at):
                part = slice(h * HALF, (h + 1) * HALF)
                dve.tensor_copy(cur_dst[:, part], k.dst[:, bass.ds(at, HALF)])
                dve.tensor_copy(cur_idx[:, part], k.idx[:, bass.ds(at, HALF)]).then_inc(s_cur, 1)

            def hot(it, u):
                if u % HALF == 0:
                    dve.wait_ge(s_cur, it * 2 + (1 + u // HALF))
                dve.wait_ge(s_turn, it * U + (u + QUAD))
                compare(dve, k, by_edge[:, u % HALF:u % HALF + QUAD, :], None,
                        cur_dst[:, u % U:u % U + QUAD]).then_inc(s_mark, QUAD)

            def score(it, u):
                dve.wait_ge(s_q, it * U + (u + 1 + 4))
                dve.wait_ge(s_row[u], it * 16 + (row0 + 16))
                dve.wait_ge(s_sim, it * U + (u + 1))
                dve.tensor_tensor(prod[:, u % 2, :], qps[u % 4][:, 0:D], ring[:, u, 0:D], ALU.mult).then_inc(s_prod, 1)

            def heads(it, u):
                dve.wait_ge(s_prod, it * U + (U + u + 1))
                dve.tensor_reduce(cur_sim[:, u, :], prod[:, u % 2, :].rearrange("p (h d) -> p h d", h=HEADS), AX.X,
                                  ALU.add).then_inc(s_sim, 1)

            for h in range(2):
                refill(h, h * HALF)
            dve.sem_inc(s_prod, U)
            dve.sem_inc(s_sim, 2)
            dve.sem_inc(s_copied, 2)
            def keep(it, h):
                dve.wait_ge(s_sim, it * U + ((h + 1) * HALF + 2))
                dve.sem_inc(k.s_hold, 1)
                dve.tensor_copy(k.sims[:, bass.ds(it * U * HEADS + h * HALF * HEADS, HALF * HEADS)],
                                cur_sim[:, h * HALF:(h + 1) * HALF, :].rearrange("p u h -> p (u h)")).then_inc(s_copied, 1)

            hot(0, 0)
            with dve.Fori(0, IT) as it:
                for u in range(U):
                    if u % QUAD == 0:
                        hot(it, u + QUAD)
                    if u % HALF == 0:
                        dve.wait_ge(s_copied, it * 2 + (1 + u // HALF))
                    score(it, u)
                    if u:
                        heads(it, u - 1)
                    if u % HALF == HALF - 1:
                        refill(u // HALF, it * U + (U + u + 1 - HALF))
                    if u == HALF + 1:
                        keep(it, 0)
                heads(it, U - 1)
                keep(it, 1)


def softmax_weights(nc, k):
    T = 5
    STEPS_OF_SCAN = 9
    with ExitStack() as ctx:
        room = Arena(k.big[:, :])
        one = room.take([P, SCAN])
        two = room.take([P, SCAN])
        three = room.take([P, SCAN])
        neg = room.take([P, STEPS])
        stage = room.take([P, T, P])
        edge = room.take([P, 2, 2])
        carry = room.take([P, 2])
        row_last = room.take([1, P])
        row_open = room.take([1, P])
        row_scan = room.take([1, P])
        row_in = room.take([1, P])
        tps = [psum(nc, ctx, f"sm_t{i}", [P, P]) for i in range(T)]
        rps = psum(nc, ctx, "sm_r", [1, 2, P])
        cps = psum(nc, ctx, "sm_c", [P, 2])
        s_key, s_mask, s_stage, s_turn, s_in, s_c, s_edge, s_row, s_col, s_back, s_bturn, s_out = sems(
            nc, k, *(f"sm_{n}" for n in ("key", "mask", "stage", "turn", "in", "c", "edge", "row", "col", "back",
                                         "bturn", "out")))
        sims = k.sims.rearrange("p (g j h) -> p j g h", g=GROUPS, h=HEADS)
        flat = k.key_row

        def keys(offset):
            run = flat[P + offset:P + offset + GROUPS * SCAN].rearrange("(g o t) -> g o t", g=GROUPS, o=1)
            return run.to_broadcast([GROUPS, HEADS, SCAN])

        block = ctx.enter_context(nc.Block())

        @block.sync
        def _(sp):
            sp.dma_start(one, keys(0)).then_inc(s_key, 16)
            sp.dma_start(two, keys(-1)).then_inc(s_key, 16)
            sp.wait_ge(s_c, STEPS_OF_SCAN)
            sp.dma_start(three, keys(0)).then_inc(s_key, 16)
            sp.dma_start(two, keys(1)).then_inc(s_key, 16)

        @block.scalar
        def _(act):
            act.sem_inc(s_stage, T)
            act.wait_ge(s_mask, 2)
            with act.Fori(0, GS // T) as it:
                for u in range(T):
                    act.wait_ge(s_turn, it * T + (u + 1))
                    act.copy(stage[:, u, :].rearrange("p (g h) -> p g h", g=GROUPS),
                             sims[:, bass.ds(it * T + u, 1), :, :].rearrange("p j g h -> p (j g) h")).then_inc(s_stage, 1)
            act.wait_ge(s_c, 2 * STEPS_OF_SCAN)
            with act.Fori(0, GS // T) as it:
                for u in range(T):
                    act.wait_ge(s_turn, it * T + (GS + u + 1))
                    act.copy(stage[:, u, :], three[:, bass.ds(it * T * P + u * P, P)]).then_inc(s_stage, 1)
            act.wait_ge(s_out, GS + T)
            act.activation(k.sims, k.sims, ACT.Exp, scale=SCALE).then_inc(s_back, 1)

        @block.tensor
        def _(pe):
            pe.sem_inc(s_turn, T)

            def turn(base):
                with pe.Fori(0, GS // T) as it:
                    for u in range(T):
                        pe.wait_ge(s_stage, it * T + (base + T + u + 1))
                        pe.wait_ge(s_in if base == 0 else s_out, it * T + (u + 1))
                        pe.transpose(tps[u][:, :], stage[:, u, :], k.ident[:, :]).then_inc(s_turn, 1)

            def edges(n):
                pe.wait_ge(s_edge, 2 * n + 2)
                pe.transpose(rps[:, 0, :], edge[:, n, 0:1], k.ident[:, :])
                pe.transpose(rps[:, 1, :], edge[:, n, 1:2], k.ident[:, :]).then_inc(s_row, 1)
                pe.wait_ge(s_col, n + 1)
                pe.matmul(cps[:, n:n + 1], row_in[:, :], k.ones[0:1, 0:1], start=True, stop=True).then_inc(s_row, 1)

            turn(0)
            edges(0)
            edges(1)
            turn(GS)

        @block.vector
        def _(dve):
            dve.tensor_scalar(neg[:, :], k.own[:, 0:STEPS], 0.0, -BIG, ALU.is_lt, ALU.mult).then_inc(s_mask, 1)
            dve.wait_ge(s_mask, 1)
            by_step = k.sims.rearrange("p (i h) -> p i h", h=HEADS)
            dve.tensor_tensor(by_step, by_step, neg[:, :].unsqueeze(2).to_broadcast([P, STEPS, HEADS]),
                              ALU.add).then_inc(s_mask, 1)
            dve.sem_inc(s_in, T)
            with dve.Fori(0, GS // T) as it:
                for u in range(T):
                    dve.wait_ge(s_turn, it * T + (T + u + 1))
                    dve.tensor_scalar(three[:, bass.ds(it * T * P + u * P, P)], tps[u][:, :], 1.0, None,
                                      ALU.mult).then_inc(s_in, 1)

            def scan(n, out, key, near, data, lead, tail, done):
                flip = (lambda x: x) if n == 0 else (lambda x: x[:, ::-1])
                c = lambda: dve.wait_ge(s_c, done[0])

                def next_c(ins):
                    ins.then_inc(s_c, 1)
                    done[0] += 1
                down = (lambda far, at: (at, far)) if n == 0 else (lambda far, at: (far, at))
                dve.tensor_tensor(edge[:, n, 1:2], *down(key[:, tail], near[:, lead]), ALU.subtract).then_inc(s_edge, 1)
                dve.wait_ge(s_edge, 2 * n + 1)
                next_c(dve.tensor_tensor(near, *down(key, near), ALU.subtract))
                c()
                next_c(dve.tensor_tensor_scan(flip(out), flip(near), flip(data), LOW, ALU.add, ALU.max))
                c()
                dve.tensor_copy(edge[:, n, 0:1], out[:, tail]).then_inc(s_edge, 1)
                by_head = lambda row: row.rearrange("o (h g) -> o h g", h=HEADS)
                by_run = lambda row: row.rearrange("o (g h) -> o h g", h=HEADS)
                dve.wait_ge(s_row, 2 * n + 1)
                next_c(dve.tensor_copy(by_head(row_last), by_run(rps[:, 0, :])))
                next_c(dve.tensor_copy(by_head(row_open), by_run(rps[:, 1, :])))
                c()
                first = 0 if n == 0 else GROUPS - 1
                next_c(dve.memset(by_head(row_open)[:, :, first:first + 1], LOW))
                next_c(dve.memset(row_in[:, :], LOW))
                c()
                next_c(dve.tensor_tensor_scan(flip(row_scan), flip(row_open), flip(row_last), LOW, ALU.add, ALU.max))
                c()
                to, of = (slice(1, GROUPS), slice(0, GROUPS - 1)) if n == 0 else (slice(0, GROUPS - 1), slice(1, GROUPS))
                dve.tensor_copy(by_run(row_in)[:, :, to], by_head(row_scan)[:, :, of]).then_inc(s_col, 1)
                dve.wait_ge(s_row, 2 * n + 2)
                next_c(dve.tensor_copy(carry[:, n:n + 1], cps[:, n:n + 1]))
                c()
                next_c(dve.tensor_tensor_scan(flip(out), flip(near), flip(data), carry[:, n:n + 1], ALU.add, ALU.max))
                c()
            done = [0]
            start, end = slice(0, 1), slice(SCAN - 1, SCAN)
            dve.wait_ge(s_in, GS + T)
            dve.wait_ge(s_key, 32)
            scan(0, one, one, two, three, start, end, done)
            assert done[0] == STEPS_OF_SCAN, done
            dve.wait_ge(s_key, 64)
            scan(1, three, three, two, one, end, start, done)
            dve.sem_inc(s_out, T)
            with dve.Fori(0, GS // T) as it:
                for u in range(T):
                    here = sims[:, bass.ds(it * T + u, 1), :, :].rearrange("p j g h -> p (j g) h")
                    dve.wait_ge(s_turn, it * T + (GS + T + u + 1))
                    dve.tensor_tensor(here, here, tps[u][:, :].rearrange("p (g h) -> p g h", g=GROUPS),
                                      ALU.subtract).then_inc(s_out, 1)


def weighted_sums(nc, k, attr_rows):
    with ExitStack() as ctx:
        room = Arena(k.side)
        ring = room.take([P, U, D])
        weighted = room.take([P, 4, AW])
        onehot = room.take([P, HALF, P])
        cur_dst = room.take([P, U])
        attr = room.take([P, U, EW])
        equal = room.take([P, HALF, P])
        ready = room.take([P, HALF, EW])
        cur_own = room.take([P, U])
        cur_src = room.take([P, U])
        cur_row = room.take([P, U], I32)
        spare = room.take([P, 1], I32)
        sums = [psum(nc, ctx, f"ws_sums{i}", [P, 512]) for i in range(4)]
        asums = [psum(nc, ctx, f"at_sums{i}", [P, 512]) for i in range(2)]
        wide = [psum(nc, ctx, f"at_wide{i}", [P, 512]) for i in range(2)]
        s_cur, s_hot, s_weight, s_side, s_sum, s_acc, s_zero = sems(
            nc, k, *(f"ws_{n}" for n in ("cur", "hot", "weight", "side", "sum", "acc", "zero")))
        s_one, s_rowcur, s_equal, s_mm, s_ready, s_prime, s_tick, s_wide = sems(
            nc, k, *(f"at_{n}" for n in ("one", "rowcur", "equal", "mm", "ready", "prime", "tick", "wide")))
        s_v = sems(nc, k, *(f"ws_v{q}" for q in range(U // 2)))
        s_attr = sems(nc, k, *(f"at_attr{q}" for q in range(U // QUAD)))
        s_sent = k.s_sent
        block = ctx.enter_context(nc.Block())

        @block.sync
        def _(sp):
            with sp.Fori(0, IT) as it:
                chunk = load_steps(nc, sp, k.chunk, it, NC - 1)
                for u in range(U):
                    if u % QUAD == 0:
                        sp.wait_ge(s_mm, it * U + (u + QUAD))
                        sp.dma_start(attr[:, u:u + QUAD, 0:EA], attr_rows[bass.ds(chunk[u] * P, QUAD * P), :].rearrange(
                            "(c p) d -> p c d", p=P)).then_inc(s_attr[u // QUAD], 16)
                    if u % 2 == 0:
                        sp.wait_ge(s_weight, it * U + (u + 2))
                        sp.dma_start(ring[:, u:u + 2, :], k.v_edge[bass.ds(it * U * P + u * P, 2 * P), :].rearrange(
                            "(s p) d -> p s d", p=P)).then_inc(s_v[u // 2], 16)

        @block.scalar
        def _(act):
            act.sem_inc(s_ready, U)
            with act.Fori(0, IT) as it:
                for u in range(U):
                    act.wait_ge(s_sum, it * U + (u + 1 + 4))
                    act.copy(weighted[:, u % 4, D:], k.sims[:, bass.ds(it * U * HEADS + u * HEADS, HEADS)]).then_inc(
                        s_side, 1)
                    act.wait_ge(s_mm, it * U + (U + u + 1))
                    act.wait_ge(s_sent[u % HALF], it * 32 + 16 * (1 + u // HALF))
                    act.copy(ready[:, u % HALF, :], asums[u % 2][:, 0:EW]).then_inc(s_ready, 1)

        @block.gpsimd
        def _(pool):
            pool.wait_ge(s_prime, 2)
            for v in range(HALF):
                if v >= BANKS:
                    pool.wait_ge(s_sent[v - BANKS], 16)
                pool.indirect_dma_start(k.attr_sum[v % BANKS], bass.IndirectOffsetOnAxis(ap=spare[:, 0:1], axis=0),
                                        ready[:, v, :], None, compute_op=ALU.add).then_inc(s_sent[v], 16)
            with pool.Fori(0, IT) as it:
                for u in range(U):
                    if u % HALF == 0:
                        pool.wait_ge(s_rowcur, it * 2 + (u // HALF + 1))
                    pool.wait_ge(s_ready, it * U + (U + u + 1))
                    pool.wait_ge(s_sent[(u - BANKS) % HALF], it * 32 + 16 * (2 + (u - BANKS) // HALF))
                    pool.sem_inc(s_tick, 1)
                    pool.indirect_dma_start(k.attr_sum[u % BANKS], bass.IndirectOffsetOnAxis(ap=cur_row[:, u:u + 1], axis=0),
                                            ready[:, u % HALF, :], None, compute_op=ALU.add).then_inc(s_sent[u % HALF], 16)
            for v in range(HALF):
                pool.wait_ge(s_sent[v], 16 * (1 + 2 * IT))

        @block.tensor
        def _(pe):
            pe.sem_inc(s_sum, HALF)
            pe.sem_inc(s_mm, U)
            pe.wait_ge(s_one, 1)
            by_chunk = attr.rearrange("p c d -> p (c d)")

            def sources(it, u):
                if u % HALF == 0:
                    pe.wait_ge(s_cur, it * 2 + (1 + u // HALF))
                if u >= HALF:
                    pe.wait_ge(s_equal, it * U + (u - QUAD))
                widen(pe, k, wide[u // QUAD % 2], cur_src[:, u % U:u % U + QUAD]).then_inc(s_wide, QUAD)

            sources(0, 0)
            sources(0, QUAD)
            with pe.Fori(0, IT) as it:
                beyond = load_steps(nc, pe, k.beyond, it, QUAD - 1)
                for u in range(U):
                    first = u // QUAD * QUAD
                    if u == first:
                        sources(it, u + HALF)
                    if u == first:
                        pe.wait_ge(s_attr[u // QUAD], it * 16 + 16)
                    pe.wait_ge(s_equal, it * U + (u + 1))
                    pe.wait_ge(s_ready, it * U + (U + u + 1 - 2))
                    pe.matmul(asums[u % 2][:, 0:EW], equal[:, u % HALF, :],
                              by_chunk[:, bass.ds((beyond[u] + first) * EW, EW)],
                              start=True, stop=True).then_inc(s_mm, 1)
                    pe.wait_ge(s_weight, it * U + (U + u + 1))
                    pe.wait_ge(s_side, it * U + (u + 1))
                    pe.wait_ge(s_hot, it * U + (u + 1))
                    pe.wait_ge(s_acc, it * U + (u + 1))
                    pe.matmul(sums[u % 4][:, 0:AW], onehot[:, u % HALF, :], weighted[:, u % 4, :],
                              start=True, stop=True).then_inc(s_sum, 1)

        @block.vector
        def _(dve):
            def refill(h, at):
                part = slice(h * HALF, (h + 1) * HALF)
                dve.tensor_copy(cur_dst[:, part], k.dst[:, bass.ds(at, HALF)])
                dve.tensor_copy(cur_src[:, part], k.src[:, bass.ds(at, HALF)])
                dve.tensor_copy(cur_own[:, part], k.own[:, bass.ds(at, HALF)]).then_inc(s_cur, 1)

            def tables(it, u):
                at, slots = u % U, slice(u % HALF, u % HALF + QUAD)
                if u % HALF == 0:
                    dve.wait_ge(s_cur, it * 2 + (1 + u // HALF))
                dve.wait_ge(s_wide, it * U + (u + QUAD))
                dve.wait_ge(s_mm, it * U + (u + QUAD + U - HALF))
                compare(dve, k, equal[:, slots, :], wide[u // QUAD % 2][:, :].rearrange("p (s e) -> p s e", s=QUAD), cur_own[:, at:at + QUAD]).then_inc(
                    s_equal, QUAD)
                dve.wait_ge(s_sum, it * U + (u + QUAD))
                compare(dve, k, onehot[:, slots, :], None, cur_dst[:, at:at + QUAD]).then_inc(s_hot, QUAD)

            def weigh(it, u):
                at, more = u % U, u // U
                dve.wait_ge(s_sum, it * U + (u + 1 + 4))
                if u % 2 == 0:
                    dve.wait_ge(s_v[at // 2], it * 16 + 16 * (1 + more))
                weight = k.sims[:, bass.ds(it * U * HEADS + u * HEADS, HEADS)]
                dve.tensor_tensor(weighted[:, u % 4, 0:D].rearrange("p (h d) -> p h d", h=HEADS),
                                  ring[:, at, :].rearrange("p (h d) -> p h d", h=HEADS),
                                  weight.unsqueeze(2).to_broadcast([P, HEADS, HD]), ALU.mult).then_inc(s_weight, 1)

            def add(it, u, win):
                dve.wait_ge(s_sum, it * U + (u + 1 + HALF))
                dve.wait_ge(s_acc, it * U + (u + 4))
                here = k.acc[:, sum_window(win, AW)]
                dve.tensor_tensor(here, sums[u % 4][:, 0:AW], here, ALU.add).then_inc(s_acc, 1)

            dve.memset(attr[:, :, EA:EW], 1.0).then_inc(s_one, 1)
            dve.memset(ready[:, :, :], 0.0).then_inc(s_prime, 1)
            dve.tensor_copy(spare[:, :], k.trash[:, :]).then_inc(s_prime, 1)
            dve.memset(k.acc, 0.0).then_inc(s_zero, 1)
            dve.wait_ge(s_zero, 1)
            for h in range(2):
                refill(h, h * HALF)
            dve.sem_inc(s_weight, U)
            dve.sem_inc(s_acc, 4)
            def turn(it, last=False):
                win = load_steps(nc, dve, k.win, it, NW - 1)
                for h in range(2):
                    part = slice(h * HALF, (h + 1) * HALF)
                    dve.wait_ge(s_ready, it * U + (U + h * HALF))
                    dve.tensor_copy(cur_row[:, part], k.sidx[:, bass.ds(it * U + h * HALF, HALF)]).then_inc(s_rowcur, 1)
                    for u in range(h * HALF, (h + 1) * HALF):
                        if u % QUAD == 0 and not (last and u + QUAD >= U):
                            tables(it, u + QUAD)
                        if not (last and u + 2 >= U):
                            weigh(it, u + 2)
                        add(it, u, win[u])
                    dve.wait_ge(s_equal, it * U + (h + 1) * HALF)
                    dve.wait_ge(s_hot, it * U + (h + 1) * HALF)
                    refill(h, it * U + (U + h * HALF))

            tables(0, 0)
            weigh(0, 0)
            weigh(0, 1)
            with dve.Fori(0, IT - 1) as it:
                turn(it)
            turn(IT - 1, last=True)


def attend_close(nc, k, a):
    S = 4
    with ExitStack() as ctx:
        room = Arena(k.sims)
        wo = room.take([P, 2, D])
        w_sum = room.take([P, D])
        bo = room.take([1, D])
        sum_t = room.take([P, S, P])
        degree = room.take([P, S, P])
        index = room.take([P, S, 2], I32)
        quarter = room.take([P, 1])
        share = room.take([P, NW, HEADS])
        stats = room.take([P, S * 2 * 9])
        gates = room.take([P, S, D])
        sets = Arena(k.side)
        banks = sets.take([P, S * BANKS, EW])
        z = sets.take([P, S * 2, D])
        b_sum = sets.take([P, D])
        agg = sets.take([P, S, D])
        agg_t = room.take([P, S, D])
        part = sets.take([P, S, D])
        tps = [psum(nc, ctx, f"ac_t{i}", [P, 512]) for i in range(2)]
        ops = [psum(nc, ctx, f"ac_o{i}", [P, 512]) for i in range(2)]
        sps = [psum(nc, ctx, f"ac_s{i}", [P, 512]) for i in range(2)]
        pps = [psum(nc, ctx, f"ac_p{i}", [P, 512]) for i in range(2)]
        x = k.X.rearrange("p w d -> p (w d)")
        s_w, s_share, s_agg, s_turn, s_turned, s_out, s_part, s_mom1, s_mom2, s_root1, s_root2, s_inv1, s_inv2, s_two, \
            s_new, s_sent = sems(nc, k, *(f"ac_{n}" for n in (
                "w", "share", "agg", "turn", "turned", "out", "part", "mom1", "mom2", "root1", "root2", "inv1", "inv2",
                "two", "new", "sent")))
        s_count, s_index, s_diag, s_bturn, s_bturned, s_proj, s_term, s_tick = sems(
            nc, k, *(f"nt_{n}" for n in ("count", "index", "diag", "turn", "turned", "proj", "term", "tick")))
        s_gate = sems(nc, k, *(f"nt_gate{i}" for i in range(S)))
        s_bank = sems(nc, k, *(f"nt_bank{i}" for i in range(S)))
        block = ctx.enter_context(nc.Block())
        over = lambda engine, *stages: over_windows(engine, *stages, slots=S)
        turns = lambda w, slot, per: (w - slot) * (16 * per // S)
        moments = lambda slot, n: stats[:, (slot * 2 + n) * 9:(slot * 2 + n) * 9 + 9]

        @block.sync
        def _(sp):
            sp.dma_start(wo[:, :, :], a["wo_t"].rearrange("(c p) m -> p c m", p=P)).then_inc(s_w, 16)
            sp.dma_start(bo[:, :], a["L1_gnn_bo"]).then_inc(s_w, 16)
            sp.dma_start(w_sum, a["L2_gnn_W_sum"]).then_inc(s_w, 16)
            sp.dma_start(b_sum, a["L2_gnn_b_sum"].to_broadcast([P, D])).then_inc(s_w, 16)

            def load(w, slot, nodes):
                if not early(w, S):
                    sp.wait_ge(s_bturn, w - (S - 1))
                    sp.wait_ge(s_count, w - (S - 1))
                for b in range(BANKS):
                    sp.dma_start(banks[:, slot * BANKS + b, :], k.attr_sum[b][bass.ds(w * P, P), :]).then_inc(
                        s_bank[slot], 16)
                if not early(w, S):
                    sp.wait_ge(s_proj, w - (S - 1))
                sp.dma_start(gates[:, slot, :], k.node_gates[bass.ds(w * P, P), :]).then_inc(s_gate[slot], 16)

            def send(w, slot, nodes):
                sp.wait_ge(s_new, w + 1)
                sp.dma_start(k.x3_rows[bass.ds(w * P, P), :], x[:, node_window(w)]).then_inc(s_sent, 16)

            over(sp, (load, 0), (send, 4))
            sp.wait_ge(s_sent, 16 * NW)

        @block.gpsimd
        def _(pool):
            def fetch(w, slot, nodes):
                pool.wait_ge(s_index, w * 2 + 2)
                if not early(w, S):
                    pool.wait_ge(s_proj, w - (S - 1))
                pool.sem_inc(s_tick, 1)
                for n, table in enumerate((a["L2_gnn_z_in"], a["L2_gnn_z_out"])):
                    pool.indirect_dma_start(z[:, slot * 2 + n, :], None, table, bass.IndirectOffsetOnAxis(
                        ap=index[:, slot, n:n + 1], axis=0)).then_inc(k.s_z[slot], 16)

            over(pool, (fetch, 0))

        @block.tensor
        def _(pe):
            pe.wait_ge(s_w, 16 * 4)

            def turn(w, slot, nodes):
                pe.wait_ge(s_agg, w + 1)
                if not early(w, 2):
                    pe.wait_ge(s_turned, w - 1)
                for c in range(2):
                    ins = pe.transpose(tps[slot % 2][:, c * P:(c + 1) * P], agg[:, slot, c * P:(c + 1) * P], k.ident[:, :])
                ins.then_inc(s_turn, 1)

            def project(w, slot, nodes):
                pe.wait_ge(s_turned, w + 1)
                if not early(w, 2):
                    pe.wait_ge(s_part, (w - 2) * 2 + 1)
                for c in range(2):
                    pe.matmul(ops[slot % 2][:, 0:D], agg_t[:, slot, c * P:(c + 1) * P], wo[:, c, :], start=(c == 0), stop=False)
                pe.matmul(ops[slot % 2][:, 0:D], k.ones[0:1, :], bo[:, :], start=False, stop=True).then_inc(s_out, 1)

            def turn_banks(w, slot, nodes):
                pe.wait_ge(s_bank[slot], turns(w, slot, BANKS) + 16 * BANKS)
                if not early(w, 2):
                    pe.wait_ge(s_bturned, w - 1)
                for b in range(BANKS):
                    ins = pe.matmul(sps[slot % 2][:, 0:P], banks[:, slot * BANKS + b, 0:EA], k.ident[:, :],
                                    start=(b == 0), stop=(b == BANKS - 1))
                ins.then_inc(s_bturn, 1)

            def project_sums(w, slot, nodes):
                pe.wait_ge(s_bturned, w + 1)
                pe.wait_ge(s_diag, w + 1)
                pe.wait_ge(k.s_z[slot], turns(w, slot, 2) + 32)
                pe.wait_ge(s_gate[slot], turns(w, slot, 1) + 16)
                if not early(w, 2):
                    pe.wait_ge(s_term, w - 1)
                out = pps[slot % 2][:, 0:D]
                pe.matmul(out, sum_t[:, slot, :], w_sum[:, :], start=True, stop=False)
                pe.matmul(out, degree[:, slot, :], b_sum, start=False, stop=False)
                pe.matmul(out, k.ident[:, :], z[:, slot * 2, :], start=False, stop=False)
                pe.matmul(out, k.ident[:, :], z[:, slot * 2 + 1, :], start=False, stop=False)
                pe.matmul(out, k.ident[:, :], gates[:, slot, :], start=False, stop=True).then_inc(s_proj, 1)

            over(pe, (project_sums, 2), (project, 1), (turn, 0), (turn_banks, 0))

        @block.scalar
        def _(act):
            def copy_turned(w, slot, nodes):
                act.wait_ge(s_turn, w + 1)
                if not early(w, S):
                    act.wait_ge(s_out, w - (S - 1))
                act.copy(agg_t[:, slot, :], tps[slot % 2][:, 0:D]).then_inc(s_turned, 1)
                act.wait_ge(s_bturn, w + 1)
                if not early(w, S):
                    act.wait_ge(s_proj, w - (S - 1))
                act.copy(sum_t[:, slot, :], sps[slot % 2][:, 0:P]).then_inc(s_bturned, 1)

            def first_root(w, slot, nodes):
                act.wait_ge(s_mom1, w + 1)
                act.activation(moments(slot, 0)[:, 8:9], moments(slot, 0)[:, 7:8], ACT.Sqrt, bias=quarter[:, 0:1],
                               scale=0.25).then_inc(s_root1, 1)

            def second_root(w, slot, nodes):
                act.wait_ge(s_mom2, w + 1)
                act.activation(moments(slot, 1)[:, 8:9], moments(slot, 1)[:, 7:8], ACT.Sqrt,
                               bias=k.eps[:, 0:1]).then_inc(s_root2, 1)

            over(act, (second_root, 3), (first_root, 2), (copy_turned, 0))

        @block.vector
        def _(dve):
            dve.tensor_scalar(share[:, :, :], k.acc.rearrange("p (w d) -> p w d", d=AW)[:, :, D:], 0.5, None,
                              ALU.max).then_inc(s_share, 1)
            dve.tensor_scalar(quarter[:, :], k.eps[:, :], 0.25, None, ALU.mult).then_inc(s_share, 1)
            dve.wait_ge(s_share, 2)
            dve.reciprocal(share[:, :, :], share[:, :, :]).then_inc(s_share, 1)
            dve.wait_ge(s_share, 3)
            dve.wait_ge(s_w, 16 * 4)

            def count(w, slot, nodes):
                dve.wait_ge(s_bank[slot], turns(w, slot, BANKS) + 16 * BANKS)
                dve.sem_inc(k.s_hold, 1)
                dve.tensor_reduce(k.count_out[:, bass.ds(w, 1)], banks[:, slot * BANKS:(slot + 1) * BANKS, EA],
                                  AX.X, ALU.add).then_inc(s_count, 1)
                if not early(w, S):
                    dve.wait_ge(k.s_z[slot], turns(w, slot, 2))
                dve.tensor_scalar(index[:, slot, 0:1], k.count_in[:, bass.ds(w, 1)], float(DEGMAX), None,
                                  ALU.min).then_inc(s_index, 1)
                if not early(w, S):
                    dve.wait_ge(s_proj, w - (S - 1))
                dve.wait_ge(s_count, w + 1)
                dve.tensor_scalar(index[:, slot, 1:2], k.count_out[:, bass.ds(w, 1)], float(DEGMAX), None,
                                  ALU.min).then_inc(s_index, 1)
                dve.tensor_scalar(degree[:, slot, :], k.ident[:, :], k.count_out[:, bass.ds(w, 1)], None,
                                  ALU.mult).then_inc(s_diag, 1)

            def divide(w, slot, nodes):
                if not early(w, S):
                    dve.wait_ge(s_turn, w - (S - 1))
                shares = share.rearrange("p w h -> p (w h)")[:, bass.ds(w * HEADS, HEADS)]
                dve.tensor_tensor(agg[:, slot, :].rearrange("p (h d) -> p h d", h=HEADS),
                                  k.acc[:, sum_window(w)].rearrange("p (h d) -> p h d", h=HEADS),
                                  shares.unsqueeze(2).to_broadcast([P, HEADS, HD]), ALU.mult).then_inc(s_agg, 1)

            def add(w, slot, nodes):
                dve.wait_ge(s_out, w + 1)
                dve.tensor_tensor(part[:, slot, :], ops[slot % 2][:, 0:D], x[:, node_window(w)], ALU.add).then_inc(s_part, 1)
                dve.wait_ge(s_part, w * 2 + 1)
                row_moments(dve, k, part[:, slot, :], moments(slot, 0), s_part, w * 2 + 1).then_inc(s_mom1, 1)

            def second(w, slot, nodes):
                here, st = part[:, slot, :], moments(slot, 0)
                dve.wait_ge(s_root1, w + 1)
                dve.reciprocal(st[:, 8:9], st[:, 8:9]).then_inc(s_inv1, 1)
                dve.wait_ge(s_inv1, w + 1)
                dve.tensor_scalar(here, here, st[:, 6:7], st[:, 8:9], ALU.subtract, ALU.mult).then_inc(s_two, 1)
                dve.wait_ge(s_two, w * 2 + 1)
                dve.wait_ge(s_proj, w + 1)
                dve.tensor_tensor(here, here, pps[slot % 2][:, 0:D], ALU.add).then_inc(s_term, 1)
                dve.wait_ge(s_term, w + 1)
                row_moments(dve, k, here, moments(slot, 1), s_two, w * 2 + 1).then_inc(s_mom2, 1)

            def third(w, slot, nodes):
                st = moments(slot, 1)
                dve.wait_ge(s_root2, w + 1)
                dve.reciprocal(st[:, 8:9], st[:, 8:9]).then_inc(s_inv2, 1)
                dve.wait_ge(s_inv2, w + 1)
                dve.tensor_scalar(x[:, node_window(w)], part[:, slot, :], st[:, 6:7], st[:, 8:9], ALU.subtract,
                                  ALU.mult).then_inc(s_new, 1)

            over(dve, (third, 4), (second, 3), (add, 2), (divide, 0), (count, 0))


def scatter_features(nc, k):
    with ExitStack() as ctx:
        room = Arena(k.acc)
        equal = room.take([P, HALF, P], BF16)
        target = room.take([P, HALF, P], BF16)
        often = room.take([P, 4, P])
        ready = room.take([P, HALF, D])
        cur_own = room.take([P, U])
        cur_src = room.take([P, U])
        cur_dst = room.take([P, U])
        cur_row = room.take([P, U], I32)
        wps = [psum(nc, ctx, f"sf_w{i}", [P, 512]) for i in range(2)]
        wide = [psum(nc, ctx, f"sf_wide{i}", [P, 512]) for i in range(2)]
        sums = [psum(nc, ctx, f"sf_s{i}", [P, 512]) for i in range(4)]
        x = k.X.rearrange("p w d -> p (w d)")
        s_cur, s_rowcur, s_tables, s_w, s_often, s_mm, s_ready, s_tick, s_wide = sems(
            nc, k, *(f"sf_{n}" for n in ("cur", "rowcur", "tables", "w", "often", "mm", "ready", "tick", "wide")))
        s_sent, sent0 = k.s_sent, k.sent_before
        k.sent_before += 32 * IT
        block = ctx.enter_context(nc.Block())

        @block.vector
        def _(dve):
            def refill(h, at):
                part = slice(h * HALF, (h + 1) * HALF)
                dve.tensor_copy(cur_src[:, part], k.src[:, bass.ds(at, HALF)])
                dve.tensor_copy(cur_own[:, part], k.own[:, bass.ds(at, HALF)])
                dve.tensor_copy(cur_dst[:, part], k.dst[:, bass.ds(at, HALF)]).then_inc(s_cur, 1)

            for h in range(2):
                refill(h, h * HALF)
            dve.sem_inc(s_tables, 2 * U)
            with dve.Fori(0, IT) as it:
                for h in range(2):
                    part = slice(h * HALF, (h + 1) * HALF)
                    for v in range(HALF):
                        dve.wait_ge(s_sent[v], it * 32 + (sent0 - 16 + 16 * h))
                    dve.sem_inc(k.s_hold, 1)
                    dve.tensor_copy(cur_row[:, part], k.sidx[:, bass.ds(it * U + h * HALF, HALF)]).then_inc(s_rowcur, 1)
                    dve.wait_ge(s_cur, it * 2 + (h + 1))
                    for u in range(h * HALF, (h + 1) * HALF, QUAD):
                        slots, at = slice(u % HALF, u % HALF + QUAD), slice(u, u + QUAD)
                        dve.wait_ge(s_wide, it * U + (u + QUAD))
                        dve.wait_ge(s_w, it * U + (u + QUAD))
                        compare(dve, k, equal[:, slots, :], wide[u // QUAD % 2][:, :].rearrange("p (s e) -> p s e", s=QUAD),
                                cur_own[:, at]).then_inc(s_tables, QUAD)
                        compare(dve, k, target[:, slots, :], None, cur_dst[:, at]).then_inc(s_tables, QUAD)
                    dve.wait_ge(s_tables, it * 2 * U + (2 * U + (h + 1) * 2 * HALF))
                    refill(h, it * U + (U + h * HALF))

        @block.tensor
        def _(pe):
            pe.sem_inc(s_w, HALF)
            pe.sem_inc(s_mm, 4)

            def weights(it, u):
                pe.wait_ge(s_tables, it * 2 * U + (2 * U + 2 * (u // QUAD * QUAD + QUAD)))
                pe.wait_ge(s_often, it * U + (u + 1 + 2))
                pe.matmul(wps[u % 2][:, 0:P], target[:, u % HALF, :], equal[:, u % HALF, :], start=True, stop=True).then_inc(s_w, 1)

            def carried(it, u, win):
                pe.wait_ge(s_often, it * U + (4 + u + 1))
                pe.wait_ge(s_ready, it * U + (u + 1))
                pe.matmul(sums[u % 4][:, 0:D], often[:, u % 4, :], x[:, node_window(win)], start=True, stop=True).then_inc(s_mm, 1)

            def sources(it, u):
                if u % HALF == 0:
                    pe.wait_ge(s_cur, it * 2 + (1 + u // HALF))
                pe.wait_ge(s_tables, it * 2 * U + (2 * U + 2 * u - HALF))
                widen(pe, k, wide[u // QUAD % 2], cur_src[:, u % U:u % U + QUAD]).then_inc(s_wide, QUAD)

            sources(0, 0)
            sources(0, QUAD)
            with pe.Fori(0, IT) as it:
                win = load_steps(nc, pe, k.win, it, NW - 1)
                weights(it, 0)
                weights(it, 1)
                for u in range(U):
                    if u % QUAD == 0:
                        sources(it, u + HALF)
                    if u + 2 < U:
                        weights(it, u + 2)
                    carried(it, u, win[u])

        @block.scalar
        def _(act):
            act.sem_inc(s_often, 4)
            act.sem_inc(s_ready, 4)

            def copy_often(it, u):
                act.wait_ge(s_w, it * U + (HALF + u + 1))
                act.wait_ge(s_mm, it * U + (u + 1))
                act.copy(often[:, u % 4, :], wps[u % 2][:, 0:P]).then_inc(s_often, 1)

            def copy_sums(it, u):
                act.wait_ge(s_mm, it * U + (4 + u + 1))
                act.wait_ge(s_sent[u % HALF], it * 32 + (sent0 + 16 * (u // HALF)))
                act.copy(ready[:, u % HALF, :], sums[u % 4][:, 0:D]).then_inc(s_ready, 1)

            with act.Fori(0, IT) as it:
                copy_often(it, 0)
                copy_often(it, 1)
                for u in range(U):
                    if u + 2 < U:
                        copy_often(it, u + 2)
                    copy_sums(it, u)

        @block.gpsimd
        def _(pool):
            with pool.Fori(0, IT) as it:
                for u in range(U):
                    if u % HALF == 0:
                        pool.wait_ge(s_rowcur, it * 2 + (u // HALF + 1))
                    pool.wait_ge(s_ready, it * U + (4 + u + 1))
                    pool.wait_ge(s_sent[(u - BANKS) % HALF], it * 32 + (sent0 + 16 * (1 + (u - BANKS) // HALF)))
                    pool.sem_inc(s_tick, 1)
                    pool.indirect_dma_start(k.out_sum[u % BANKS], bass.IndirectOffsetOnAxis(ap=cur_row[:, u:u + 1], axis=0),
                                            ready[:, u % HALF, :], None, compute_op=ALU.add).then_inc(s_sent[u % HALF], 16)
            for v in range(HALF):
                pool.wait_ge(s_sent[v], sent0 + 32 * IT)


H3 = 3 * D


def gate_weights(k):
    w = Kit()
    room = Arena(k.sims)
    w.hidden = room.take([P, 2, H3])
    w.ways = room.take([P, 4, H3])
    w.ways_bias = room.take([P, 2, H3])
    w.share = room.take([P, 2, NW])
    w.met = room.take([P, 2, NW])
    return w


def fold_weights(nc, k, a):
    w = k.gate = gate_weights(k)
    with ExitStack() as ctx:
        room = Arena(k.side)
        w_ih = room.take([P, 4, H3])
        w_dir = room.take([P, 4, D])
        b_dir = room.take([P, 4])
        b_wide = room.take([P, 4, P])
        fps = [psum(nc, ctx, f"fw_{i}", [P, 2, 512]) for i in range(3)]
        s_w, s_wide, s_mm, s_read, s_share = sems(nc, k, "fw_w", "fw_wide", "fw_mm", "fw_read", "fw_share")
        block = ctx.enter_context(nc.Block())
        jobs = [(way, part) for way in range(2) for part in range(3)]

        @block.sync
        def _(sp):
            sp.dma_start(w_ih[:, :, :], a["w_ih_t"].rearrange("(c p) m -> p c m", p=P)).then_inc(s_w, 16)
            for n, name in enumerate(("in", "out")):
                sp.dma_start(w_dir[:, 2 * n:2 * n + 2, :],
                             a[f"L3_gnn_W_{name}"].rearrange("(c p) m -> p c m", p=P)).then_inc(s_w, 16)
                sp.dma_start(b_dir[:, 2 * n:2 * n + 2], a[f"L3_gnn_b_{name}"].rearrange("(c p) o -> p (c o)", p=P),
                             allow_slow_non_contiguous=True).then_inc(s_w, 16)
            sp.dma_start(w.hidden[:, :, :], a["w_hh_t"].rearrange("(c p) m -> p c m", p=P)).then_inc(s_w, 16)
            sp.wait_ge(s_w, 16 * 6)

        @block.tensor
        def _(pe):
            pe.wait_ge(s_w, 16 * 6)
            pe.wait_ge(s_wide, 4)
            for n, (way, part) in enumerate(jobs):
                if n >= 3:
                    pe.wait_ge(s_read, n - 2)
                for lo, hi in ((0, 2 * D), (2 * D, H3)):
                    for c in range(2):
                        left = b_wide[:, way * 2 + c, :] if part == 2 else w_dir[:, way * 2 + c, part * P:(part + 1) * P]
                        ins = pe.matmul(fps[n % 3][:, lo // (2 * D), 0:hi - lo], left, w_ih[:, way * 2 + c, lo:hi],
                                        start=(c == 0), stop=(c == 1))
                ins.then_inc(s_mm, 1)

        @block.scalar
        def _(act):
            for n, (way, part) in enumerate(jobs):
                act.wait_ge(s_mm, n + 1)
                to = w.ways_bias[:, way, :] if part == 2 else w.ways[:, way * 2 + part, :]
                act.copy(to, fps[n % 3][:, :, :].rearrange("p b d -> p (b d)")[:, 0:H3]).then_inc(s_read, 1)

        @block.vector
        def _(dve):
            dve.wait_ge(s_w, 16 * 6)
            for n in range(4):
                dve.tensor_scalar(b_wide[:, n, :], k.ones[:, :], b_dir[:, n:n + 1], None, ALU.mult).then_inc(s_wide, 1)
            for n, count in enumerate((k.count_in, k.count_out)):
                dve.tensor_scalar(w.met[:, n, :], count[:, :], 1.0, None, ALU.min)
                dve.tensor_scalar(w.share[:, n, :], count[:, :], 1.0, None, ALU.max).then_inc(s_share, 1)
            dve.wait_ge(s_share, 2)
            dve.reciprocal(w.share[:, :, :], w.share[:, :, :])


def gate_parts(nc, k, ctx, room):
    w = k.gate
    banks = room.take([P, BANKS, D])
    rows = room.take([P, 2, D])
    turned = room.take([P, 4 * P])
    gates = room.take([P, 4 * D])
    bias = room.take([P, 4 * D])
    bias_hh = room.take([P, 2 * D])
    tps = psum(nc, ctx, "gp_t", [P, 512])
    gps = psum(nc, ctx, "gp_g", [P, 2 * 512])
    x = k.X.rearrange("p w d -> p (w d)")
    s_b, s_bias, s_bank, s_add, s_rows, s_turn, s_turned, s_mm, s_gate, s_sent, s_out = sems(
        nc, k, *(f"gp_{n}" for n in ("b", "bias", "bank", "add", "rows", "turn", "turned", "mm", "gate", "sent", "out")))
    work = Kit()

    def sync(sp):
        sp.dma_start(bias[:, 0:H3], k.gate_bias[0].to_broadcast([P, H3])).then_inc(s_b, 16)
        sp.dma_start(bias[:, H3:], k.gate_bias[1][:, 2 * D:].to_broadcast([P, D])).then_inc(s_b, 16)
        sp.dma_start(bias_hh[:, :], k.gate_bias[1][:, 0:2 * D].to_broadcast([P, 2 * D])).then_inc(s_b, 16)
        def load(at):
            for b in range(BANKS):
                sp.dma_start(banks[:, b, :], k.out_sum[b][bass.ds(at * P, P), :]).then_inc(s_bank, 16)

        sp.sem_inc(s_sent, 1)
        load(0)
        with sp.Fori(0, NW) as it:
            sp.wait_ge(s_add, it * 3 + 6)
            load(it + 1)
            sp.wait_ge(s_gate, it * 3 + 6)
            sp.dma_start(k.gate_rows[bass.ds(it * P, P), :], gates).then_inc(s_out, 16)
            sp.wait_ge(s_out, it * 16 + 16)
            sp.sem_inc(s_sent, 1)
        sp.wait_ge(s_bank, 16 * BANKS * (NW + 1))

    def vector(dve):
        dve.wait_ge(s_b, 48)
        dve.tensor_tensor(bias[:, 0:2 * D], bias[:, 0:2 * D], bias_hh[:, :], ALU.add).then_inc(s_bias, 1)
        dve.sem_inc(s_add, 3)
        dve.sem_inc(s_gate, 3)
        dve.wait_ge(s_bias, 1)

        def step(it, u):
            if u == 1:
                dve.wait_ge(s_bank, it * (16 * BANKS) + 16 * BANKS)
                dve.wait_ge(s_turn, it + 1)
                dve.tensor_scalar(rows[:, 1, :], x[:, node_window(it)], 1.0, None, ALU.mult).then_inc(s_rows, 1)
                dve.tensor_tensor(banks[:, 0, :], banks[:, 0, :], banks[:, 1, :], ALU.add).then_inc(s_add, 1)
                dve.tensor_tensor(banks[:, 2, :], banks[:, 2, :], banks[:, 3, :], ALU.add).then_inc(s_add, 1)
            if u == 2:
                dve.wait_ge(s_add, it * 3 + 5)
                dve.tensor_tensor(rows[:, 0, :], banks[:, 0, :], banks[:, 2, :], ALU.add).then_inc(s_add, 1)
            if u == 3:
                dve.wait_ge(s_add, it * 3 + 6)
                dve.tensor_scalar(rows[:, 0, :], rows[:, 0, :], w.share[:, 1, bass.ds(it, 1)], None,
                                  ALU.mult).then_inc(s_rows, 1)
            if u == 13:
                dve.wait_ge(s_mm, it + 2)
                dve.wait_ge(s_sent, it + 1)
                dve.tensor_tensor(gates, gps[:, :], bias, ALU.add).then_inc(s_gate, 1)
            if u in (14, 15):
                way = u - 14
                dve.wait_ge(s_gate, it * 3 + (u - 10))
                dve.scalar_tensor_tensor(out=gates[:, 0:H3], in0=w.ways_bias[:, way, :],
                                         scalar=w.met[:, way, bass.ds(it, 1)], in1=gates[:, 0:H3], op0=ALU.mult,
                                         op1=ALU.add).then_inc(s_gate, 1)
        return step

    def tensor(pe):
        pe.sem_inc(s_turn, 1)
        pe.sem_inc(s_mm, 1)

        def step(it, u):
            if u == 7:
                pe.wait_ge(s_rows, it * 2 + 2)
                pe.wait_ge(s_turned, it + 1)
                for n in range(4):
                    ins = pe.transpose(tps[:, n * P:(n + 1) * P], rows[:, n // 2, (n % 2) * P:(n % 2 + 1) * P],
                                       k.ident[:, :])
                ins.then_inc(s_turn, 1)
            if u in (9, 10, 11, 12):
                c = u - 9
                pe.wait_ge(s_turned, it + 2)
                if c == 0:
                    pe.wait_ge(s_gate, it * 3 + 1)
                left = turned[:, c * P:(c + 1) * P]
                right = w.ways[:, 2 + c, :] if c < 2 else w.hidden[:, c - 2, :]
                pe.matmul(gps[:, 0:2 * D], left, right[:, 0:2 * D], start=(c == 0), stop=(c == 3))
                at = 2 * D if c < 2 else 3 * D
                ins = pe.matmul(gps[:, at:at + D], left, right[:, 2 * D:], start=(c % 2 == 0), stop=(c % 2 == 1))
                if c == 3:
                    ins.then_inc(s_mm, 1)
        return step

    def scalar(act):
        act.sem_inc(s_turned, 1)
        with act.Fori(0, NW) as it:
            act.wait_ge(s_turn, it + 2)
            act.wait_ge(s_mm, it + 1)
            act.copy(turned, tps[:, :]).then_inc(s_turned, 1)

    work.sync, work.vector, work.tensor, work.scalar = sync, vector, tensor, scalar
    return work


def gru_close(nc, k, a):
    w = k.gate
    S = 4
    GROUP = 4
    with ExitStack() as ctx:
        room = Arena(k.side)
        mean = room.take([P, S, D])
        mean_t = room.take([P, S, D])
        gates = room.take([P, S, 4 * D])
        part = room.take([P, S, D])
        stats = room.take([P, S * 6])
        moments_now = room.take([P, S * 2])
        moments = room.take([P, NW, 2])
        root = room.take([P, NW])
        tps = [psum(nc, ctx, f"gr_t{i}", [P, 512]) for i in range(2)]
        gps = [psum(nc, ctx, f"gr_g{i}", [P, 2 * 512]) for i in range(2)]
        x = k.X.rearrange("p w d -> p (w d)")
        s_mean, s_turn, s_turned, s_mm, s_ri, s_n, s_gate, s_cand, s_tanh, s_new, s_mom, s_kept, s_root, s_inv, s_done, \
            s_out = sems(nc, k, *(f"gr_{n}" for n in (
                "mean", "turn", "turned", "mm", "ri", "n", "gate", "cand", "tanh", "new", "mom", "kept", "root", "inv",
                "done", "out")))
        s_in = sems(nc, k, *(f"gr_in{i}" for i in range(S)))
        block = ctx.enter_context(nc.Block())
        over = lambda engine, *stages: over_windows(engine, *stages, slots=S)
        turns = lambda w_, slot: (w_ - slot) * (16 // S)

        @block.sync
        def _(sp):
            def load(w_, slot, nodes):
                if not early(w_, S):
                    sp.wait_ge(s_mom, w_ - (S - 1))
                sp.dma_start(gates[:, slot, :],
                             k.gate_rows[bass.ds(w_ * P, P), :]).then_inc(s_in[slot], 16)

            over(sp, (load, 0))
            for first in range(0, NW - 1, GROUP):
                sp.wait_ge(s_done, first + GROUP)
                sp.dma_start(a["out"][first * P:(first + GROUP) * P, :].rearrange("(w p) d -> p w d", p=P),
                             k.X[:, first:first + GROUP, :]).then_inc(s_out, 16)
            sp.wait_ge(s_done, NW)
            sp.dma_start(a["out"][(NW - 1) * P:N, :], k.X[0:TAIL, NW - 1, :]).then_inc(s_out, 16)
            sp.wait_ge(s_out, 16 * ((NW - 1) // GROUP + 1))

        @block.tensor
        def _(pe):
            def turn(w_, slot, nodes):
                pe.wait_ge(s_mean, w_ + 1)
                if not early(w_, 2):
                    pe.wait_ge(s_turned, w_ - 1)
                for c in range(2):
                    ins = pe.transpose(tps[slot % 2][:, c * P:(c + 1) * P], mean[:, slot, c * P:(c + 1) * P], k.ident[:, :])
                ins.then_inc(s_turn, 1)

            def products(w_, slot, nodes):
                pe.wait_ge(s_turned, w_ + 1)
                if not early(w_, 2):
                    pe.wait_ge(s_n, w_ - 1)
                for lo, hi in ((0, 2 * D), (2 * D, H3)):
                    for c in range(2):
                        ins = pe.matmul(gps[slot % 2][:, lo:hi], mean_t[:, slot, c * P:(c + 1) * P], w.ways[:, c, lo:hi],
                                        start=(c == 0), stop=(c == 1))
                ins.then_inc(s_mm, 1)

            over(pe, (products, 1), (turn, 0))

        @block.scalar
        def _(act):
            def copy_turned(w_, slot, nodes):
                act.wait_ge(s_turn, w_ + 1)
                if not early(w_, S):
                    act.wait_ge(s_mm, w_ - (S - 1))
                act.copy(mean_t[:, slot, :], tps[slot % 2][:, 0:D]).then_inc(s_turned, 1)

            def sigmoids(w_, slot, nodes):
                act.wait_ge(s_ri, w_ + 1)
                act.activation(gates[:, slot, 0:2 * D], gates[:, slot, 0:2 * D], ACT.Sigmoid).then_inc(s_gate, 1)

            def candidate(w_, slot, nodes):
                act.wait_ge(s_cand, w_ * 2 + 2)
                act.activation(gates[:, slot, 2 * D:H3], gates[:, slot, 2 * D:H3], ACT.Tanh).then_inc(s_tanh, 1)

            over(act, (candidate, 3), (sigmoids, 2), (copy_turned, 0))
            act.wait_ge(s_kept, NW)
            act.activation(root[:, :], moments[:, :, 1], ACT.Sqrt, bias=k.eps[:, 0:1]).then_inc(s_root, 1)

        @block.vector
        def _(dve):
            def means(w_, slot, nodes):
                if not early(w_, S):
                    dve.wait_ge(s_turn, w_ - (S - 1))
                dve.tensor_scalar(mean[:, slot, :], k.acc[:, sum_window(w_)], w.share[:, 0, bass.ds(w_, 1)], None,
                                  ALU.mult).then_inc(s_mean, 1)

            def sums(w_, slot, nodes):
                dve.wait_ge(s_in[slot], turns(w_, slot) + 16)
                dve.wait_ge(s_mm, w_ + 1)
                dve.tensor_tensor(gates[:, slot, 0:2 * D], gates[:, slot, 0:2 * D], gps[slot % 2][:, 0:2 * D],
                                  ALU.add).then_inc(s_ri, 1)
                dve.tensor_tensor(gates[:, slot, 2 * D:H3], gates[:, slot, 2 * D:H3], gps[slot % 2][:, 2 * D:H3],
                                  ALU.add).then_inc(s_n, 1)

            def candidate(w_, slot, nodes):
                cand, state_part = gates[:, slot, 2 * D:H3], gates[:, slot, H3:]
                dve.wait_ge(s_gate, w_ + 1)
                dve.wait_ge(s_n, w_ + 1)
                dve.tensor_tensor(state_part, gates[:, slot, 0:D], state_part, ALU.mult).then_inc(s_cand, 1)
                dve.wait_ge(s_cand, w_ * 2 + 1)
                dve.tensor_tensor(cand, cand, state_part, ALU.add).then_inc(s_cand, 1)

            def state(w_, slot, nodes):
                here = part[:, slot, :]
                old = x[:, node_window(w_)]
                dve.wait_ge(s_tanh, w_ + 1)
                dve.tensor_tensor(here, gates[:, slot, 2 * D:H3], old, ALU.subtract).then_inc(s_new, 1)
                dve.wait_ge(s_new, w_ * 4 + 1)
                dve.tensor_tensor(here, here, gates[:, slot, D:2 * D], ALU.mult).then_inc(s_new, 1)
                dve.wait_ge(s_new, w_ * 4 + 2)
                dve.scalar_tensor_tensor(out=old, in0=old, scalar=2.0, in1=here, op0=ALU.mult,
                                         op1=ALU.add).then_inc(s_new, 1)
                dve.wait_ge(s_new, w_ * 4 + 3)
                dve.sem_inc(k.s_hold, 1)
                dve.bn_stats(stats[:, slot * 6:slot * 6 + 6], old).then_inc(s_new, 1)
                dve.wait_ge(s_new, w_ * 4 + 4)
                dve.sem_inc(k.s_hold, 1)
                dve.bn_aggr(moments_now[:, slot * 2:slot * 2 + 2], stats[:, slot * 6:slot * 6 + 6]).then_inc(s_mom, 1)

            def keep_moments(w_, slot, nodes):
                dve.wait_ge(s_mom, w_ + 1)
                dve.tensor_scalar(moments[:, bass.ds(w_, 1), :].rearrange("p w m -> p (w m)"),
                                  moments_now[:, slot * 2:slot * 2 + 2], 1.0, None, ALU.mult).then_inc(s_kept, 1)

            over(dve, (means, 0), (state, 4), (sums, 2), (keep_moments, 4), (candidate, 3))
            dve.wait_ge(s_root, 1)
            dve.reciprocal(root[:, :], root[:, :]).then_inc(s_inv, 1)
            dve.wait_ge(s_inv, 1)
            for n in range(NW):
                dve.tensor_scalar(x[:, n * D:(n + 1) * D], x[:, n * D:(n + 1) * D], moments[:, n, 0:1], root[:, n:n + 1],
                                  ALU.subtract, ALU.mult).then_inc(s_done, 1)


def build(nc, k, a):
    with ExitStack() as ctx:
        k.ctx = ctx
        k.rows_before = 0
        k.sent_before = 16 * (1 + 2 * IT)
        dram = lambda name, shape, dt=F32: nc.dram_tensor(name, shape, dt)
        k.key_row = dram("key_row", [P + ROWS * P]).ap()
        k.kv_rows = dram("kv_rows", [NPAD, 2 * D]).ap()
        k.x3_rows = dram("x3_rows", [NPAD, D]).ap()
        k.node_gates = dram("node_gates", [NPAD, D]).ap()
        k.gate_rows = dram("gate_rows", [NPAD, 4 * D]).ap()
        k.v_edge = dram("v_edge", [STEPS * P, D]).ap()
        k.attr_sum = [dram(f"attr_sum{b}", [SUMROWS, EW]).ap() for b in range(BANKS)]
        k.out_sum = [dram(f"out_sum{b}", [SUMROWS, D]).ap() for b in range(BANKS)]
        k.xs = sbuf(nc, ctx, "xs", [P, NW, D])
        k.X = k.xs[:, :, :]
        k.big = sbuf(nc, ctx, "big", [P, NW * AW + NW * D])
        k.acc = k.big[:, 0:NW * AW]
        k.side = k.big[:, NW * AW:NW * AW + NW * D]
        k.sims = sbuf(nc, ctx, "sims", [P, STEPS * HEADS])[:, :]
        k.dst = sbuf(nc, ctx, "dst_tab", [P, ROWS])
        k.src = sbuf(nc, ctx, "src_tab", [P, ROWS])
        k.own = sbuf(nc, ctx, "own_tab", [P, ROWS])
        k.count_in = sbuf(nc, ctx, "count_in", [P, NW])
        k.count_out = sbuf(nc, ctx, "count_out", [P, NW])
        k.norm2 = k.sims[:, 0:2 * D]
        k.idx = sbuf(nc, ctx, "idx_tab", [P, ROWS], I32)
        k.sidx = sbuf(nc, ctx, "sidx_tab", [P, ROWS], I32)
        k.win = sbuf(nc, ctx, "win_row", [1, ROWS], I32)
        k.chunk = sbuf(nc, ctx, "chunk_row", [1, ROWS], I32)
        k.beyond = sbuf(nc, ctx, "beyond_row", [1, ROWS], I32)
        k.ident = sbuf(nc, ctx, "ident", [P, P])
        k.ones = sbuf(nc, ctx, "ones", [P, P])
        k.below = sbuf(nc, ctx, "below", [P, P])
        k.iota_row = sbuf(nc, ctx, "iota_row", [P, P])
        k.iota_col = sbuf(nc, ctx, "iota_col", [P, 1])
        k.eps = sbuf(nc, ctx, "eps", [P, 1])
        k.trash = sbuf(nc, ctx, "trash", [P, 1])
        k.stage_sems = []
        k.s_hold = nc.alloc_semaphore("s_hold")
        k.s_row = [nc.alloc_semaphore(f"s_row{u}") for u in range(U)]
        k.gate_bias = (a["L3_gnn_b_ih"], a["L3_gnn_b_hh"])
        k.s_z = [nc.alloc_semaphore(f"s_z{i}") for i in range(4)]
        k.s_sent = [nc.alloc_semaphore(f"s_sent{v}") for v in range(HALF)]
        step_tables(nc, k, a["dst"], a["src"], a["x"])
        end_stage(nc, k)
        gather_sums(nc, k, "l0", a["x"], True)
        end_stage(nc, k)
        gin_mlp(nc, k, a)
        end_stage(nc, k)
        gin_close_and_project(nc, k, a)
        end_stage(nc, k)
        edge_scores(nc, k)
        end_stage(nc, k)
        softmax_weights(nc, k)
        end_stage(nc, k)
        weighted_sums(nc, k, a["attr"])
        end_stage(nc, k)
        attend_close(nc, k, a)
        end_stage(nc, k)
        scatter_features(nc, k)
        end_stage(nc, k)
        fold_weights(nc, k, a)
        end_stage(nc, k)
        gather_sums(nc, k, "l3", k.x3_rows, False, beside=gate_parts)
        end_stage(nc, k)
        gru_close(nc, k, a)
        end_stage(nc, k)




def padded(rows, shape, fill):
    out = np.full(shape, fill, rows.dtype)
    out.reshape((-1,) + rows.shape[1:])[:rows.shape[0]] = rows
    return out


def kernel(**inputs):
    import concourse.bacc as bacc
    from concourse.bass_utils import run_bass_kernel_spmd

    host = {n: np.ascontiguousarray(v) for n, v in inputs.items()}
    lay = {
        "x": padded(host["x"], (NPAD, D), 0),
        "dst": padded(host["dst"], (NC, P), PAD_DST),
        "src": padded(host["src"], (NC, P), 0),
        "attr": padded(host["edge_attr_128"], ((NC + QUAD) * P, EA), 0),
    }
    for name in ("L0_gnn_W1", "L0_gnn_W2"):
        lay[name] = host[name]
    for name in ("b1", "g1", "bt1", "b2", "g2", "bt2", "eps_gin"):
        lay[f"L0_gnn_{name}"] = host[f"L0_gnn_{name}"].reshape(1, -1)
    for name in "qkvo":
        lay[f"w{name}_t"] = np.ascontiguousarray(host[f"L1_gnn_W{name}"].T)
        lay[f"L1_gnn_b{name}"] = host[f"L1_gnn_b{name}"].reshape(1, -1)
    for name in ("z_in", "z_out", "W_cent", "W_vor", "W_sum"):
        lay[f"L2_gnn_{name}"] = host[f"L2_gnn_{name}"]
    for name in ("L2_gnn_b_cent", "L2_gnn_b_vor", "L2_gnn_b_sum", "L3_gnn_b_ih", "L3_gnn_b_hh"):
        lay[name] = host[name].reshape(1, -1)
    for name in ("in", "out"):
        lay[f"L3_gnn_W_{name}"] = host[f"L3_gnn_W_{name}"]
        lay[f"L3_gnn_b_{name}"] = host[f"L3_gnn_b_{name}"].reshape(-1, 1)
    for name in ("ih", "hh"):
        lay[f"w_{name}_t"] = np.ascontiguousarray(host[f"L3_gnn_W_{name}"].T)
    for name in ("node_vec1", "node_vec1_n2"):
        lay[name] = np.ascontiguousarray(padded(host[name], (NPAD, 1), 0).reshape(NW, P).T)
    nc = bacc.Bacc("TRN2", target_bir_lowering=False, num_devices=1)
    arrays, handles = {}, {}
    for name, array in lay.items():
        arrays[f"in_{name}"] = array
        handles[name] = nc.dram_tensor(f"in_{name}", array.shape, mybir.dt.from_np(array.dtype), kind="ExternalInput").ap()
    handles["out"] = nc.dram_tensor("out", (N, D), F32, kind="ExternalOutput").ap()
    build(nc, Kit(), handles)
    return run_bass_kernel_spmd(nc, [arrays], core_ids=[0]).results[0]["out"]
```

```python
import numpy as np
import concourse.bass as bass
from concourse import mybir
from contextlib import ExitStack

F32 = mybir.dt.float32
BF16 = mybir.dt.bfloat16
I32 = mybir.dt.int32
ALU = mybir.AluOpType
ACT = mybir.ActivationFunctionType
AX = mybir.AxisListType

P = 128
N, D, E, EA = 6250, 256, 106250, 128
HID = 2 * D
HEADS, HD = 8, 32
SCALE = 1.0 / float(np.sqrt(HD))
EPS = 1e-5
NW = -(-N // P)
NPAD = NW * P
TAIL = N - (NW - 1) * P
NC = -(-E // P) + 1
U = 16
IT = -(-(NC - 1 + NW - 1) // U)
STEPS = IT * U
ROWS = -(-STEPS // P) * P
RT = ROWS // P
HALF = U // 2
QUAD = 4
AW = D + HEADS
GROUPS = P // HEADS
GS = STEPS // GROUPS
SCAN = GS * P
PAD_DST = 1 << 20
BIG = 1e30
LOW = -1e37
PLACES = 4
KEY = 2.0 ** 110
BANKS = 4
SUMROWS = NPAD + P
EW = EA + 1
DEGMAX = 511

assert (NW - 1) % PLACES == 0
assert STEPS % GROUPS == 0 and STEPS >= NC - 1 + NW - 1


class Kit:
    pass


def sbuf(nc, ctx, name, shape, dt=F32):
    return ctx.enter_context(nc.sbuf_tensor(name, shape, dt))


class Arena:

    def __init__(self, region):
        self.region, self.at = region, 0

    def take(self, shape, dt=F32):
        words = int(np.prod(shape[1:])) * (2 if dt == BF16 else 4)
        words = -(-words // 4)
        part = self.region[0:shape[0], self.at:self.at + words]
        self.at += words
        assert self.at <= self.region.shape[1], (self.at, self.region.shape)
        if dt != F32:
            part = part.bitcast(dt)
        if len(shape) == 3:
            part = part.rearrange("p (a b) -> p a b", a=shape[1])
        return part


def psum(nc, ctx, name, shape, dt=F32):
    return ctx.enter_context(nc.psum_tensor(name, shape, dt))


def sems(nc, k, *names):
    new = [nc.alloc_semaphore(n) for n in names]
    k.stage_sems += new
    return new


def end_stage(nc, k):
    nc.clear_and_free_semaphores(k.stage_sems)
    k.stage_sems = []
    nc.all_engine_barrier()


def load_steps(nc, engine, row, it, top):
    return nc.values_load_multi_w_load_instructions(
        row[0:1, bass.ds(it * U, U)], engines=[engine.engine], min_val=0, max_val=top,
        skip_runtime_bounds_check_because="step_tables clamps the entries")[1]


def compare(dve, k, out, rows, columns):
    if rows is None:
        rows = k.iota_row[:, :].unsqueeze(1).to_broadcast([P, QUAD, P])
    return dve.tensor_tensor(out, rows, columns.unsqueeze(2).to_broadcast([P, QUAD, P]), ALU.is_equal)


def widen(pe, k, wide, columns):
    for j in range(QUAD):
        ins = pe.transpose(wide[:, j * P:(j + 1) * P], columns[:, j:j + 1].to_broadcast([P, P]), k.ident[:, :])
    return ins


def step_tables(nc, k, dst_rows, src_rows, x_rows):
    with ExitStack() as ctx:
        room = Arena(k.big[:, :])
        last_i = room.take([1, NC], I32)
        last_f = room.take([1, NC])
        limit = room.take([NW - 1, 1])
        wnum = room.take([NW - 1, 1])
        ahead = room.take([NW - 1, NC])
        count = room.take([NW - 1, 1])
        ends = room.take([NW - 1, 1])
        step_no = room.take([NW - 1, ROWS])
        ended = room.take([NW - 1, ROWS])
        step_col = room.take([P, RT])
        win_col = room.take([P, RT])
        base_col = room.take([P, RT])
        chunk_f = room.take([P, RT])
        chunk_i = room.take([P, RT], I32)
        crow_f = room.take([1, ROWS])
        dst_i = room.take([P, RT, P], I32)
        src_i = room.take([P, RT, P], I32)
        dst_f = room.take([P, RT, P])
        src_f = room.take([P, RT, P])
        key_f = room.take([P, RT, P])
        flag = room.take([P, ROWS])
        low_key = room.take([1, 1])
        last_ps = psum(nc, ctx, "last_ps", [NW - 1, 2, 512])
        wrow_ps = psum(nc, ctx, "wrow_ps", [1, 2, 512])
        wcol_ps = psum(nc, ctx, "wcol_ps", [P, RT])
        turn_ps = [psum(nc, ctx, f"turn_ps{i}", [P, P]) for i in range(2)]
        (s_last, s_x, s_const, s_ident, s_lastf, s_lastb, s_ended, s_wps, s_chunk, s_gat, s_rel, s_rows,
         s_turn, s_tab, s_dve) = sems(
            nc, k, "t_last", "t_x", "t_const", "t_ident", "t_lastf", "t_lastb", "t_ended", "t_wps",
            "t_chunk", "t_gat", "t_rel", "t_rows", "t_turn", "t_tab", "t_dve")
        HB, HR = NC // 2, ROWS // 2
        block = ctx.enter_context(nc.Block())

        @block.sync
        def _(sp):
            sp.dma_start(last_i[:, :], dst_rows[:, P - 1:P].rearrange("c o -> o c"),
                         allow_slow_non_contiguous=True).then_inc(s_last, 16)
            sp.dma_start(k.X, x_rows.rearrange("(w p) d -> p w d", p=P)).then_inc(s_x, 16)
            sp.wait_ge(s_rel, 3 * RT)
            sp.dma_start(k.key_row[P:].rearrange("(t p e) -> p t e", p=P, e=P), key_f[:, :, :]).then_inc(s_rows, 16)
            sp.dma_start(k.key_row[P - 1:P].rearrange("(a b) -> a b", a=1), low_key[:, :]).then_inc(s_rows, 16)
            sp.wait_ge(s_rows, 32)
            sp.wait_ge(s_x, 16)

        @block.gpsimd
        def _(pool):
            iota = lambda out, pattern, base, mult: pool.iota(
                out, pattern, base=base, channel_multiplier=mult, allow_small_or_imprecise_dtypes=True)
            pool.memset(k.ident[:, :], 0.0).then_inc(s_ident, 1)
            pool.memset(k.ones[:, :], 1.0).then_inc(s_const, 1)
            pool.memset(k.eps[:, :], EPS)
            pool.memset(low_key[:, :], -5.0 * KEY).then_inc(s_const, 1)
            iota(limit[:, :], [[0, 1]], P, P).then_inc(s_const, 1)
            iota(wnum[:, :], [[0, 1]], 0, 1).then_inc(s_const, 1)
            iota(step_no[:, :], [[1, ROWS]], 0, 0).then_inc(s_const, 1)
            iota(step_col[:, :], [[P, RT]], 0, 1).then_inc(s_const, 1)
            iota(k.iota_row[:, :], [[1, P]], 0, 0).then_inc(s_const, 1)
            iota(k.iota_col[:, :], [[0, 1]], 0, 1).then_inc(s_const, 1)
            iota(k.trash[:, :], [[0, 1]], NPAD, 1).then_inc(s_const, 1)
            pool.wait_ge(s_ident, 1)
            pool.affine_select(out=k.ident[:, :], in_=k.ident[:, :], compare_op=ALU.not_equal, fill=1.0, base=0,
                               pattern=[[-1, P]], channel_multiplier=1).then_inc(s_ident, 1)
            pool.wait_ge(s_const, 1)
            pool.affine_select(out=k.below[:, :], in_=k.ones[:, :], compare_op=ALU.is_gt, fill=0.0, base=0,
                               pattern=[[-1, P]], channel_multiplier=1).then_inc(s_const, 1)
            pool.wait_ge(s_chunk, 1)
            for t in range(RT):
                for table, rows in ((dst_i, dst_rows), (src_i, src_rows)):
                    pool.indirect_dma_start(table[:, t, :], None, rows,
                                            bass.IndirectOffsetOnAxis(ap=chunk_i[:, t:t + 1], axis=0)).then_inc(s_gat, 16)
            pool.wait_ge(s_gat, 32 * RT)

        @block.tensor
        def _(pe):
            pe.wait_ge(s_const, 10)
            pe.wait_ge(s_lastf, 1)
            for h in range(2):
                pe.matmul(last_ps[:, h, 0:HB], k.ones[0:1, 0:NW - 1], last_f[:, h * HB:(h + 1) * HB],
                          start=True, stop=True).then_inc(s_lastb, 1)
            pe.wait_ge(s_ended, 1)
            for h in range(2):
                pe.matmul(wrow_ps[:, h, 0:HR], k.ones[0:NW - 1, 0:1], ended[:, h * HR:(h + 1) * HR],
                          start=True, stop=True).then_inc(s_wps, 1)
            for t in range(RT):
                pe.matmul(wcol_ps[:, t:t + 1], ended[:, t * P:(t + 1) * P], k.ones[0:NW - 1, 0:1],
                          start=True, stop=True).then_inc(s_wps, 1)
            pe.wait_ge(s_ident, 2)
            for t in range(RT):
                for n, rows in enumerate((dst_f, src_f)):
                    pe.wait_ge(s_rel, 3 * t + 1 + n)
                    if t:
                        pe.wait_ge(s_tab, 2 * t - 1 + n)
                    pe.transpose(turn_ps[n][:, :], rows[:, t, :], k.ident[:, :]).then_inc(s_turn, 1)

        @block.vector
        def _(dve):
            dve.wait_ge(s_last, 16)
            dve.tensor_copy(last_f[:, :], last_i[:, :]).then_inc(s_lastf, 1)
            dve.wait_ge(s_lastb, 2)
            dve.wait_ge(s_const, 10)
            dve.tensor_scalar(ahead[:, :].rearrange("w (h c) -> w h c", h=2), last_ps[:, :, 0:HB], limit[:, 0:1], None,
                              ALU.is_lt).then_inc(s_dve, 1)
            dve.wait_ge(s_dve, 1)
            dve.tensor_reduce(count[:, :], ahead[:, :], AX.X, ALU.add).then_inc(s_dve, 1)
            dve.wait_ge(s_dve, 2)
            dve.tensor_tensor(ends[:, :], count[:, :], wnum[:, :], ALU.add).then_inc(s_dve, 1)
            dve.wait_ge(s_dve, 3)
            dve.tensor_scalar(ended[:, :], step_no[:, :], ends[:, 0:1], None, ALU.is_gt).then_inc(s_ended, 1)
            dve.wait_ge(s_wps, 2 + RT)
            dve.tensor_copy(win_col[:, :], wcol_ps[:, :]).then_inc(s_dve, 1)
            dve.tensor_copy(k.win[:, :].rearrange("o (h c) -> o h c", h=2), wrow_ps[:, :, 0:HR]).then_inc(s_dve, 1)
            dve.tensor_tensor(crow_f[:, :].rearrange("o (h c) -> o h c", h=2),
                              step_no[0:1, :].rearrange("o (h c) -> o h c", h=2), wrow_ps[:, :, 0:HR],
                              ALU.subtract).then_inc(s_dve, 1)
            dve.wait_ge(s_dve, 4)
            dve.tensor_scalar(base_col[:, :], win_col[:, :], float(P), None, ALU.mult).then_inc(s_dve, 1)
            dve.tensor_tensor(chunk_f[:, :], step_col[:, :], win_col[:, :], ALU.subtract).then_inc(s_dve, 1)
            dve.wait_ge(s_dve, 8)
            dve.tensor_scalar(chunk_i[:, :], chunk_f[:, :], float(NC - 1), None, ALU.min).then_inc(s_chunk, 1)
            dve.tensor_scalar(k.chunk[:, :], crow_f[:, :], float(NC - 1), None, ALU.min).then_inc(s_dve, 1)
            dve.wait_ge(s_dve, 9)
            by_quad = k.chunk[:, :].rearrange("o (h u) -> o h u", u=QUAD)
            dve.tensor_tensor(k.beyond[:, :].rearrange("o (h u) -> o h u", u=QUAD), by_quad,
                              by_quad[:, :, 0:1].to_broadcast([1, ROWS // QUAD, QUAD]), ALU.subtract)
            dve.wait_ge(s_gat, 32 * RT)
            for t in range(RT):
                dve.tensor_scalar(dst_f[:, t, :], dst_i[:, t, :], base_col[:, t:t + 1], None,
                                  ALU.subtract).then_inc(s_rel, 1)
                dve.tensor_copy(src_f[:, t, :], src_i[:, t, :]).then_inc(s_rel, 1)
                dve.wait_ge(s_rel, 3 * t + 1)
                dve.tensor_scalar(key_f[:, t, :], dst_f[:, t, :], -0.5, P - 0.5, ALU.max, ALU.min).then_inc(s_dve, 1)
                dve.wait_ge(s_dve, 10 + t)
                dve.tensor_scalar(key_f[:, t, :], key_f[:, t, :], base_col[:, t:t + 1], KEY,
                                  ALU.add, ALU.mult).then_inc(s_rel, 1)
            for t in range(RT):
                dve.wait_ge(s_turn, 2 * t + 1)
                dve.tensor_copy(k.dst[:, t * P:(t + 1) * P], turn_ps[0][:, :]).then_inc(s_tab, 1)
                dve.wait_ge(s_turn, 2 * t + 2)
                dve.tensor_copy(k.src[:, t * P:(t + 1) * P], turn_ps[1][:, :]).then_inc(s_tab, 1)
            dve.wait_ge(s_tab, 2 * RT)
            dve.tensor_scalar(flag, k.dst[:, :], 0.0, None, ALU.is_ge).then_inc(s_dve, 1)
            dve.wait_ge(s_dve, 10 + RT)
            dve.scalar_tensor_tensor(out=flag, in0=k.dst[:, :], scalar=float(P), in1=flag,
                                     op0=ALU.is_lt, op1=ALU.mult).then_inc(s_dve, 1)
            dve.tensor_copy(k.idx[:, :], k.src[:, :]).then_inc(s_dve, 1)
            dve.wait_ge(s_dve, 12 + RT)
            dve.scalar_tensor_tensor(out=k.own[:, :], in0=k.src[:, :], scalar=1.0, in1=flag, op0=ALU.add,
                                     op1=ALU.mult).then_inc(s_dve, 1)
            dve.wait_ge(s_dve, 13 + RT)
            dve.tensor_scalar(k.own[:, :], k.own[:, :], -1.0, None, ALU.add).then_inc(s_dve, 1)


def gather_sums(nc, k, tag, table, first, beside=None):
    def turns(engine, one, work=None):
        if beside is None:
            with engine.Fori(0, IT) as it:
                one(it, lambda u: None)
        else:
            with engine.Fori(0, NW) as it:
                one(it, lambda u: work(it, u))
            with engine.Fori(NW, IT) as it:
                one(it, lambda u: None)

    width = D + 1 if first else D
    with ExitStack() as ctx:
        room = Arena(k.side)
        ring = room.take([P, U, D + 1])
        onehot = room.take([P, HALF, P])
        cur_idx = room.take([P, U], I32)
        cur_src = room.take([P, U])
        same = room.take([P, P], BF16)
        before = room.take([P, U])
        repeats = room.take([P, STEPS]) if first else None
        away = room.take([P, STEPS]) if first else None
        sums = [psum(nc, ctx, f"{tag}_sums{i}", [P, 512]) for i in range(4)]
        s_zero, s_cur, s_tick, s_hot, s_sum, s_acc, s_seen, s_idx = sems(
            nc, k, *(f"{tag}_{n}" for n in ("zero", "cur", "tick", "hot", "sum", "acc", "seen", "idx")))
        wide = [psum(nc, ctx, f"{tag}_wide{i}", [P, 512]) for i in range(2)] if first else None
        s_wide, s_src = sems(nc, k, f"{tag}_wide", f"{tag}_src")
        s_row, row0 = k.s_row, k.rows_before
        k.rows_before += 16 * IT
        work = beside(nc, k, ctx, room) if beside else Kit()
        block = ctx.enter_context(nc.Block())

        @block.gpsimd
        def _(pool):
            with pool.Fori(0, IT) as it:
                for u in range(U):
                    if u % QUAD == 0:
                        pool.wait_ge(s_cur, it * (U // QUAD) + (1 + u // QUAD))
                    pool.wait_ge(s_sum, it * U + (u + 1))
                    pool.sem_inc(s_tick, 1)
                    pool.indirect_dma_start(ring[:, u, 0:D], None, table, bass.IndirectOffsetOnAxis(
                        ap=cur_idx[:, u:u + 1], axis=0)).then_inc(s_row[u], 16)

        if beside:
            @block.sync
            def _(sp):
                work.sync(sp)

            @block.scalar
            def _(act):
                work.scalar(act)

        @block.tensor
        def _(pe):
            def sources(it, u):
                if u % HALF == 0:
                    pe.wait_ge(s_src, it * 2 + (1 + u // HALF))
                pe.wait_ge(s_seen, it * U + (u + U - QUAD))
                widen(pe, k, wide[u // QUAD % 2], cur_src[:, u % U:u % U + QUAD]).then_inc(s_wide, QUAD)

            def one(it, beside_step):
                for u in range(U):
                    if first and u % QUAD == 0:
                        sources(it, u + QUAD)
                    pe.wait_ge(s_row[u], it * 16 + (row0 + 16))
                    pe.wait_ge(s_hot, it * U + (u + 1))
                    pe.wait_ge(s_acc, it * U + (u + 1))
                    pe.matmul(sums[u % 4][:, 0:width], onehot[:, u % HALF, :], ring[:, u, 0:width],
                              start=True, stop=True).then_inc(s_sum, 1)
                    beside_step(u)

            pe.sem_inc(s_sum, U)
            if first:
                sources(0, 0)
            turns(pe, one, work.tensor(pe) if beside else None)

        @block.vector
        def _(dve):
            def refill(q, at):
                part = slice(q * QUAD, (q + 1) * QUAD)
                dve.tensor_copy(cur_idx[:, part], k.idx[:, bass.ds(at, QUAD)]).then_inc(s_cur, 1)

            def refill_sources(h, at):
                part = slice(h * HALF, (h + 1) * HALF)
                dve.tensor_copy(cur_src[:, part], k.src[:, bass.ds(at, HALF)]).then_inc(s_src, 1)

            hot_ahead = HALF if beside else QUAD

            def hot(it, u):
                dve.wait_ge(s_sum, it * U + (u + QUAD + U - HALF))
                compare(dve, k, onehot[:, u % HALF:u % HALF + QUAD, :], None,
                        k.dst[:, bass.ds(it * U + u, QUAD)]).then_inc(s_hot, QUAD)

            def add(it, u, win):
                dve.wait_ge(s_sum, it * U + (u + 1 + U))
                dve.wait_ge(s_acc, it * U + (u + 4))
                here = k.acc[:, bass.ds(win * AW, width)]
                dve.tensor_tensor(here, sums[u % 4][:, 0:width], here, ALU.add).then_inc(s_acc, 1)

            def earlier(it, u):
                if u % HALF == 0:
                    dve.wait_ge(s_src, it * 2 + (1 + u // HALF))
                if u % QUAD == 0:
                    dve.wait_ge(s_wide, it * U + (u + QUAD))
                dve.wait_ge(s_seen, it * U + (U + u))
                row = wide[u // QUAD % 2][:, u % QUAD * P:(u % QUAD + 1) * P]
                dve.scalar_tensor_tensor(out=same[:, :], in0=row, scalar=cur_src[:, u:u + 1],
                                         in1=k.below[:, :], op0=ALU.is_equal, op1=ALU.mult,
                                         accum_out=before[:, u:u + 1]).then_inc(s_seen, 1)

            def keep_repeats(it, h):
                dve.wait_ge(s_seen, it * U + (U + (h + 1) * HALF))
                dve.tensor_copy(repeats[:, bass.ds(it * U + h * HALF, HALF)], before[:, h * HALF:(h + 1) * HALF])

            def scatter_rows():
                src = k.src[:, 0:STEPS]
                dve.tensor_scalar(away, src, -1.0, k.trash[:, 0:1], ALU.mult, ALU.add).then_inc(s_idx, 1)
                dve.wait_ge(s_idx, 1)
                dve.scalar_tensor_tensor(out=away, in0=repeats, scalar=0.0, in1=away, op0=ALU.is_gt,
                                         op1=ALU.mult).then_inc(s_idx, 1)
                dve.wait_ge(s_idx, 2)
                dve.tensor_tensor(k.sidx[:, 0:STEPS], away, src, ALU.add).then_inc(s_idx, 1)
                dve.wait_ge(s_idx, 3)

            dve.memset(k.acc[:, :], 0.0)
            if first:
                dve.memset(ring[:, :, D:D + 1], 1.0).then_inc(s_zero, 1)
                dve.wait_ge(s_zero, 1)
                dve.sem_inc(s_seen, U)
            def one(it, beside_step):
                win = load_steps(nc, dve, k.win, it, NW - 1)
                for h in range(2):
                    for u in range(h * HALF, (h + 1) * HALF):
                        if u % QUAD == (2 if beside else 0):
                            hot(it, u - u % QUAD + hot_ahead)
                        if first:
                            earlier(it, u)
                        add(it, u, win[u])
                        if u % QUAD == QUAD - 1:
                            refill(u // QUAD, it * U + (u + 1 - QUAD + U))
                        beside_step(u)
                    if first:
                        keep_repeats(it, h)
                        refill_sources(h, it * U + (U + h * HALF))

            for q in range(U // QUAD):
                refill(q, q * QUAD)
            if first:
                for h in range(2):
                    refill_sources(h, h * HALF)
            dve.sem_inc(s_acc, 4)
            for u in range(0, hot_ahead, QUAD):
                hot(0, u)
            turns(dve, one, work.vector(dve) if beside else None)
            if first:
                scatter_rows()


def node_window(w):
    return bass.ds(w * D, D)


def sum_window(w, width=D):
    return bass.ds(w * AW, width)


def over_windows(engine, *stages, slots=2):
    lead = -(-(slots + max(lag for _, lag in stages)) // PLACES) * PLACES

    def place(n):
        for function, lag in stages:
            if 0 <= n - lag < NW:
                function(n - lag, (n - lag) % slots, TAIL if n - lag == NW - 1 else P)

    for n in range(lead):
        place(n)
    with engine.Fori(0, (NW - 1 - lead) // PLACES) as turn:
        for part in range(PLACES):
            for function, lag in stages:
                function(turn * PLACES + (lead + part - lag), (part - lag) % slots, P)
    for n in range(NW - 1, NW + max(lag for _, lag in stages)):
        place(n)


def early(w, n):
    return isinstance(w, int) and w < n


def row_moments(dve, k, x, stats, chain, base):
    dve.bn_stats(stats[:, 0:6], x).then_inc(chain, 1)
    dve.wait_ge(chain, base + 1)
    dve.sem_inc(k.s_hold, 1)
    return dve.bn_aggr(stats[:, 6:8], stats[:, 0:6])


def gin_front(nc, k, g, tag, t_free):
    s_z, s_zps, s_zt, s_t = sems(nc, k, *(f"{tag}_{n}" for n in ("z", "zps", "zt", "t")))
    x = k.X.rearrange("p w d -> p (w d)")

    def combine(dve):
        def stage(w, slot, nodes):
            dve.wait_ge(s_zps, w + 1)
            dve.scalar_tensor_tensor(out=g.z[:, slot, :], in0=x[:, node_window(w)], scalar=g.eps1[:, 0:1],
                                     in1=k.acc[:, sum_window(w)], op0=ALU.mult, op1=ALU.add).then_inc(s_z, 1)
        return stage

    def turn(pe):
        pe.sem_inc(s_zps, 2)
        pe.sem_inc(s_t, 2)

        def stage(w, slot, nodes):
            pe.wait_ge(s_z, w + 1)
            pe.wait_ge(s_zt, w + 1)
            for c in range(2):
                ins = pe.transpose(g.zps[slot][:, c * P:(c + 1) * P], g.z[:, slot, c * P:(c + 1) * P], k.ident[:, :])
            ins.then_inc(s_zps, 1)
        return stage

    def copy_turned(act):
        act.sem_inc(s_zt, 2)

        def stage(w, slot, nodes):
            act.wait_ge(s_zps, w + 3)
            act.wait_ge(s_t, w + 1)
            act.copy(g.zt[:, slot, :], g.zps[slot][:, 0:D]).then_inc(s_zt, 1)
        return stage

    def hidden(pe):
        def stage(w, slot, nodes):
            pe.wait_ge(s_zt, w + 3)
            pe.wait_ge(t_free, w + 1)
            for m in range(4):
                for c in range(2):
                    ins = pe.matmul(g.tps[slot][:, m * P:(m + 1) * P], g.w1[:, c, m * P:(m + 1) * P],
                                    g.zt[:, slot, c * P:(c + 1) * P], start=(c == 0), stop=(c == 1))
            ins.then_inc(s_t, 1)
        return stage

    return combine, turn, copy_turned, hidden, s_t


def gin_mlp(nc, k, a):
    with ExitStack() as ctx:
        g = Kit()
        room = Arena(k.side)
        g.w1 = room.take([P, 2, HID])
        w2 = room.take([P, 4, D])
        b2 = room.take([P, D])
        cols = room.take([P, 3, 4])
        g2 = room.take([1, D])
        bt2 = room.take([1, D])
        g.eps1 = room.take([P, 1])
        g.z = room.take([P, 2, D])
        g.zt = room.take([P, 2, D])
        act1 = room.take([P, 2, HID])
        part = room.take([P, 2, D])
        squares = room.take([P, 2, D])
        total = room.take([P, 2 * D])
        stats = room.take([P, 4, NW * 6])
        moments = room.take([P, 4, 2])
        scale1 = room.take([P, 4])
        shift1 = room.take([P, 4])
        mean1 = room.take([P, 4])
        root1 = room.take([P, 4])
        row = room.take([1, 4, D])
        zeros = k.sims[:, 2 * D:]
        half_zeros = SUMROWS // P * EW // 2
        lines = room.take([P, 4, D])
        nodes_in = room.take([P, 2, NW])
        gates = room.take([P, 4, D])
        both = room.take([P, 2, D])
        g.zps = [psum(nc, ctx, f"gin_z{i}", [P, 512]) for i in range(2)]
        g.tps = [psum(nc, ctx, f"gin_t{i}", [P, 512]) for i in range(2)]
        ups = [psum(nc, ctx, f"gin_u{i}", [P, 512]) for i in range(2)]
        tot_ps = psum(nc, ctx, "gin_tot", [1, 512])
        bc_ps = psum(nc, ctx, "gin_bc", [P, 512])
        x = k.X.rearrange("p w d -> p (w d)")
        s_w, s_eps, s_stat, s_norm1, s_act1, s_u, s_x, s_usum, s_usq, s_tot, s_row, s_bc, s_all, s_zero, s_clear, s_tick, \
            s_root = sems(
            nc, k, *(f"gin_{n}" for n in ("w", "eps", "stat", "norm1", "act1", "u", "x", "usum", "usq", "tot", "row",
                                          "bc", "all", "zero", "clear", "tick", "root")))

        s_line, s_gate, s_both = sems(nc, k, "ng_line", "ng_gate", "ng_both")
        s_sent = sems(nc, k, "ng_sent0", "ng_sent1")

        combine, turn, copy_turned, hidden, s_t = gin_front(nc, k, g, "gina", s_stat)
        with nc.Block() as block:
            @block.sync
            def _(sp):
                sp.dma_start(g.w1[:, :, :], a["L0_gnn_W1"].rearrange("(c p) m -> p c m", p=P)).then_inc(s_w, 16)
                sp.dma_start(w2[:, :, :], a["L0_gnn_W2"].rearrange("(c p) m -> p c m", p=P)).then_inc(s_w, 16)
                sp.dma_start(b2[:, :], a["L0_gnn_b2"].to_broadcast([P, D])).then_inc(s_w, 16)
                for n, name in enumerate(("L0_gnn_b1", "L0_gnn_g1", "L0_gnn_bt1")):
                    sp.dma_start(cols[:, n, :], a[name].rearrange("o (c p) -> p (o c)", p=P),
                                 allow_slow_non_contiguous=True).then_inc(s_w, 16)
                sp.dma_start(g2[:, :], a["L0_gnn_g2"]).then_inc(s_w, 16)
                sp.dma_start(bt2[:, :], a["L0_gnn_bt2"]).then_inc(s_w, 16)
                sp.dma_start(g.eps1[:, :], a["L0_gnn_eps_gin"].to_broadcast([P, 1])).then_inc(s_w, 16)
                for n, name in enumerate(("W_cent", "b_cent", "W_vor", "b_vor")):
                    sp.dma_start(lines[:, n, :], a[f"L2_gnn_{name}"].to_broadcast([P, D])).then_inc(s_w, 16)
                sp.dma_start(nodes_in[:, 0, :], a["node_vec1_n2"]).then_inc(s_w, 16)
                sp.dma_start(nodes_in[:, 1, :], a["node_vec1"]).then_inc(s_w, 16)

                def send(w, slot, nodes):
                    sp.wait_ge(s_both, w + 1)
                    sp.dma_start(k.node_gates[bass.ds(w * P, P), :], both[:, slot, :]).then_inc(s_sent[slot], 16)

                over_windows(sp, (send, 0))
                sp.wait_ge(s_sent[0], 16 * (NW + 1) // 2)
                sp.wait_ge(s_sent[1], 16 * (NW // 2))

            @block.gpsimd
            def _(pool):
                def add_gates(w, slot, nodes):
                    pool.wait_ge(s_gate, w + 1)
                    if not early(w, 2):
                        pool.wait_ge(s_sent[slot], (w - slot) * 8)
                    pool.tensor_tensor(both[:, slot, :], gates[:, slot * 2, :], gates[:, slot * 2 + 1, :],
                                       ALU.add).then_inc(s_both, 1)

                over_windows(pool, (add_gates, 0))

            @block.vector
            def _(dve):
                dve.tensor_copy(k.count_in[:, :], k.acc.rearrange("p (w d) -> p w d", d=AW)[:, :, D])
                dve.wait_ge(s_w, 16 * 15)
                dve.tensor_scalar(g.eps1[:, :], g.eps1[:, :], 1.0, None, ALU.add).then_inc(s_eps, 1)
                dve.sem_inc(s_stat, 2)
                dve.wait_ge(s_eps, 1)

                def measure(w, slot, nodes):
                    dve.wait_ge(s_t, w + 3)
                    for m in range(4):
                        ins = dve.bn_stats(stats[:, m, bass.ds(w * 6, 6)], g.tps[slot][:, m * P:m * P + nodes])
                    ins.then_inc(s_stat, 1)

                def line(w, slot, nodes):
                    if not early(w, 2):
                        dve.wait_ge(s_both, w - 1)
                    for n in range(2):
                        dve.scalar_tensor_tensor(out=gates[:, slot * 2 + n, :], in0=lines[:, 2 * n, :],
                                                 scalar=nodes_in[:, n, bass.ds(w, 1)], in1=lines[:, 2 * n + 1, :],
                                                 op0=ALU.mult, op1=ALU.add).then_inc(s_line, 1)

                over_windows(dve, (combine(dve), 0), (measure, 2), (line, 1))
                dve.wait_ge(s_stat, NW + 2)
                for m in range(4):
                    dve.bn_aggr(moments[:, m, :], stats[:, m, :]).then_inc(s_norm1, 1)
                dve.wait_ge(s_norm1, 4)
                dve.wait_ge(s_root, 1)
                dve.reciprocal(scale1[:, :], root1[:, :]).then_inc(s_norm1, 1)
                dve.tensor_tensor(mean1[:, :], moments[:, :, 0], cols[:, 0, :], ALU.add).then_inc(s_norm1, 1)
                dve.wait_ge(s_norm1, 6)
                dve.tensor_tensor(scale1[:, :], scale1[:, :], cols[:, 1, :], ALU.mult).then_inc(s_norm1, 1)
                dve.tensor_tensor(shift1[:, :], cols[:, 0, :], mean1[:, :], ALU.subtract).then_inc(s_norm1, 1)
                dve.wait_ge(s_norm1, 8)
                dve.tensor_tensor(shift1[:, :], shift1[:, :], scale1[:, :], ALU.mult).then_inc(s_norm1, 1)
                dve.wait_ge(s_norm1, 9)
                dve.tensor_tensor(shift1[:, :], shift1[:, :], cols[:, 2, :], ALU.add).then_inc(s_norm1, 1)

            @block.tensor
            def _(pe):
                turn_z, hidden_t = turn(pe), hidden(pe)
                pe.wait_ge(s_w, 16 * 15)
                over_windows(pe, (turn_z, 0), (hidden_t, 1))

            @block.scalar
            def _(act):
                def gate(w, slot, nodes):
                    act.wait_ge(s_line, w * 2 + 2)
                    act.activation(gates[:, slot * 2:slot * 2 + 2, :], gates[:, slot * 2:slot * 2 + 2, :],
                                   ACT.Sigmoid).then_inc(s_gate, 1)

                over_windows(act, (gate, 2), (copy_turned(act), 0))
                act.wait_ge(s_norm1, 4)
                act.activation(root1[:, :], moments[:, :, 1], ACT.Sqrt, bias=k.eps[:, 0:1]).then_inc(s_root, 1)

        combine, turn, copy_turned, hidden, s_t = gin_front(nc, k, g, "ginb", s_act1)
        with nc.Block() as block:
            @block.sync
            def _(sp):
                sp.wait_ge(s_zero, 2)
                for b in range(BANKS):
                    sp.dma_start(k.attr_sum[b].rearrange("(p r) d -> p (r d)", p=P),
                                 zeros[:, 0:SUMROWS // P * EW]).then_inc(s_clear, 16)
                    for half in range(2):
                        sp.dma_start(k.out_sum[b].rearrange("(p h r) d -> p h (r d)", p=P, h=2)[:, half, :],
                                     zeros[:, 0:SUMROWS // P * D // 2]).then_inc(s_clear, 16)
                sp.wait_ge(s_clear, 16 * 3 * BANKS)

            @block.gpsimd
            def _(pool):
                pool.memset(total[:, :], 0.0).then_inc(s_tot, 2)

                def column_sums(w, slot, nodes):
                    pool.wait_ge(s_usq, w + 1)
                    pool.wait_ge(s_tot, w * 2 + 2)
                    pool.sem_inc(s_tick, 1)
                    pool.tensor_tensor(total[0:nodes, 0:D], total[0:nodes, 0:D], k.acc[0:nodes, sum_window(w)],
                                       ALU.add).then_inc(s_tot, 1)
                    pool.tensor_tensor(total[0:nodes, D:2 * D], total[0:nodes, D:2 * D], squares[0:nodes, slot, :],
                                       ALU.add).then_inc(s_tot, 1)

                over_windows(pool, (column_sums, 4))

            @block.vector
            def _(dve):
                dve.memset(zeros[:, 0:half_zeros], 0.0).then_inc(s_zero, 1)
                dve.memset(zeros[:, half_zeros:], 0.0).then_inc(s_zero, 1)
                dve.sem_inc(s_u, 2)

                def close(w, slot, nodes):
                    dve.wait_ge(s_x, w + 3)
                    dve.wait_ge(s_usum, w + 1)
                    dve.tensor_tensor(part[:, slot, :], ups[slot][:, 0:D], x[:, node_window(w)], ALU.add).then_inc(s_u, 1)
                    dve.wait_ge(s_u, w + 3)
                    dve.tensor_tensor(k.acc[:, sum_window(w)], part[:, slot, :], b2[:, :], ALU.add).then_inc(s_usum, 1)

                dve.sem_inc(s_usum, 2)
                over_windows(dve, (combine(dve), 0), (close, 4))
                mean, var, scale, shift = (row[:, n, :] for n in range(4))
                dve.wait_ge(s_all, 1)
                dve.tensor_scalar(mean, tot_ps[:, 0:D], 1.0 / N, None, ALU.mult).then_inc(s_row, 1)
                dve.wait_ge(s_row, 1)
                dve.tensor_tensor(scale, mean, mean, ALU.mult).then_inc(s_row, 1)
                dve.wait_ge(s_row, 2)
                dve.scalar_tensor_tensor(out=var, in0=tot_ps[:, D:2 * D], scalar=1.0 / N, in1=scale, op0=ALU.mult,
                                         op1=ALU.subtract).then_inc(s_row, 1)
                dve.wait_ge(s_row, 3)
                dve.tensor_scalar(var, var, 0.0, None, ALU.max).then_inc(s_row, 1)
                dve.wait_ge(s_root, 2)
                dve.reciprocal(var, shift).then_inc(s_row, 1)
                dve.wait_ge(s_row, 5)
                dve.tensor_tensor(scale, var, g2[:, :], ALU.mult).then_inc(s_row, 1)
                dve.wait_ge(s_row, 6)
                dve.tensor_tensor(mean, mean, scale, ALU.mult).then_inc(s_row, 1)
                dve.wait_ge(s_row, 7)
                dve.tensor_tensor(shift, bt2[:, :], mean, ALU.subtract).then_inc(s_row, 1)
                dve.wait_ge(s_bc, 1)
                dve.tensor_copy(k.norm2, bc_ps[:, :])

            @block.scalar
            def _(act):
                act.sem_inc(s_act1, 2)

                def activate(w, slot, nodes):
                    act.wait_ge(s_t, w + 3)
                    act.wait_ge(s_x, w + 1)
                    for m in range(4):
                        ins = act.activation(act1[:, slot, m * P:(m + 1) * P], g.tps[slot][:, m * P:(m + 1) * P],
                                             ACT.Relu, bias=shift1[:, m:m + 1], scale=scale1[:, m:m + 1])
                    ins.then_inc(s_act1, 1)

                def square(w, slot, nodes):
                    act.wait_ge(s_usum, w + 3)
                    if not early(w, 2):
                        act.wait_ge(s_tot, w * 2)
                    act.sem_inc(k.s_hold, 1)
                    act.activation(squares[:, slot, :], k.acc[:, sum_window(w)], ACT.Square).then_inc(s_usq, 1)

                over_windows(act, (copy_turned(act), 0), (activate, 1), (square, 4))
                act.wait_ge(s_row, 4)
                act.activation(row[:, 3, :], row[:, 1, :], ACT.Sqrt, bias=k.eps[0:1, 0:1]).then_inc(s_root, 1)

            @block.tensor
            def _(pe):
                pe.sem_inc(s_x, 2)
                turn_z, hidden_t = turn(pe), hidden(pe)

                def product(w, slot, nodes):
                    pe.wait_ge(s_act1, w + 3)
                    pe.wait_ge(s_u, w + 1)
                    for m in range(4):
                        ins = pe.matmul(ups[slot][:, 0:D], act1[:, slot, m * P:(m + 1) * P], w2[:, m, :],
                                        start=(m == 0), stop=(m == 3))
                    ins.then_inc(s_x, 1)

                over_windows(pe, (turn_z, 0), (hidden_t, 1), (product, 3))
                pe.wait_ge(s_tot, 2 * NW + 2)
                pe.matmul(tot_ps[:, :], k.ones[:, 0:1], total[:, :], start=True, stop=True).then_inc(s_all, 1)
                pe.wait_ge(s_row, 8)
                pe.matmul(bc_ps[:, :], k.ones[0:1, :], row[:, 2:4, :].rearrange("o a d -> o (a d)"),
                          start=True, stop=True).then_inc(s_bc, 1)


def gin_close_and_project(nc, k, a):
    with ExitStack() as ctx:
        room = Arena(k.sims[:, 2 * D:])
        wq = room.take([P, 2, D])
        wkv = room.take([P, 2, 2 * D])
        bias = room.take([P, 3 * D])
        new = room.take([P, 2, D])
        turned = room.take([P, 2, D])
        kv = room.take([P, 2, 2 * D])
        part = room.take([P, 2, D])
        stats = room.take([P, 2 * 9])
        zps = [psum(nc, ctx, f"qkv_z{i}", [P, 512]) for i in range(2)]
        qps = [psum(nc, ctx, f"qkv_q{i}", [P, 512]) for i in range(2)]
        kps = [psum(nc, ctx, f"qkv_k{i}", [P, 512]) for i in range(2)]
        x = k.X.rearrange("p w d -> p (w d)")
        s_w, s_part, s_res, s_mom, s_root, s_inv, s_new, s_kept, s_zps, s_zt, s_qkv, s_kv, s_tick = sems(
            nc, k, *(f"qkv_{n}" for n in ("w", "part", "res", "mom", "root", "inv", "new", "kept", "zps", "zt", "qkv",
                                          "kv", "tick")))
        s_out = sems(nc, k, "qkv_out0", "qkv_out1")
        block = ctx.enter_context(nc.Block())

        @block.sync
        def _(sp):
            sp.dma_start(wq[:, :, :], a["wq_t"].rearrange("(c p) m -> p c m", p=P)).then_inc(s_w, 16)
            sp.dma_start(wkv[:, :, 0:D], a["wk_t"].rearrange("(c p) m -> p c m", p=P)).then_inc(s_w, 16)
            sp.dma_start(wkv[:, :, D:], a["wv_t"].rearrange("(c p) m -> p c m", p=P)).then_inc(s_w, 16)
            for n, name in enumerate(("L1_gnn_bq", "L1_gnn_bk", "L1_gnn_bv")):
                sp.dma_start(bias[:, n * D:(n + 1) * D], a[name].to_broadcast([P, D])).then_inc(s_w, 16)

            def send(w, slot, nodes):
                sp.wait_ge(s_kv, w + 1)
                sp.dma_start(k.kv_rows[bass.ds(w * P, P), :], kv[:, slot, :]).then_inc(s_out[slot], 16)

            over_windows(sp, (send, 0))
            sp.wait_ge(s_out[0], 16 * (NW + 1) // 2)
            sp.wait_ge(s_out[1], 16 * (NW // 2))

        @block.vector
        def _(dve):
            dve.sem_inc(s_new, 2)
            dve.wait_ge(s_w, 16 * 6)

            def residual(w, slot, nodes):
                here = part[:, slot, :]
                dve.wait_ge(s_part, w * 2 + 2)
                dve.scalar_tensor_tensor(out=here, in0=here, scalar=0.0, in1=x[:, node_window(w)], op0=ALU.max,
                                         op1=ALU.add).then_inc(s_res, 1)

            def measure(w, slot, nodes):
                dve.wait_ge(s_res, w * 2 + 1)
                row_moments(dve, k, part[:, slot, :], stats[:, slot * 9:slot * 9 + 9], s_res, w * 2 + 1).then_inc(s_mom, 1)

            def scale(w, slot, nodes):
                st = stats[:, slot * 9:slot * 9 + 9]
                dve.wait_ge(s_root, w + 1)
                dve.reciprocal(st[:, 8:9], st[:, 8:9]).then_inc(s_inv, 1)
                dve.wait_ge(s_inv, w + 1)
                dve.wait_ge(s_zps, w + 1)
                dve.wait_ge(s_kept, w + 1)
                dve.tensor_scalar(new[:, slot, :], part[:, slot, :], st[:, 6:7], st[:, 8:9], ALU.subtract,
                                  ALU.mult).then_inc(s_new, 1)

            def bias_q(w, slot, nodes):
                dve.wait_ge(s_qkv, w + 3)
                dve.tensor_tensor(k.side[:, node_window(w)], qps[slot][:, 0:D], bias[:, 0:D], ALU.add)

            def bias_kv(w, slot, nodes):
                if not early(w, 2):
                    dve.wait_ge(s_out[slot], (w - slot) * 8)
                dve.tensor_tensor(kv[:, slot, :], kps[slot][:, :], bias[:, D:], ALU.add).then_inc(s_kv, 1)

            over_windows(dve, (scale, 2), (residual, 1), (bias_q, 5), (measure, 1), (bias_kv, 5))

        @block.gpsimd
        def _(pool):
            def norm(w, slot, nodes):
                here = part[:, slot, :]
                pool.wait_ge(s_new, w + 1)
                pool.sem_inc(s_tick, 1)
                pool.tensor_tensor(here, k.acc[:, sum_window(w)], k.norm2[:, 0:D], ALU.mult).then_inc(s_part, 1)
                pool.wait_ge(s_part, w * 2 + 1)
                pool.tensor_tensor(here, here, k.norm2[:, D:2 * D], ALU.add).then_inc(s_part, 1)

            over_windows(pool, (norm, 0))

        @block.tensor
        def _(pe):
            pe.sem_inc(s_zps, 2)
            pe.sem_inc(s_qkv, 2)
            pe.wait_ge(s_w, 16 * 6)

            def turn(w, slot, nodes):
                pe.wait_ge(s_new, w + 3)
                pe.wait_ge(s_zt, w + 1)
                for c in range(2):
                    ins = pe.transpose(zps[slot][:, c * P:(c + 1) * P], new[:, slot, c * P:(c + 1) * P], k.ident[:, :])
                ins.then_inc(s_zps, 1)

            def project(w, slot, nodes):
                pe.wait_ge(s_zt, w + 3)
                if isinstance(w, int) and w < 2:
                    pass
                else:
                    pe.wait_ge(s_kv, w - 1)
                for c in range(2):
                    pe.matmul(qps[slot][:, 0:D], turned[:, slot, c * P:(c + 1) * P], wq[:, c, :], start=(c == 0),
                              stop=(c == 1))
                for c in range(2):
                    ins = pe.matmul(kps[slot][:, :], turned[:, slot, c * P:(c + 1) * P], wkv[:, c, :], start=(c == 0),
                                    stop=(c == 1))
                ins.then_inc(s_qkv, 1)

            over_windows(pe, (turn, 3), (project, 4))

        @block.scalar
        def _(act):
            act.sem_inc(s_zt, 2)
            act.sem_inc(s_kept, 2)

            def keep(w, slot, nodes):
                act.wait_ge(s_new, w + 3)
                act.copy(x[:, node_window(w)], new[:, slot, :]).then_inc(s_kept, 1)
                act.wait_ge(s_zps, w + 3)
                act.wait_ge(s_qkv, w + 1)
                act.copy(turned[:, slot, :], zps[slot][:, 0:D]).then_inc(s_zt, 1)

            def root(w, slot, nodes):
                act.wait_ge(s_mom, w + 1)
                st = stats[:, slot * 9:slot * 9 + 9]
                act.activation(st[:, 8:9], st[:, 7:8], ACT.Sqrt, bias=k.eps[:, 0:1]).then_inc(s_root, 1)

            over_windows(act, (keep, 3), (root, 1))


def edge_scores(nc, k):
    with ExitStack() as ctx:
        room = Arena(k.acc)
        ring = room.take([P, U, 2 * D])
        by_edge = room.take([P, HALF, P])
        onehot = room.take([P, 4, P])
        prod = room.take([P, 2, D])
        cur_idx = room.take([P, U], I32)
        cur_dst = room.take([P, U])
        cur_sim = room.take([P, U, HEADS])
        query = k.side
        qps = [psum(nc, ctx, f"es_q{i}", [P, 512]) for i in range(4)]
        tps = [psum(nc, ctx, f"es_t{i}", [P, 512]) for i in range(4)]
        s_cur, s_tick, s_mark, s_turn, s_hot, s_q, s_prod, s_sim, s_stored, s_copied = sems(
            nc, k, *(f"es_{n}" for n in ("cur", "tick", "mark", "turn", "hot", "q", "prod", "sim", "stored", "copied")))
        s_vout = sems(nc, k, *(f"es_vout{u}" for u in range(U)))
        s_row, row0 = k.s_row, k.rows_before
        k.rows_before += 16 * IT
        block = ctx.enter_context(nc.Block())

        @block.gpsimd
        def _(pool):
            with pool.Fori(0, IT) as it:
                for u in range(U):
                    if u % HALF == 0:
                        pool.wait_ge(s_cur, it * 2 + (1 + u // HALF))
                    pool.wait_ge(s_prod, it * U + (u + 1))
                    pool.wait_ge(s_stored, it * U + (u + 1))
                    pool.sem_inc(s_tick, 1)
                    pool.indirect_dma_start(ring[:, u, :], None, k.kv_rows, bass.IndirectOffsetOnAxis(
                        ap=cur_idx[:, u:u + 1], axis=0)).then_inc(s_row[u], 16)

        @block.sync
        def _(sp):
            sp.sem_inc(s_stored, U)
            LAG = 4

            def stored(it, u):
                sp.wait_ge(s_vout[u], it * 16 + 16)
                sp.sem_inc(s_stored, 1)

            with sp.Fori(0, IT) as it:
                for u in range(U):
                    sp.wait_ge(s_row[u], it * 16 + (row0 + 16))
                    sp.dma_start(k.v_edge[bass.ds(it * U * P + u * P, P), :], ring[:, u, D:]).then_inc(s_vout[u], 16)
                    if u >= LAG:
                        stored(it, u - LAG)
                for u in range(U - LAG, U):
                    stored(it, u)

        @block.tensor
        def _(pe):
            def turn(it, u):
                pe.wait_ge(s_mark, it * U + (u + 1))
                pe.wait_ge(s_hot, it * U + (u + 1))
                pe.transpose(tps[u % 4][:, 0:P], by_edge[:, u % HALF, :], k.ident[:, :]).then_inc(s_turn, 1)

            pe.sem_inc(s_q, 4)
            pe.sem_inc(s_turn, HALF)
            turn(0, 0)
            turn(0, 1)
            with pe.Fori(0, IT) as it:
                win = load_steps(nc, pe, k.win, it, NW - 1)
                for u in range(U):
                    turn(it, u + 2)
                    pe.wait_ge(s_hot, it * U + (4 + u + 1))
                    pe.wait_ge(s_prod, it * U + (U + u + 1 - 4))
                    pe.matmul(qps[u % 4][:, 0:D], onehot[:, u % 4, :], query[:, node_window(win[u])],
                              start=True, stop=True).then_inc(s_q, 1)

        @block.scalar
        def _(act):
            act.sem_inc(s_hot, 4)
            with act.Fori(0, IT) as it:
                for u in range(U):
                    act.wait_ge(s_turn, it * U + (HALF + u + 1))
                    act.wait_ge(s_q, it * U + (u + 1))
                    act.copy(onehot[:, u % 4, :], tps[u % 4][:, 0:P]).then_inc(s_hot, 1)

        @block.vector
        def _(dve):
            def refill(h, at):
                part = slice(h * HALF, (h + 1) * HALF)
                dve.tensor_copy(cur_dst[:, part], k.dst[:, bass.ds(at, HALF)])
                dve.tensor_copy(cur_idx[:, part], k.idx[:, bass.ds(at, HALF)]).then_inc(s_cur, 1)

            def hot(it, u):
                if u % HALF == 0:
                    dve.wait_ge(s_cur, it * 2 + (1 + u // HALF))
                dve.wait_ge(s_turn, it * U + (u + QUAD))
                compare(dve, k, by_edge[:, u % HALF:u % HALF + QUAD, :], None,
                        cur_dst[:, u % U:u % U + QUAD]).then_inc(s_mark, QUAD)

            def score(it, u):
                dve.wait_ge(s_q, it * U + (u + 1 + 4))
                dve.wait_ge(s_row[u], it * 16 + (row0 + 16))
                dve.wait_ge(s_sim, it * U + (u + 1))
                dve.tensor_tensor(prod[:, u % 2, :], qps[u % 4][:, 0:D], ring[:, u, 0:D], ALU.mult).then_inc(s_prod, 1)

            def heads(it, u):
                dve.wait_ge(s_prod, it * U + (U + u + 1))
                dve.tensor_reduce(cur_sim[:, u, :], prod[:, u % 2, :].rearrange("p (h d) -> p h d", h=HEADS), AX.X,
                                  ALU.add).then_inc(s_sim, 1)

            for h in range(2):
                refill(h, h * HALF)
            dve.sem_inc(s_prod, U)
            dve.sem_inc(s_sim, 2)
            dve.sem_inc(s_copied, 2)
            def keep(it, h):
                dve.wait_ge(s_sim, it * U + ((h + 1) * HALF + 2))
                dve.sem_inc(k.s_hold, 1)
                dve.tensor_copy(k.sims[:, bass.ds(it * U * HEADS + h * HALF * HEADS, HALF * HEADS)],
                                cur_sim[:, h * HALF:(h + 1) * HALF, :].rearrange("p u h -> p (u h)")).then_inc(s_copied, 1)

            hot(0, 0)
            with dve.Fori(0, IT) as it:
                for u in range(U):
                    if u % QUAD == 0:
                        hot(it, u + QUAD)
                    if u % HALF == 0:
                        dve.wait_ge(s_copied, it * 2 + (1 + u // HALF))
                    score(it, u)
                    if u:
                        heads(it, u - 1)
                    if u % HALF == HALF - 1:
                        refill(u // HALF, it * U + (U + u + 1 - HALF))
                    if u == HALF + 1:
                        keep(it, 0)
                heads(it, U - 1)
                keep(it, 1)


def softmax_weights(nc, k):
    T = 5
    STEPS_OF_SCAN = 9
    with ExitStack() as ctx:
        room = Arena(k.big[:, :])
        one = room.take([P, SCAN])
        two = room.take([P, SCAN])
        three = room.take([P, SCAN])
        neg = room.take([P, STEPS])
        stage = room.take([P, T, P])
        edge = room.take([P, 2, 2])
        carry = room.take([P, 2])
        row_last = room.take([1, P])
        row_open = room.take([1, P])
        row_scan = room.take([1, P])
        row_in = room.take([1, P])
        tps = [psum(nc, ctx, f"sm_t{i}", [P, P]) for i in range(T)]
        rps = psum(nc, ctx, "sm_r", [1, 2, P])
        cps = psum(nc, ctx, "sm_c", [P, 2])
        s_key, s_mask, s_stage, s_turn, s_in, s_c, s_edge, s_row, s_col, s_back, s_bturn, s_out = sems(
            nc, k, *(f"sm_{n}" for n in ("key", "mask", "stage", "turn", "in", "c", "edge", "row", "col", "back",
                                         "bturn", "out")))
        sims = k.sims.rearrange("p (g j h) -> p j g h", g=GROUPS, h=HEADS)
        flat = k.key_row

        def keys(offset):
            run = flat[P + offset:P + offset + GROUPS * SCAN].rearrange("(g o t) -> g o t", g=GROUPS, o=1)
            return run.to_broadcast([GROUPS, HEADS, SCAN])

        block = ctx.enter_context(nc.Block())

        @block.sync
        def _(sp):
            sp.dma_start(one, keys(0)).then_inc(s_key, 16)
            sp.dma_start(two, keys(-1)).then_inc(s_key, 16)
            sp.wait_ge(s_c, STEPS_OF_SCAN)
            sp.dma_start(three, keys(0)).then_inc(s_key, 16)
            sp.dma_start(two, keys(1)).then_inc(s_key, 16)

        @block.scalar
        def _(act):
            act.sem_inc(s_stage, T)
            act.wait_ge(s_mask, 2)
            with act.Fori(0, GS // T) as it:
                for u in range(T):
                    act.wait_ge(s_turn, it * T + (u + 1))
                    act.copy(stage[:, u, :].rearrange("p (g h) -> p g h", g=GROUPS),
                             sims[:, bass.ds(it * T + u, 1), :, :].rearrange("p j g h -> p (j g) h")).then_inc(s_stage, 1)
            act.wait_ge(s_c, 2 * STEPS_OF_SCAN)
            with act.Fori(0, GS // T) as it:
                for u in range(T):
                    act.wait_ge(s_turn, it * T + (GS + u + 1))
                    act.copy(stage[:, u, :], three[:, bass.ds(it * T * P + u * P, P)]).then_inc(s_stage, 1)
            act.wait_ge(s_out, GS + T)
            act.activation(k.sims, k.sims, ACT.Exp, scale=SCALE).then_inc(s_back, 1)

        @block.tensor
        def _(pe):
            pe.sem_inc(s_turn, T)

            def turn(base):
                with pe.Fori(0, GS // T) as it:
                    for u in range(T):
                        pe.wait_ge(s_stage, it * T + (base + T + u + 1))
                        pe.wait_ge(s_in if base == 0 else s_out, it * T + (u + 1))
                        pe.transpose(tps[u][:, :], stage[:, u, :], k.ident[:, :]).then_inc(s_turn, 1)

            def edges(n):
                pe.wait_ge(s_edge, 2 * n + 2)
                pe.transpose(rps[:, 0, :], edge[:, n, 0:1], k.ident[:, :])
                pe.transpose(rps[:, 1, :], edge[:, n, 1:2], k.ident[:, :]).then_inc(s_row, 1)
                pe.wait_ge(s_col, n + 1)
                pe.matmul(cps[:, n:n + 1], row_in[:, :], k.ones[0:1, 0:1], start=True, stop=True).then_inc(s_row, 1)

            turn(0)
            edges(0)
            edges(1)
            turn(GS)

        @block.vector
        def _(dve):
            dve.tensor_scalar(neg[:, :], k.own[:, 0:STEPS], 0.0, -BIG, ALU.is_lt, ALU.mult).then_inc(s_mask, 1)
            dve.wait_ge(s_mask, 1)
            by_step = k.sims.rearrange("p (i h) -> p i h", h=HEADS)
            dve.tensor_tensor(by_step, by_step, neg[:, :].unsqueeze(2).to_broadcast([P, STEPS, HEADS]),
                              ALU.add).then_inc(s_mask, 1)
            dve.sem_inc(s_in, T)
            with dve.Fori(0, GS // T) as it:
                for u in range(T):
                    dve.wait_ge(s_turn, it * T + (T + u + 1))
                    dve.tensor_scalar(three[:, bass.ds(it * T * P + u * P, P)], tps[u][:, :], 1.0, None,
                                      ALU.mult).then_inc(s_in, 1)

            def scan(n, out, key, near, data, lead, tail, done):
                flip = (lambda x: x) if n == 0 else (lambda x: x[:, ::-1])
                c = lambda: dve.wait_ge(s_c, done[0])

                def next_c(ins):
                    ins.then_inc(s_c, 1)
                    done[0] += 1
                down = (lambda far, at: (at, far)) if n == 0 else (lambda far, at: (far, at))
                dve.tensor_tensor(edge[:, n, 1:2], *down(key[:, tail], near[:, lead]), ALU.subtract).then_inc(s_edge, 1)
                dve.wait_ge(s_edge, 2 * n + 1)
                next_c(dve.tensor_tensor(near, *down(key, near), ALU.subtract))
                c()
                next_c(dve.tensor_tensor_scan(flip(out), flip(near), flip(data), LOW, ALU.add, ALU.max))
                c()
                dve.tensor_copy(edge[:, n, 0:1], out[:, tail]).then_inc(s_edge, 1)
                by_head = lambda row: row.rearrange("o (h g) -> o h g", h=HEADS)
                by_run = lambda row: row.rearrange("o (g h) -> o h g", h=HEADS)
                dve.wait_ge(s_row, 2 * n + 1)
                next_c(dve.tensor_copy(by_head(row_last), by_run(rps[:, 0, :])))
                next_c(dve.tensor_copy(by_head(row_open), by_run(rps[:, 1, :])))
                c()
                first = 0 if n == 0 else GROUPS - 1
                next_c(dve.memset(by_head(row_open)[:, :, first:first + 1], LOW))
                next_c(dve.memset(row_in[:, :], LOW))
                c()
                next_c(dve.tensor_tensor_scan(flip(row_scan), flip(row_open), flip(row_last), LOW, ALU.add, ALU.max))
                c()
                to, of = (slice(1, GROUPS), slice(0, GROUPS - 1)) if n == 0 else (slice(0, GROUPS - 1), slice(1, GROUPS))
                dve.tensor_copy(by_run(row_in)[:, :, to], by_head(row_scan)[:, :, of]).then_inc(s_col, 1)
                dve.wait_ge(s_row, 2 * n + 2)
                next_c(dve.tensor_copy(carry[:, n:n + 1], cps[:, n:n + 1]))
                c()
                next_c(dve.tensor_tensor_scan(flip(out), flip(near), flip(data), carry[:, n:n + 1], ALU.add, ALU.max))
                c()
            done = [0]
            start, end = slice(0, 1), slice(SCAN - 1, SCAN)
            dve.wait_ge(s_in, GS + T)
            dve.wait_ge(s_key, 32)
            scan(0, one, one, two, three, start, end, done)
            assert done[0] == STEPS_OF_SCAN, done
            dve.wait_ge(s_key, 64)
            scan(1, three, three, two, one, end, start, done)
            dve.sem_inc(s_out, T)
            with dve.Fori(0, GS // T) as it:
                for u in range(T):
                    here = sims[:, bass.ds(it * T + u, 1), :, :].rearrange("p j g h -> p (j g) h")
                    dve.wait_ge(s_turn, it * T + (GS + T + u + 1))
                    dve.tensor_tensor(here, here, tps[u][:, :].rearrange("p (g h) -> p g h", g=GROUPS),
                                      ALU.subtract).then_inc(s_out, 1)


def weighted_sums(nc, k, attr_rows):
    with ExitStack() as ctx:
        room = Arena(k.side)
        ring = room.take([P, U, D])
        weighted = room.take([P, 4, AW])
        onehot = room.take([P, HALF, P])
        attr = room.take([P, U, EW])
        equal = room.take([P, HALF, P])
        ready = room.take([P, HALF, EW])
        cur_src = room.take([P, U])
        cur_row = room.take([P, U], I32)
        spare = room.take([P, 1], I32)
        sums = [psum(nc, ctx, f"ws_sums{i}", [P, 512]) for i in range(4)]
        asums = [psum(nc, ctx, f"at_sums{i}", [P, 512]) for i in range(2)]
        wide = [psum(nc, ctx, f"at_wide{i}", [P, 512]) for i in range(2)]
        s_cur, s_hot, s_weight, s_side, s_sum, s_acc, s_zero = sems(
            nc, k, *(f"ws_{n}" for n in ("cur", "hot", "weight", "side", "sum", "acc", "zero")))
        s_one, s_rowcur, s_equal, s_mm, s_ready, s_prime, s_tick, s_wide = sems(
            nc, k, *(f"at_{n}" for n in ("one", "rowcur", "equal", "mm", "ready", "prime", "tick", "wide")))
        s_v = sems(nc, k, *(f"ws_v{q}" for q in range(U // 2)))
        s_attr = sems(nc, k, *(f"at_attr{q}" for q in range(U // QUAD)))
        s_sent = k.s_sent
        block = ctx.enter_context(nc.Block())

        @block.sync
        def _(sp):
            with sp.Fori(0, IT) as it:
                chunk = load_steps(nc, sp, k.chunk, it, NC - 1)
                for u in range(U):
                    if u % QUAD == 0:
                        sp.wait_ge(s_mm, it * U + (u + QUAD))
                        sp.dma_start(attr[:, u:u + QUAD, 0:EA], attr_rows[bass.ds(chunk[u] * P, QUAD * P), :].rearrange(
                            "(c p) d -> p c d", p=P)).then_inc(s_attr[u // QUAD], 16)
                    if u % 2 == 0:
                        sp.wait_ge(s_weight, it * U + (u + 2))
                        sp.dma_start(ring[:, u:u + 2, :], k.v_edge[bass.ds(it * U * P + u * P, 2 * P), :].rearrange(
                            "(s p) d -> p s d", p=P)).then_inc(s_v[u // 2], 16)

        @block.scalar
        def _(act):
            act.sem_inc(s_ready, U)
            with act.Fori(0, IT) as it:
                for u in range(U):
                    act.wait_ge(s_sum, it * U + (u + 1 + 4))
                    act.copy(weighted[:, u % 4, D:], k.sims[:, bass.ds(it * U * HEADS + u * HEADS, HEADS)]).then_inc(
                        s_side, 1)
                    act.wait_ge(s_mm, it * U + (U + u + 1))
                    act.wait_ge(s_sent[u % HALF], it * 32 + 16 * (1 + u // HALF))
                    act.copy(ready[:, u % HALF, :], asums[u % 2][:, 0:EW]).then_inc(s_ready, 1)

        @block.gpsimd
        def _(pool):
            pool.wait_ge(s_prime, 2)
            for v in range(HALF):
                if v >= BANKS:
                    pool.wait_ge(s_sent[v - BANKS], 16)
                pool.indirect_dma_start(k.attr_sum[v % BANKS], bass.IndirectOffsetOnAxis(ap=spare[:, 0:1], axis=0),
                                        ready[:, v, :], None, compute_op=ALU.add).then_inc(s_sent[v], 16)
            with pool.Fori(0, IT) as it:
                for u in range(U):
                    if u % QUAD == 0:
                        pool.wait_ge(s_rowcur, it * (U // QUAD) + (1 + u // QUAD))
                    pool.wait_ge(s_ready, it * U + (U + u + 1))
                    pool.wait_ge(s_sent[(u - BANKS) % HALF], it * 32 + 16 * (2 + (u - BANKS) // HALF))
                    pool.sem_inc(s_tick, 1)
                    pool.indirect_dma_start(k.attr_sum[u % BANKS], bass.IndirectOffsetOnAxis(ap=cur_row[:, u:u + 1], axis=0),
                                            ready[:, u % HALF, :], None, compute_op=ALU.add).then_inc(s_sent[u % HALF], 16)
            for v in range(HALF):
                pool.wait_ge(s_sent[v], 16 * (1 + 2 * IT))

        @block.tensor
        def _(pe):
            pe.sem_inc(s_sum, HALF)
            pe.sem_inc(s_mm, U)
            pe.wait_ge(s_one, 1)
            by_chunk = attr.rearrange("p c d -> p (c d)")

            def sources(it, u):
                if u % HALF == 0:
                    pe.wait_ge(s_cur, it * 2 + (1 + u // HALF))
                if u >= HALF:
                    pe.wait_ge(s_equal, it * U + (u - QUAD))
                widen(pe, k, wide[u // QUAD % 2], cur_src[:, u % U:u % U + QUAD]).then_inc(s_wide, QUAD)

            sources(0, 0)
            sources(0, QUAD)
            with pe.Fori(0, IT) as it:
                beyond = load_steps(nc, pe, k.beyond, it, QUAD - 1)
                for u in range(U):
                    first = u // QUAD * QUAD
                    if u == first:
                        sources(it, u + HALF)
                    if u == first:
                        pe.wait_ge(s_attr[u // QUAD], it * 16 + 16)
                    pe.wait_ge(s_equal, it * U + (u + 1))
                    pe.wait_ge(s_ready, it * U + (U + u + 1 - 2))
                    pe.matmul(asums[u % 2][:, 0:EW], equal[:, u % HALF, :],
                              by_chunk[:, bass.ds((beyond[u] + first) * EW, EW)],
                              start=True, stop=True).then_inc(s_mm, 1)
                    pe.wait_ge(s_weight, it * U + (U + u + 1))
                    pe.wait_ge(s_side, it * U + (u + 1))
                    pe.wait_ge(s_hot, it * U + (u + 1))
                    pe.wait_ge(s_acc, it * U + (u + 1))
                    pe.matmul(sums[u % 4][:, 0:AW], onehot[:, u % HALF, :], weighted[:, u % 4, :],
                              start=True, stop=True).then_inc(s_sum, 1)

        @block.vector
        def _(dve):
            def refill(h, at):
                part = slice(h * HALF, (h + 1) * HALF)
                dve.tensor_copy(cur_src[:, part], k.src[:, bass.ds(at, HALF)]).then_inc(s_cur, 1)

            def tables(it, u):
                at, slots = bass.ds(it * U + u, QUAD), slice(u % HALF, u % HALF + QUAD)
                dve.wait_ge(s_wide, it * U + (u + QUAD))
                dve.wait_ge(s_mm, it * U + (u + QUAD + U - HALF))
                compare(dve, k, equal[:, slots, :], wide[u // QUAD % 2][:, :].rearrange("p (s e) -> p s e", s=QUAD),
                        k.own[:, at]).then_inc(s_equal, QUAD)
                dve.wait_ge(s_sum, it * U + (u + QUAD))
                compare(dve, k, onehot[:, slots, :], None, k.dst[:, at]).then_inc(s_hot, QUAD)

            def weigh(it, u):
                at, more = u % U, u // U
                dve.wait_ge(s_sum, it * U + (u + 1 + 4))
                if u % 2 == 0:
                    dve.wait_ge(s_v[at // 2], it * 16 + 16 * (1 + more))
                weight = k.sims[:, bass.ds(it * U * HEADS + u * HEADS, HEADS)]
                dve.tensor_tensor(weighted[:, u % 4, 0:D].rearrange("p (h d) -> p h d", h=HEADS),
                                  ring[:, at, :].rearrange("p (h d) -> p h d", h=HEADS),
                                  weight.unsqueeze(2).to_broadcast([P, HEADS, HD]), ALU.mult).then_inc(s_weight, 1)

            def add(it, u, win):
                dve.wait_ge(s_sum, it * U + (u + 1 + HALF))
                dve.wait_ge(s_acc, it * U + (u + 4))
                here = k.acc[:, sum_window(win, AW)]
                dve.tensor_tensor(here, sums[u % 4][:, 0:AW], here, ALU.add).then_inc(s_acc, 1)

            dve.memset(attr[:, :, EA:EW], 1.0).then_inc(s_one, 1)
            dve.memset(ready[:, :, :], 0.0).then_inc(s_prime, 1)
            dve.tensor_copy(spare[:, :], k.trash[:, :]).then_inc(s_prime, 1)
            dve.memset(k.acc, 0.0).then_inc(s_zero, 1)
            dve.wait_ge(s_zero, 1)
            for h in range(2):
                refill(h, h * HALF)
            dve.sem_inc(s_weight, U)
            dve.sem_inc(s_acc, 4)

            def next_rows(it, u):
                at = u % U
                dve.wait_ge(s_ready, it * U + u + (U - QUAD))
                dve.tensor_copy(cur_row[:, at:at + QUAD], k.sidx[:, bass.ds(it * U + u, QUAD)]).then_inc(s_rowcur, 1)

            next_rows(0, 0)

            def turn(it, last=False):
                win = load_steps(nc, dve, k.win, it, NW - 1)
                for h in range(2):
                    for u in range(h * HALF, (h + 1) * HALF):
                        if u % QUAD == 1 and not (last and u + QUAD > U):
                            next_rows(it, u + QUAD - 1)
                        if u % QUAD == 0 and not (last and u + QUAD >= U):
                            tables(it, u + QUAD)
                        if not (last and u + 2 >= U):
                            weigh(it, u + 2)
                        add(it, u, win[u])
                    dve.wait_ge(s_equal, it * U + (h + 1) * HALF)
                    refill(h, it * U + (U + h * HALF))

            tables(0, 0)
            weigh(0, 0)
            weigh(0, 1)
            with dve.Fori(0, IT - 1) as it:
                turn(it)
            turn(IT - 1, last=True)


def attend_close(nc, k, a):
    S = 4
    with ExitStack() as ctx:
        room = Arena(k.sims)
        wo = room.take([P, 2, D])
        w_sum = room.take([P, D])
        bo = room.take([1, D])
        sum_t = room.take([P, S, P])
        degree = room.take([P, S, P])
        index = room.take([P, S, 2], I32)
        quarter = room.take([P, 1])
        share = room.take([P, NW, HEADS])
        stats = room.take([P, S * 2 * 9])
        gates = room.take([P, S, D])
        sets = Arena(k.side)
        banks = sets.take([P, S * BANKS, EW])
        z = sets.take([P, S * 2, D])
        b_sum = sets.take([P, D])
        agg = sets.take([P, S, D])
        agg_t = room.take([P, S, D])
        part = sets.take([P, S, D])
        tps = [psum(nc, ctx, f"ac_t{i}", [P, 512]) for i in range(2)]
        ops = [psum(nc, ctx, f"ac_o{i}", [P, 512]) for i in range(2)]
        sps = [psum(nc, ctx, f"ac_s{i}", [P, 512]) for i in range(2)]
        pps = [psum(nc, ctx, f"ac_p{i}", [P, 512]) for i in range(2)]
        x = k.X.rearrange("p w d -> p (w d)")
        s_w, s_share, s_agg, s_turn, s_turned, s_out, s_part, s_mom1, s_mom2, s_root1, s_root2, s_inv1, s_inv2, s_two, \
            s_new, s_sent = sems(nc, k, *(f"ac_{n}" for n in (
                "w", "share", "agg", "turn", "turned", "out", "part", "mom1", "mom2", "root1", "root2", "inv1", "inv2",
                "two", "new", "sent")))
        s_count, s_index, s_diag, s_bturn, s_bturned, s_proj, s_term, s_tick, s_fetched = sems(
            nc, k, *(f"nt_{n}" for n in ("count", "index", "diag", "turn", "turned", "proj", "term", "tick",
                                         "fetched")))
        s_gate = sems(nc, k, *(f"nt_gate{i}" for i in range(S)))
        s_bank = sems(nc, k, *(f"nt_bank{i}" for i in range(S)))
        block = ctx.enter_context(nc.Block())
        over = lambda engine, *stages: over_windows(engine, *stages, slots=S)
        turns = lambda w, slot, per: (w - slot) * (16 * per // S)
        moments = lambda slot, n: stats[:, (slot * 2 + n) * 9:(slot * 2 + n) * 9 + 9]

        @block.sync
        def _(sp):
            sp.dma_start(wo[:, :, :], a["wo_t"].rearrange("(c p) m -> p c m", p=P)).then_inc(s_w, 16)
            sp.dma_start(bo[:, :], a["L1_gnn_bo"]).then_inc(s_w, 16)
            sp.dma_start(w_sum, a["L2_gnn_W_sum"]).then_inc(s_w, 16)
            sp.dma_start(b_sum, a["L2_gnn_b_sum"].to_broadcast([P, D])).then_inc(s_w, 16)

            def load(w, slot, nodes):
                if not early(w, S):
                    sp.wait_ge(s_bturn, w - (S - 1))
                    sp.wait_ge(s_count, w - (S - 1))
                for b in range(BANKS):
                    sp.dma_start(banks[:, slot * BANKS + b, :], k.attr_sum[b][bass.ds(w * P, P), :]).then_inc(
                        s_bank[slot], 16)
                if not early(w, S):
                    sp.wait_ge(s_proj, w - (S - 1))
                sp.dma_start(gates[:, slot, :], k.node_gates[bass.ds(w * P, P), :]).then_inc(s_gate[slot], 16)

            def send(w, slot, nodes):
                sp.wait_ge(s_new, w + 1)
                sp.dma_start(k.x3_rows[bass.ds(w * P, P), :], x[:, node_window(w)]).then_inc(s_sent, 16)

            over(sp, (load, 0), (send, 6))
            sp.wait_ge(s_sent, 16 * NW)

        @block.gpsimd
        def _(pool):
            def fetch(w, slot, nodes):
                pool.wait_ge(s_index, w * 2 + 2)
                if not early(w, S):
                    pool.wait_ge(s_proj, w - (S - 1))
                pool.sem_inc(s_tick, 1)
                for n, table in enumerate((a["L2_gnn_z_in"], a["L2_gnn_z_out"])):
                    pool.indirect_dma_start(z[:, slot * 2 + n, :], None, table, bass.IndirectOffsetOnAxis(
                        ap=index[:, slot, n:n + 1], axis=0)).then_inc(k.s_z[slot], 16)

            def add_fetched(w, slot, nodes):
                here = z[:, slot * 2, :]
                pool.wait_ge(k.s_z[slot], turns(w, slot, 2) + 32)
                pool.sem_inc(s_tick, 1)
                pool.tensor_tensor(here, here, z[:, slot * 2 + 1, :], ALU.add).then_inc(s_fetched, 1)
                pool.wait_ge(s_gate[slot], turns(w, slot, 1) + 16)
                pool.wait_ge(s_fetched, w * 2 + 1)
                pool.tensor_tensor(here, here, gates[:, slot, :], ALU.add).then_inc(s_fetched, 1)

            over(pool, (fetch, 0), (add_fetched, 1))

        @block.tensor
        def _(pe):
            pe.wait_ge(s_w, 16 * 4)

            def turn(w, slot, nodes):
                pe.wait_ge(s_agg, w + 1)
                if not early(w, 2):
                    pe.wait_ge(s_turned, w - 1)
                for c in range(2):
                    ins = pe.transpose(tps[slot % 2][:, c * P:(c + 1) * P], agg[:, slot, c * P:(c + 1) * P], k.ident[:, :])
                ins.then_inc(s_turn, 1)

            def project(w, slot, nodes):
                pe.wait_ge(s_turned, w + 1)
                if not early(w, 2):
                    pe.wait_ge(s_part, (w - 2) * 2 + 1)
                for c in range(2):
                    pe.matmul(ops[slot % 2][:, 0:D], agg_t[:, slot, c * P:(c + 1) * P], wo[:, c, :], start=(c == 0),
                              stop=False)
                pe.matmul(ops[slot % 2][:, 0:D], k.ones[0:1, :], bo[:, :], start=False, stop=True).then_inc(s_out, 1)

            def turn_banks(w, slot, nodes):
                pe.wait_ge(s_bank[slot], turns(w, slot, BANKS) + 16 * BANKS)
                if not early(w, 2):
                    pe.wait_ge(s_bturned, w - 1)
                for b in range(BANKS):
                    ins = pe.matmul(sps[slot % 2][:, 0:P], banks[:, slot * BANKS + b, 0:EA], k.ident[:, :],
                                    start=(b == 0), stop=(b == BANKS - 1))
                ins.then_inc(s_bturn, 1)

            def project_sums(w, slot, nodes):
                pe.wait_ge(s_bturned, w + 1)
                pe.wait_ge(s_diag, w + 1)
                pe.wait_ge(s_fetched, w * 2 + 2)
                if not early(w, 2):
                    pe.wait_ge(s_term, w - 1)
                out = pps[slot % 2][:, 0:D]
                pe.matmul(out, sum_t[:, slot, :], w_sum[:, :], start=True, stop=False)
                pe.matmul(out, degree[:, slot, :], b_sum, start=False, stop=False)
                pe.matmul(out, k.ident[:, :], z[:, slot * 2, :], start=False, stop=True).then_inc(s_proj, 1)

            over(pe, (turn, 0), (project, 1), (turn_banks, 0), (project_sums, 2))

        @block.scalar
        def _(act):
            def copy_turned(w, slot, nodes):
                act.wait_ge(s_turn, w + 1)
                if not early(w, S):
                    act.wait_ge(s_out, w - (S - 1))
                act.copy(agg_t[:, slot, :], tps[slot % 2][:, 0:D]).then_inc(s_turned, 1)
                act.wait_ge(s_bturn, w + 1)
                if not early(w, S):
                    act.wait_ge(s_proj, w - (S - 1))
                act.copy(sum_t[:, slot, :], sps[slot % 2][:, 0:P]).then_inc(s_bturned, 1)

            def first_root(w, slot, nodes):
                act.wait_ge(s_mom1, w + 1)
                act.activation(moments(slot, 0)[:, 8:9], moments(slot, 0)[:, 7:8], ACT.Sqrt, bias=quarter[:, 0:1],
                               scale=0.25).then_inc(s_root1, 1)

            def second_root(w, slot, nodes):
                act.wait_ge(s_mom2, w + 1)
                act.activation(moments(slot, 1)[:, 8:9], moments(slot, 1)[:, 7:8], ACT.Sqrt,
                               bias=k.eps[:, 0:1]).then_inc(s_root2, 1)

            over(act, (second_root, 3), (first_root, 2), (copy_turned, 0))

        @block.vector
        def _(dve):
            dve.tensor_scalar(share[:, :, :], k.acc.rearrange("p (w d) -> p w d", d=AW)[:, :, D:], 0.5, None,
                              ALU.max).then_inc(s_share, 1)
            dve.tensor_scalar(quarter[:, :], k.eps[:, :], 0.25, None, ALU.mult).then_inc(s_share, 1)
            dve.wait_ge(s_share, 2)
            dve.reciprocal(share[:, :, :], share[:, :, :]).then_inc(s_share, 1)
            dve.wait_ge(s_share, 3)
            dve.wait_ge(s_w, 16 * 4)

            def count(w, slot, nodes):
                dve.wait_ge(s_bank[slot], turns(w, slot, BANKS) + 16 * BANKS)
                dve.sem_inc(k.s_hold, 1)
                dve.tensor_reduce(k.count_out[:, bass.ds(w, 1)], banks[:, slot * BANKS:(slot + 1) * BANKS, EA],
                                  AX.X, ALU.add).then_inc(s_count, 1)
                if not early(w, S):
                    dve.wait_ge(k.s_z[slot], turns(w, slot, 2))
                dve.tensor_scalar(index[:, slot, 0:1], k.count_in[:, bass.ds(w, 1)], float(DEGMAX), None,
                                  ALU.min).then_inc(s_index, 1)
                if not early(w, S):
                    dve.wait_ge(s_proj, w - (S - 1))
                dve.wait_ge(s_count, w + 1)
                dve.tensor_scalar(index[:, slot, 1:2], k.count_out[:, bass.ds(w, 1)], float(DEGMAX), None,
                                  ALU.min).then_inc(s_index, 1)
                dve.tensor_scalar(degree[:, slot, :], k.ident[:, :], k.count_out[:, bass.ds(w, 1)], None,
                                  ALU.mult).then_inc(s_diag, 1)

            def divide(w, slot, nodes):
                if not early(w, S):
                    dve.wait_ge(s_turn, w - (S - 1))
                shares = share.rearrange("p w h -> p (w h)")[:, bass.ds(w * HEADS, HEADS)]
                dve.tensor_tensor(agg[:, slot, :].rearrange("p (h d) -> p h d", h=HEADS),
                                  k.acc[:, sum_window(w)].rearrange("p (h d) -> p h d", h=HEADS),
                                  shares.unsqueeze(2).to_broadcast([P, HEADS, HD]), ALU.mult).then_inc(s_agg, 1)

            def add(w, slot, nodes):
                dve.wait_ge(s_out, w + 1)
                dve.tensor_tensor(part[:, slot, :], ops[slot % 2][:, 0:D], x[:, node_window(w)], ALU.add).then_inc(s_part, 1)

            def measure_first(w, slot, nodes):
                dve.wait_ge(s_part, w * 2 + 1)
                dve.sem_inc(k.s_hold, 1)
                dve.bn_stats(moments(slot, 0)[:, 0:6], part[:, slot, :]).then_inc(s_part, 1)

            def first_moments(w, slot, nodes):
                dve.wait_ge(s_part, w * 2 + 2)
                dve.sem_inc(k.s_hold, 1)
                dve.bn_aggr(moments(slot, 0)[:, 6:8], moments(slot, 0)[:, 0:6]).then_inc(s_mom1, 1)

            def first_inverse(w, slot, nodes):
                st = moments(slot, 0)
                dve.wait_ge(s_root1, w + 1)
                dve.reciprocal(st[:, 8:9], st[:, 8:9]).then_inc(s_inv1, 1)

            def twice(w, slot, nodes):
                here, st = part[:, slot, :], moments(slot, 0)
                dve.wait_ge(s_inv1, w + 1)
                dve.tensor_scalar(here, here, st[:, 6:7], st[:, 8:9], ALU.subtract, ALU.mult).then_inc(s_two, 1)

            def add_terms(w, slot, nodes):
                here = part[:, slot, :]
                dve.wait_ge(s_two, w * 2 + 1)
                dve.wait_ge(s_proj, w + 1)
                dve.tensor_tensor(here, here, pps[slot % 2][:, 0:D], ALU.add).then_inc(s_term, 1)

            def measure_second(w, slot, nodes):
                dve.wait_ge(s_term, w + 1)
                dve.sem_inc(k.s_hold, 1)
                dve.bn_stats(moments(slot, 1)[:, 0:6], part[:, slot, :]).then_inc(s_two, 1)

            def second_moments(w, slot, nodes):
                dve.wait_ge(s_two, w * 2 + 2)
                dve.sem_inc(k.s_hold, 1)
                dve.bn_aggr(moments(slot, 1)[:, 6:8], moments(slot, 1)[:, 0:6]).then_inc(s_mom2, 1)

            def second_inverse(w, slot, nodes):
                st = moments(slot, 1)
                dve.wait_ge(s_root2, w + 1)
                dve.reciprocal(st[:, 8:9], st[:, 8:9]).then_inc(s_inv2, 1)

            def close(w, slot, nodes):
                st = moments(slot, 1)
                dve.wait_ge(s_inv2, w + 1)
                dve.tensor_scalar(x[:, node_window(w)], part[:, slot, :], st[:, 6:7], st[:, 8:9], ALU.subtract,
                                  ALU.mult).then_inc(s_new, 1)

            over(dve, (count, 0), (first_inverse, 3), (divide, 0), (twice, 3), (add, 2), (add_terms, 3),
                 (measure_first, 2), (second_inverse, 4), (measure_second, 3), (first_moments, 2), (close, 4),
                 (second_moments, 3))


def scatter_features(nc, k):
    with ExitStack() as ctx:
        room = Arena(k.acc)
        equal = room.take([P, HALF, P], BF16)
        target = room.take([P, HALF, P], BF16)
        often = room.take([P, 4, P])
        ready = room.take([P, HALF, D])
        cur_own = room.take([P, U])
        cur_src = room.take([P, U])
        cur_dst = room.take([P, U])
        cur_row = room.take([P, U], I32)
        wps = [psum(nc, ctx, f"sf_w{i}", [P, 512]) for i in range(2)]
        wide = [psum(nc, ctx, f"sf_wide{i}", [P, 512]) for i in range(2)]
        sums = [psum(nc, ctx, f"sf_s{i}", [P, 512]) for i in range(4)]
        x = k.X.rearrange("p w d -> p (w d)")
        s_cur, s_rowcur, s_tables, s_w, s_often, s_mm, s_ready, s_tick, s_wide = sems(
            nc, k, *(f"sf_{n}" for n in ("cur", "rowcur", "tables", "w", "often", "mm", "ready", "tick", "wide")))
        s_sent, sent0 = k.s_sent, k.sent_before
        k.sent_before += 32 * IT
        block = ctx.enter_context(nc.Block())

        @block.vector
        def _(dve):
            def refill(h, at):
                part = slice(h * HALF, (h + 1) * HALF)
                dve.tensor_copy(cur_src[:, part], k.src[:, bass.ds(at, HALF)])
                dve.tensor_copy(cur_own[:, part], k.own[:, bass.ds(at, HALF)])
                dve.tensor_copy(cur_dst[:, part], k.dst[:, bass.ds(at, HALF)]).then_inc(s_cur, 1)

            for h in range(2):
                refill(h, h * HALF)
            dve.sem_inc(s_tables, 2 * U)
            with dve.Fori(0, IT) as it:
                for h in range(2):
                    part = slice(h * HALF, (h + 1) * HALF)
                    for v in range(HALF):
                        dve.wait_ge(s_sent[v], it * 32 + (sent0 - 16 + 16 * h))
                    dve.sem_inc(k.s_hold, 1)
                    dve.tensor_copy(cur_row[:, part], k.sidx[:, bass.ds(it * U + h * HALF, HALF)]).then_inc(s_rowcur, 1)
                    dve.wait_ge(s_cur, it * 2 + (h + 1))
                    for u in range(h * HALF, (h + 1) * HALF, QUAD):
                        slots, at = slice(u % HALF, u % HALF + QUAD), slice(u, u + QUAD)
                        dve.wait_ge(s_wide, it * U + (u + QUAD))
                        dve.wait_ge(s_w, it * U + (u + QUAD))
                        compare(dve, k, equal[:, slots, :], wide[u // QUAD % 2][:, :].rearrange("p (s e) -> p s e", s=QUAD),
                                cur_own[:, at]).then_inc(s_tables, QUAD)
                        compare(dve, k, target[:, slots, :], None, cur_dst[:, at]).then_inc(s_tables, QUAD)
                    dve.wait_ge(s_tables, it * 2 * U + (2 * U + (h + 1) * 2 * HALF))
                    refill(h, it * U + (U + h * HALF))

        @block.tensor
        def _(pe):
            pe.sem_inc(s_w, HALF)
            pe.sem_inc(s_mm, 4)

            def weights(it, u):
                pe.wait_ge(s_tables, it * 2 * U + (2 * U + 2 * (u // QUAD * QUAD + QUAD)))
                pe.wait_ge(s_often, it * U + (u + 1 + 2))
                pe.matmul(wps[u % 2][:, 0:P], target[:, u % HALF, :], equal[:, u % HALF, :], start=True,
                          stop=True).then_inc(s_w, 1)

            def carried(it, u, win):
                pe.wait_ge(s_often, it * U + (4 + u + 1))
                pe.wait_ge(s_ready, it * U + (u + 1))
                pe.matmul(sums[u % 4][:, 0:D], often[:, u % 4, :], x[:, node_window(win)], start=True,
                          stop=True).then_inc(s_mm, 1)

            def sources(it, u):
                if u % HALF == 0:
                    pe.wait_ge(s_cur, it * 2 + (1 + u // HALF))
                pe.wait_ge(s_tables, it * 2 * U + (2 * U + 2 * u - HALF))
                widen(pe, k, wide[u // QUAD % 2], cur_src[:, u % U:u % U + QUAD]).then_inc(s_wide, QUAD)

            sources(0, 0)
            sources(0, QUAD)
            with pe.Fori(0, IT) as it:
                win = load_steps(nc, pe, k.win, it, NW - 1)
                weights(it, 0)
                weights(it, 1)
                for u in range(U):
                    if u % QUAD == 0:
                        sources(it, u + HALF)
                    if u + 2 < U:
                        weights(it, u + 2)
                    carried(it, u, win[u])

        @block.scalar
        def _(act):
            act.sem_inc(s_often, 4)
            act.sem_inc(s_ready, 4)

            def copy_often(it, u):
                act.wait_ge(s_w, it * U + (HALF + u + 1))
                act.wait_ge(s_mm, it * U + (u + 1))
                act.copy(often[:, u % 4, :], wps[u % 2][:, 0:P]).then_inc(s_often, 1)

            def copy_sums(it, u):
                act.wait_ge(s_mm, it * U + (4 + u + 1))
                act.wait_ge(s_sent[u % HALF], it * 32 + (sent0 + 16 * (u // HALF)))
                act.copy(ready[:, u % HALF, :], sums[u % 4][:, 0:D]).then_inc(s_ready, 1)

            with act.Fori(0, IT) as it:
                copy_often(it, 0)
                copy_often(it, 1)
                for u in range(U):
                    if u + 2 < U:
                        copy_often(it, u + 2)
                    copy_sums(it, u)

        @block.gpsimd
        def _(pool):
            with pool.Fori(0, IT) as it:
                for u in range(U):
                    if u % HALF == 0:
                        pool.wait_ge(s_rowcur, it * 2 + (u // HALF + 1))
                    pool.wait_ge(s_ready, it * U + (4 + u + 1))
                    pool.wait_ge(s_sent[(u - BANKS) % HALF], it * 32 + (sent0 + 16 * (1 + (u - BANKS) // HALF)))
                    pool.sem_inc(s_tick, 1)
                    pool.indirect_dma_start(k.out_sum[u % BANKS], bass.IndirectOffsetOnAxis(ap=cur_row[:, u:u + 1], axis=0),
                                            ready[:, u % HALF, :], None, compute_op=ALU.add).then_inc(s_sent[u % HALF], 16)
            for v in range(HALF):
                pool.wait_ge(s_sent[v], sent0 + 32 * IT)


H3 = 3 * D


def gate_weights(k):
    w = Kit()
    room = Arena(k.sims)
    w.hidden = room.take([P, 2, H3])
    w.ways = room.take([P, 4, H3])
    w.ways_bias = room.take([P, 2, H3])
    w.share = room.take([P, 2, NW])
    w.met = room.take([P, 2, NW])
    return w


def fold_weights(nc, k, a):
    w = k.gate = gate_weights(k)
    with ExitStack() as ctx:
        room = Arena(k.side)
        w_ih = room.take([P, 4, H3])
        w_dir = room.take([P, 4, D])
        b_dir = room.take([P, 4])
        b_wide = room.take([P, 4, P])
        fps = [psum(nc, ctx, f"fw_{i}", [P, 2, 512]) for i in range(3)]
        s_w, s_wide, s_mm, s_read, s_share = sems(nc, k, "fw_w", "fw_wide", "fw_mm", "fw_read", "fw_share")
        block = ctx.enter_context(nc.Block())
        jobs = [(way, part) for way in range(2) for part in range(3)]

        @block.sync
        def _(sp):
            sp.dma_start(w_ih[:, :, :], a["w_ih_t"].rearrange("(c p) m -> p c m", p=P)).then_inc(s_w, 16)
            for n, name in enumerate(("in", "out")):
                sp.dma_start(w_dir[:, 2 * n:2 * n + 2, :],
                             a[f"L3_gnn_W_{name}"].rearrange("(c p) m -> p c m", p=P)).then_inc(s_w, 16)
                sp.dma_start(b_dir[:, 2 * n:2 * n + 2], a[f"L3_gnn_b_{name}"].rearrange("(c p) o -> p (c o)", p=P),
                             allow_slow_non_contiguous=True).then_inc(s_w, 16)
            sp.dma_start(w.hidden[:, :, :], a["w_hh_t"].rearrange("(c p) m -> p c m", p=P)).then_inc(s_w, 16)
            sp.wait_ge(s_w, 16 * 6)

        @block.tensor
        def _(pe):
            pe.wait_ge(s_w, 16 * 6)
            pe.wait_ge(s_wide, 4)
            for n, (way, part) in enumerate(jobs):
                if n >= 3:
                    pe.wait_ge(s_read, n - 2)
                for lo, hi in ((0, 2 * D), (2 * D, H3)):
                    for c in range(2):
                        left = b_wide[:, way * 2 + c, :] if part == 2 else w_dir[:, way * 2 + c, part * P:(part + 1) * P]
                        ins = pe.matmul(fps[n % 3][:, lo // (2 * D), 0:hi - lo], left, w_ih[:, way * 2 + c, lo:hi],
                                        start=(c == 0), stop=(c == 1))
                ins.then_inc(s_mm, 1)

        @block.scalar
        def _(act):
            for n, (way, part) in enumerate(jobs):
                act.wait_ge(s_mm, n + 1)
                to = w.ways_bias[:, way, :] if part == 2 else w.ways[:, way * 2 + part, :]
                act.copy(to, fps[n % 3][:, :, :].rearrange("p b d -> p (b d)")[:, 0:H3]).then_inc(s_read, 1)

        @block.vector
        def _(dve):
            dve.wait_ge(s_w, 16 * 6)
            for n in range(4):
                dve.tensor_scalar(b_wide[:, n, :], k.ones[:, :], b_dir[:, n:n + 1], None, ALU.mult).then_inc(s_wide, 1)
            for n, count in enumerate((k.count_in, k.count_out)):
                dve.tensor_scalar(w.met[:, n, :], count[:, :], 1.0, None, ALU.min)
                dve.tensor_scalar(w.share[:, n, :], count[:, :], 1.0, None, ALU.max).then_inc(s_share, 1)
            dve.wait_ge(s_share, 2)
            dve.reciprocal(w.share[:, :, :], w.share[:, :, :])


def gate_parts(nc, k, ctx, room):
    w = k.gate
    banks = room.take([P, BANKS, D])
    rows = room.take([P, D])
    state = room.take([P, D])
    turned = room.take([P, 4 * P])
    gates = room.take([P, 4 * D])
    bias = room.take([P, 4 * D])
    bias_hh = room.take([P, 2 * D])
    tps = psum(nc, ctx, "gp_t", [P, 512])
    gps = [psum(nc, ctx, f"gp_g{i}", [P, 512]) for i in range(2)]
    x = k.X.rearrange("p w d -> p (w d)")
    s_b, s_bias, s_bank, s_add, s_rows, s_state, s_turn, s_turned, s_mm, s_gate, s_sent, s_out = sems(
        nc, k, *(f"gp_{n}" for n in ("b", "bias", "bank", "add", "rows", "state", "turn", "turned", "mm", "gate", "sent",
                                         "out")))
    work = Kit()

    def sync(sp):
        sp.dma_start(bias[:, 0:H3], k.gate_bias[0].to_broadcast([P, H3])).then_inc(s_b, 16)
        sp.dma_start(bias[:, H3:], k.gate_bias[1][:, 2 * D:].to_broadcast([P, D])).then_inc(s_b, 16)
        sp.dma_start(bias_hh[:, :], k.gate_bias[1][:, 0:2 * D].to_broadcast([P, 2 * D])).then_inc(s_b, 16)
        def load(at):
            for b in range(BANKS):
                sp.dma_start(banks[:, b, :], k.out_sum[b][bass.ds(at * P, P), :]).then_inc(s_bank, 16)

        def send(at):
            sp.wait_ge(s_gate, at * 6 + 12)
            sp.dma_start(k.gate_rows[bass.ds(at * P, P), :], gates).then_inc(s_out, 16)
            sp.wait_ge(s_out, at * 16 + 16)
            sp.sem_inc(s_sent, 1)

        sp.sem_inc(s_sent, 1)
        load(0)
        sp.wait_ge(s_add, 3)
        load(1)
        with sp.Fori(1, NW) as it:
            sp.wait_ge(s_add, it * 3 + 3)
            load(it + 1)
            send(it - 1)
        send(NW - 1)
        sp.wait_ge(s_bank, 16 * BANKS * (NW + 1))

    def vector(dve):
        dve.wait_ge(s_b, 48)
        dve.tensor_tensor(bias[:, 0:2 * D], bias[:, 0:2 * D], bias_hh[:, :], ALU.add).then_inc(s_bias, 1)
        dve.sem_inc(s_gate, 6)
        dve.wait_ge(s_bias, 1)
        half, last = slice(0, 2 * D), slice(2 * D, H3)

        def add_pairs(it):
            dve.wait_ge(s_bank, it * (16 * BANKS) + 16 * BANKS)
            dve.tensor_tensor(banks[:, 0, :], banks[:, 0, :], banks[:, 1, :], ALU.add).then_inc(s_add, 1)
            dve.tensor_tensor(banks[:, 2, :], banks[:, 2, :], banks[:, 3, :], ALU.add).then_inc(s_add, 1)

        def add_all(it):
            dve.wait_ge(s_add, it * 3 + 2)
            dve.wait_ge(s_turn, it + 1)
            dve.tensor_tensor(rows, banks[:, 0, :], banks[:, 2, :], ALU.add).then_inc(s_add, 1)

        def bias_of(it, way, part, before):
            dve.wait_ge(s_gate, it * 6 + (6 + before))
            dve.scalar_tensor_tensor(out=gates[:, part], in0=w.ways_bias[:, way, part],
                                     scalar=w.met[:, way, bass.ds(it, 1)], in1=gates[:, part], op0=ALU.mult,
                                     op1=ALU.add).then_inc(s_gate, 1)

        add_pairs(0)
        add_all(0)

        def step(it, u):
            if u == 5:
                add_pairs(it + 1)
            if u == 7:
                add_all(it + 1)
            if u == 10:
                dve.wait_ge(s_mm, it * 2 + 3)
                dve.wait_ge(s_sent, it + 1)
                dve.tensor_tensor(gates[:, half], gps[0][:, :], bias[:, half], ALU.add).then_inc(s_gate, 1)
            if u in (11, 12):
                bias_of(it, u - 11, half, u - 10)
            if u == 14:
                dve.wait_ge(s_mm, it * 2 + 4)
                dve.tensor_tensor(gates[:, 2 * D:], gps[1][:, :], bias[:, 2 * D:], ALU.add).then_inc(s_gate, 1)
            if u == 15:
                bias_of(it, 0, last, 4)
                bias_of(it, 1, last, 5)
        return step

    def tensor(pe):
        pe.sem_inc(s_turn, 1)
        pe.sem_inc(s_mm, 2)

        def step(it, u):
            if u == 4:
                pe.wait_ge(s_rows, it + 1)
                pe.wait_ge(s_state, it + 1)
                pe.wait_ge(s_turned, it + 1)
                for n in range(4):
                    ins = pe.transpose(tps[:, n * P:(n + 1) * P], (rows, state)[n // 2][:, n % 2 * P:(n % 2 + 1) * P],
                                       k.ident[:, :])
                ins.then_inc(s_turn, 1)
            if 6 <= u < 14:
                bank, c = (u - 6) // 4, (u - 6) % 4
                left = turned[:, c * P:(c + 1) * P]
                right = w.ways[:, 2 + c, :] if c < 2 else w.hidden[:, c - 2, :]
                if c == 0:
                    pe.wait_ge(s_turned, it + 2)
                    pe.wait_ge(s_gate, it * 6 + (1 if bank == 0 else 4))
                if bank == 0:
                    ins = pe.matmul(gps[0][:, :], left, right[:, 0:2 * D], start=(c == 0), stop=(c == 3))
                else:
                    at = 0 if c < 2 else D
                    ins = pe.matmul(gps[1][:, at:at + D], left, right[:, 2 * D:], start=(c % 2 == 0), stop=(c % 2 == 1))
                if c == 3:
                    ins.then_inc(s_mm, 1)
        return step

    def scalar(act):
        act.sem_inc(s_turned, 1)
        with act.Fori(0, NW) as it:
            act.wait_ge(s_turn, it + 1)
            act.sem_inc(k.s_hold, 1)
            act.copy(state, x[:, node_window(it)]).then_inc(s_state, 1)
            act.wait_ge(s_add, it * 3 + 3)
            act.sem_inc(k.s_hold, 1)
            act.activation(rows, rows, ACT.Copy, scale=w.share[:, 1, bass.ds(it, 1)]).then_inc(s_rows, 1)
            act.wait_ge(s_turn, it + 2)
            act.wait_ge(s_mm, it * 2 + 2)
            act.copy(turned, tps[:, :]).then_inc(s_turned, 1)

    work.sync, work.vector, work.tensor, work.scalar = sync, vector, tensor, scalar
    return work


def gru_close(nc, k, a):
    w = k.gate
    S = 4
    GROUP = 4
    with ExitStack() as ctx:
        room = Arena(k.side)
        mean = room.take([P, S, D])
        mean_t = room.take([P, S, D])
        gates = room.take([P, S, 4 * D])
        part = room.take([P, S, D])
        stats = room.take([P, S * 6])
        moments_now = room.take([P, S * 2])
        moments = room.take([P, NW, 2])
        root = room.take([P, NW])
        tps = [psum(nc, ctx, f"gr_t{i}", [P, 512]) for i in range(2)]
        gps = [psum(nc, ctx, f"gr_g{i}", [P, 2 * 512]) for i in range(2)]
        x = k.X.rearrange("p w d -> p (w d)")
        s_mean, s_turn, s_turned, s_mm, s_gate, s_cand, s_tanh, s_new, s_mom, s_kept, s_root, s_inv, s_done, \
            s_out = sems(nc, k, *(f"gr_{n}" for n in (
                "mean", "turn", "turned", "mm", "gate", "cand", "tanh", "new", "mom", "kept", "root", "inv",
                "done", "out")))
        s_in = sems(nc, k, *(f"gr_in{i}" for i in range(S)))
        block = ctx.enter_context(nc.Block())
        over = lambda engine, *stages: over_windows(engine, *stages, slots=S)
        turns = lambda w_, slot: (w_ - slot) * (16 // S)

        @block.sync
        def _(sp):
            def load(w_, slot, nodes):
                if not early(w_, S):
                    sp.wait_ge(s_mom, w_ - (S - 1))
                sp.dma_start(gates[:, slot, :],
                             k.gate_rows[bass.ds(w_ * P, P), :]).then_inc(s_in[slot], 16)

            over(sp, (load, 0))
            for first in range(0, NW - 1, GROUP):
                sp.wait_ge(s_done, first + GROUP)
                sp.dma_start(a["out"][first * P:(first + GROUP) * P, :].rearrange("(w p) d -> p w d", p=P),
                             k.X[:, first:first + GROUP, :]).then_inc(s_out, 16)
            sp.wait_ge(s_done, NW)
            sp.dma_start(a["out"][(NW - 1) * P:N, :], k.X[0:TAIL, NW - 1, :]).then_inc(s_out, 16)
            sp.wait_ge(s_out, 16 * ((NW - 1) // GROUP + 1))

        @block.tensor
        def _(pe):
            def turn(w_, slot, nodes):
                pe.wait_ge(s_mean, w_ + 1)
                if not early(w_, 2):
                    pe.wait_ge(s_turned, w_ - 1)
                for c in range(2):
                    ins = pe.transpose(tps[slot % 2][:, c * P:(c + 1) * P], mean[:, slot, c * P:(c + 1) * P], k.ident[:, :])
                ins.then_inc(s_turn, 1)

            def products(w_, slot, nodes):
                pe.wait_ge(s_turned, w_ + 1)
                for lo, hi, used, count in ((0, 2 * D, s_gate, 1), (2 * D, H3, s_cand, 3)):
                    if not early(w_, 2):
                        pe.wait_ge(used, w_ * count - count)
                    out = gps[slot % 2][:, lo:hi]
                    for c in range(2):
                        ins = pe.matmul(out, mean_t[:, slot, c * P:(c + 1) * P], w.ways[:, c, lo:hi], start=(c == 0),
                                        stop=(c == 1 and lo > 0))
                    if lo == 0:
                        pe.wait_ge(s_in[slot], turns(w_, slot) + 16)
                        ins = pe.matmul(out, k.ident[:, :], gates[:, slot, lo:hi], start=False, stop=True)
                    ins.then_inc(s_mm, 1)

            over(pe, (turn, 1), (products, 2))

        @block.scalar
        def _(act):
            def means(w_, slot, nodes):
                if not early(w_, S):
                    act.wait_ge(s_turn, w_ - (S - 1))
                    act.sem_inc(k.s_hold, 1)
                act.activation(mean[:, slot, :], k.acc[:, sum_window(w_)], ACT.Copy,
                               scale=w.share[:, 0, bass.ds(w_, 1)]).then_inc(s_mean, 1)

            def copy_turned(w_, slot, nodes):
                act.wait_ge(s_turn, w_ + 1)
                if not early(w_, S):
                    act.wait_ge(s_mm, w_ * 2 - (2 * S - 2))
                act.copy(mean_t[:, slot, :], tps[slot % 2][:, 0:D]).then_inc(s_turned, 1)

            def sigmoids(w_, slot, nodes):
                act.wait_ge(s_mm, w_ * 2 + 1)
                act.activation(gates[:, slot, 0:2 * D], gps[slot % 2][:, 0:2 * D], ACT.Sigmoid).then_inc(s_gate, 1)

            def candidate(w_, slot, nodes):
                act.wait_ge(s_cand, w_ * 3 + 3)
                act.activation(gates[:, slot, 2 * D:H3], gates[:, slot, 2 * D:H3], ACT.Tanh).then_inc(s_tanh, 1)

            over(act, (means, 0), (copy_turned, 1), (candidate, 3), (sigmoids, 2))
            act.wait_ge(s_kept, NW)
            act.activation(root[:, :], moments[:, :, 1], ACT.Sqrt, bias=k.eps[:, 0:1]).then_inc(s_root, 1)

        @block.vector
        def _(dve):
            def candidate(w_, slot, nodes):
                cand, state_part = gates[:, slot, 2 * D:H3], gates[:, slot, H3:]
                dve.wait_ge(s_mm, w_ * 2 + 2)
                dve.tensor_tensor(cand, cand, gps[slot % 2][:, 2 * D:H3], ALU.add).then_inc(s_cand, 1)
                dve.wait_ge(s_gate, w_ + 1)
                dve.tensor_tensor(state_part, gates[:, slot, 0:D], state_part, ALU.mult).then_inc(s_cand, 1)
                dve.wait_ge(s_cand, w_ * 3 + 2)
                dve.tensor_tensor(cand, cand, state_part, ALU.add).then_inc(s_cand, 1)

            def state(w_, slot, nodes):
                here = part[:, slot, :]
                old = x[:, node_window(w_)]
                dve.wait_ge(s_tanh, w_ + 1)
                dve.tensor_tensor(here, gates[:, slot, 2 * D:H3], old, ALU.subtract).then_inc(s_new, 1)
                dve.wait_ge(s_new, w_ * 4 + 1)
                dve.tensor_tensor(here, here, gates[:, slot, D:2 * D], ALU.mult).then_inc(s_new, 1)
                dve.wait_ge(s_new, w_ * 4 + 2)
                dve.scalar_tensor_tensor(out=old, in0=old, scalar=2.0, in1=here, op0=ALU.mult,
                                         op1=ALU.add).then_inc(s_new, 1)
                dve.wait_ge(s_new, w_ * 4 + 3)
                dve.sem_inc(k.s_hold, 1)
                dve.bn_stats(stats[:, slot * 6:slot * 6 + 6], old).then_inc(s_new, 1)
                dve.wait_ge(s_new, w_ * 4 + 4)
                dve.sem_inc(k.s_hold, 1)
                dve.bn_aggr(moments_now[:, slot * 2:slot * 2 + 2], stats[:, slot * 6:slot * 6 + 6]).then_inc(s_mom, 1)

            def keep_moments(w_, slot, nodes):
                dve.wait_ge(s_mom, w_ + 1)
                dve.tensor_scalar(moments[:, bass.ds(w_, 1), :].rearrange("p w m -> p (w m)"),
                                  moments_now[:, slot * 2:slot * 2 + 2], 1.0, None, ALU.mult).then_inc(s_kept, 1)

            over(dve, (candidate, 3), (state, 4), (keep_moments, 4))
            dve.wait_ge(s_root, 1)
            dve.reciprocal(root[:, :], root[:, :]).then_inc(s_inv, 1)
            dve.wait_ge(s_inv, 1)
            for n in range(NW):
                dve.tensor_scalar(x[:, n * D:(n + 1) * D], x[:, n * D:(n + 1) * D], moments[:, n, 0:1], root[:, n:n + 1],
                                  ALU.subtract, ALU.mult).then_inc(s_done, 1)


def build(nc, k, a):
    with ExitStack() as ctx:
        k.ctx = ctx
        k.rows_before = 0
        k.sent_before = 16 * (1 + 2 * IT)
        dram = lambda name, shape, dt=F32: nc.dram_tensor(name, shape, dt)
        k.key_row = dram("key_row", [P + ROWS * P]).ap()
        k.kv_rows = dram("kv_rows", [NPAD, 2 * D]).ap()
        k.x3_rows = dram("x3_rows", [NPAD, D]).ap()
        k.node_gates = dram("node_gates", [NPAD, D]).ap()
        k.gate_rows = dram("gate_rows", [NPAD, 4 * D]).ap()
        k.v_edge = dram("v_edge", [STEPS * P, D]).ap()
        k.attr_sum = [dram(f"attr_sum{b}", [SUMROWS, EW]).ap() for b in range(BANKS)]
        k.out_sum = [dram(f"out_sum{b}", [SUMROWS, D]).ap() for b in range(BANKS)]
        k.xs = sbuf(nc, ctx, "xs", [P, NW, D])
        k.X = k.xs[:, :, :]
        k.big = sbuf(nc, ctx, "big", [P, NW * AW + NW * D])
        k.acc = k.big[:, 0:NW * AW]
        k.side = k.big[:, NW * AW:NW * AW + NW * D]
        k.sims = sbuf(nc, ctx, "sims", [P, STEPS * HEADS])[:, :]
        k.dst = sbuf(nc, ctx, "dst_tab", [P, ROWS])
        k.src = sbuf(nc, ctx, "src_tab", [P, ROWS])
        k.own = sbuf(nc, ctx, "own_tab", [P, ROWS])
        k.count_in = sbuf(nc, ctx, "count_in", [P, NW])
        k.count_out = sbuf(nc, ctx, "count_out", [P, NW])
        k.norm2 = k.sims[:, 0:2 * D]
        k.idx = sbuf(nc, ctx, "idx_tab", [P, ROWS], I32)
        k.sidx = sbuf(nc, ctx, "sidx_tab", [P, ROWS], I32)
        k.win = sbuf(nc, ctx, "win_row", [1, ROWS], I32)
        k.chunk = sbuf(nc, ctx, "chunk_row", [1, ROWS], I32)
        k.beyond = sbuf(nc, ctx, "beyond_row", [1, ROWS], I32)
        k.ident = sbuf(nc, ctx, "ident", [P, P])
        k.ones = sbuf(nc, ctx, "ones", [P, P])
        k.below = sbuf(nc, ctx, "below", [P, P])
        k.iota_row = sbuf(nc, ctx, "iota_row", [P, P])
        k.iota_col = sbuf(nc, ctx, "iota_col", [P, 1])
        k.eps = sbuf(nc, ctx, "eps", [P, 1])
        k.trash = sbuf(nc, ctx, "trash", [P, 1])
        k.stage_sems = []
        k.s_hold = nc.alloc_semaphore("s_hold")
        k.s_row = [nc.alloc_semaphore(f"s_row{u}") for u in range(U)]
        k.gate_bias = (a["L3_gnn_b_ih"], a["L3_gnn_b_hh"])
        k.s_z = [nc.alloc_semaphore(f"s_z{i}") for i in range(4)]
        k.s_sent = [nc.alloc_semaphore(f"s_sent{v}") for v in range(HALF)]
        step_tables(nc, k, a["dst"], a["src"], a["x"])
        end_stage(nc, k)
        gather_sums(nc, k, "l0", a["x"], True)
        end_stage(nc, k)
        gin_mlp(nc, k, a)
        end_stage(nc, k)
        gin_close_and_project(nc, k, a)
        end_stage(nc, k)
        edge_scores(nc, k)
        end_stage(nc, k)
        softmax_weights(nc, k)
        end_stage(nc, k)
        weighted_sums(nc, k, a["attr"])
        end_stage(nc, k)
        attend_close(nc, k, a)
        end_stage(nc, k)
        scatter_features(nc, k)
        end_stage(nc, k)
        fold_weights(nc, k, a)
        end_stage(nc, k)
        gather_sums(nc, k, "l3", k.x3_rows, False, beside=gate_parts)
        end_stage(nc, k)
        gru_close(nc, k, a)
        end_stage(nc, k)




def padded(rows, shape, fill):
    out = np.full(shape, fill, rows.dtype)
    out.reshape((-1,) + rows.shape[1:])[:rows.shape[0]] = rows
    return out


def kernel(**inputs):
    import concourse.bacc as bacc
    from concourse.bass_utils import run_bass_kernel_spmd

    host = {n: np.ascontiguousarray(v) for n, v in inputs.items()}
    lay = {
        "x": padded(host["x"], (NPAD, D), 0),
        "dst": padded(host["dst"], (NC, P), PAD_DST),
        "src": padded(host["src"], (NC, P), 0),
        "attr": padded(host["edge_attr_128"], ((NC + QUAD) * P, EA), 0),
    }
    for name in ("L0_gnn_W1", "L0_gnn_W2"):
        lay[name] = host[name]
    for name in ("b1", "g1", "bt1", "b2", "g2", "bt2", "eps_gin"):
        lay[f"L0_gnn_{name}"] = host[f"L0_gnn_{name}"].reshape(1, -1)
    for name in "qkvo":
        lay[f"w{name}_t"] = np.ascontiguousarray(host[f"L1_gnn_W{name}"].T)
        lay[f"L1_gnn_b{name}"] = host[f"L1_gnn_b{name}"].reshape(1, -1)
    for name in ("z_in", "z_out", "W_cent", "W_vor", "W_sum"):
        lay[f"L2_gnn_{name}"] = host[f"L2_gnn_{name}"]
    for name in ("L2_gnn_b_cent", "L2_gnn_b_vor", "L2_gnn_b_sum", "L3_gnn_b_ih", "L3_gnn_b_hh"):
        lay[name] = host[name].reshape(1, -1)
    for name in ("in", "out"):
        lay[f"L3_gnn_W_{name}"] = host[f"L3_gnn_W_{name}"]
        lay[f"L3_gnn_b_{name}"] = host[f"L3_gnn_b_{name}"].reshape(-1, 1)
    for name in ("ih", "hh"):
        lay[f"w_{name}_t"] = np.ascontiguousarray(host[f"L3_gnn_W_{name}"].T)
    for name in ("node_vec1", "node_vec1_n2"):
        lay[name] = np.ascontiguousarray(padded(host[name], (NPAD, 1), 0).reshape(NW, P).T)
    nc = bacc.Bacc("TRN2", target_bir_lowering=False, num_devices=1)
    arrays, handles = {}, {}
    for name, array in lay.items():
        arrays[f"in_{name}"] = array
        handles[name] = nc.dram_tensor(f"in_{name}", array.shape, mybir.dt.from_np(array.dtype), kind="ExternalInput").ap()
    handles["out"] = nc.dram_tensor("out", (N, D), F32, kind="ExternalOutput").ap()
    build(nc, Kit(), handles)
    return run_bass_kernel_spmd(nc, [arrays], core_ids=[0]).results[0]["out"]
```
